# Optimizing a Trainium2 kernel written in Bass

```python
import numpy as np
import jax
import jax.numpy as jnp

def _softmax(x, axis=-1):
    return jax.nn.softmax(x, axis=axis)

def _gelu(x):
    return jax.nn.gelu(x, approximate=True)

def _silu(x):
    return jax.nn.silu(x)

def _sigmoid(x):
    return jax.nn.sigmoid(x)

def _layernorm(x, axis=-1, eps=1e-05):
    m = jnp.mean(x, axis=axis, keepdims=True)
    v = jnp.var(x, axis=axis, keepdims=True)
    return (x - m) / jnp.sqrt(v + eps)

def _scatter_add(tgt, idx, src, axis=0):
    return tgt.at[idx].add(src)

def _segment_sum(src, seg, n):
    return jax.ops.segment_sum(src, seg, n)
kernel_name = 'mk_adaln_ffn_d2_seqx_r4_28358a'

def setup_inputs(seed: int=0):
    np.random.seed(seed)
    _w = jnp.asarray

    def _rec_inputs():
        import jax
        import jax.numpy as jnp
        _rk = jax.random.key(seed)
        x = -0.0002928 + 1 * jax.random.normal(jax.random.fold_in(_rk, 1), (64, 64, 256), jnp.float32)
        _lenS = 64 - jax.random.randint(jax.random.fold_in(_rk, 7), (64,), 0, max(1, 64 // 4) + 1, jnp.int32)
        _lenS2 = 64 - jax.random.randint(jax.random.fold_in(_rk, 8), (64,), 0, max(1, 64 // 4) + 1, jnp.int32)
        cond_64 = -0.0184271 + 1.00439 * jax.random.normal(jax.random.fold_in(_rk, 12), (64, 64), jnp.float32)
        fside_16xSxS_0 = -5.72187e-05 + 0.999849 * jax.random.normal(jax.random.fold_in(_rk, 13), (16, 64, 64), jnp.float32)
        _validS = jnp.arange(64)[None, :] < _lenS[:, None]
        _validS2 = jnp.arange(64)[None, :] < _lenS2[:, None]
        _causal = jnp.tril(jnp.ones((64, 64), dtype=bool))
        mask_BxS_bf1 = jnp.ones((64, 64), dtype=bool)
        mask_BxS_bk0 = jnp.logical_not(jnp.broadcast_to(_validS[:, :], (64, 64)))
        return (x, cond_64, fside_16xSxS_0, mask_BxS_bf1, mask_BxS_bk0)
    x, cond_64, fside_16xSxS_0, mask_BxS_bf1, mask_BxS_bk0 = _rec_inputs()

    def _L0_cond_setup():
        import jax, jax.numpy as jnp
        import numpy as np
        DIM = 256
        HEADS = 16
        DIM_HEAD = 64
        SCALE = 8.0

        def ln(x, g, eps=1e-05):
            mean = x.mean(axis=-1, keepdims=True)
            var = ((x - mean) ** 2).mean(axis=-1, keepdims=True)
            return (x - mean) * jax.lax.rsqrt(var + eps) * g

        def l2norm(t):
            n = jnp.maximum(jnp.linalg.norm(t, axis=-1, keepdims=True), 1e-12)
            return t / n

        def rel_pos_bias(n, w0, b0, g0, w1, b1, g1, w2, b2, dtype):
            pos = jnp.arange(-n + 1, n, dtype=dtype)[:, None]
            h = jax.nn.silu(ln(pos @ w0 + b0, g0))
            h = jax.nn.silu(ln(h @ w1 + b1, g1))
            h = h @ w2 + b2
            i = jnp.arange(n)
            idx = i[:, None] - i[None, :] + n - 1
            bias = h[idx]
            return jnp.transpose(bias, (2, 0, 1))
        key = jax.random.key(seed)
        ks = jax.random.split(key, 16)
        b, n = (2, 512)
        inner = HEADS * DIM_HEAD
        s = 0.02
        return {'x': jax.random.normal(ks[0], (b, n, DIM), jnp.float32), 'mask': jnp.ones((b, n), dtype=bool), 'g_norm': jnp.ones((DIM,), jnp.float32), 'Wq': jax.random.normal(ks[1], (DIM, inner), jnp.float32) * s, 'Wkv': jax.random.normal(ks[2], (DIM, 2 * DIM_HEAD), jnp.float32) * s, 'q_scale': jnp.ones((DIM_HEAD,), jnp.float32), 'k_scale': jnp.ones((DIM_HEAD,), jnp.float32), 'null_kv': jax.random.normal(ks[3], (2, DIM_HEAD), jnp.float32), 'null_attn_bias': jax.random.normal(ks[4], (HEADS,), jnp.float32), 'w0': jax.random.normal(ks[5], (1, DIM), jnp.float32) * s, 'b0': jnp.zeros((DIM,), jnp.float32), 'g0': jnp.ones((DIM,), jnp.float32), 'w1': jax.random.normal(ks[6], (DIM, DIM), jnp.float32) * s, 'b1': jnp.zeros((DIM,), jnp.float32), 'g1': jnp.ones((DIM,), jnp.float32), 'w2': jax.random.normal(ks[7], (DIM, HEADS), jnp.float32) * s, 'b2': jnp.zeros((HEADS,), jnp.float32), 'Wout': jax.random.normal(ks[8], (inner, DIM), jnp.float32) * s, 'g_out': jnp.ones((DIM,), jnp.float32)}
    _L0_cond_all = _L0_cond_setup()
    _L0_cond_in = {k: v for k, v in _L0_cond_all.items() if k in ('g_norm', 'Wq', 'Wkv', 'q_scale', 'k_scale', 'null_attn_bias', 'w0', 'b0', 'g0', 'w1', 'b1', 'g1', 'w2', 'b2', 'Wout', 'g_out')}
    del _L0_cond_all

    def _L0_ffn_setup():
        import jax, jax.numpy as jnp
        import numpy as np
        import math
        BETA = 0.9
        THRESHOLD = 1.0
        NUM_STEPS = 5
        ALPHA = 2.0

        @jax.custom_vjp
        def spike_fn(u):
            return (u > 0).astype(u.dtype)

        def _spike_fwd(u):
            return (spike_fn(u), u)

        def _spike_bwd(u, g):
            s = jnp.pi / 2.0 * ALPHA * u
            return (g * (ALPHA / 2.0) / (1.0 + s * s),)
        spike_fn.defvjp(_spike_fwd, _spike_bwd)
        key = jax.random.key(seed)
        k1, k2, k3 = jax.random.split(key, 3)
        n_embd = 256
        x = jax.random.normal(k1, (4, 512, n_embd), dtype=jnp.float32)
        W_fc = jax.random.normal(k2, (4 * n_embd, n_embd), dtype=jnp.float32) / math.sqrt(n_embd)
        W_proj = jax.random.normal(k3, (n_embd, 4 * n_embd), dtype=jnp.float32) / math.sqrt(4 * n_embd)
        return {'x': x, 'W_fc': W_fc, 'W_proj': W_proj}
    _L0_ffn_all = _L0_ffn_setup()
    _L0_ffn_in = {k: v for k, v in _L0_ffn_all.items() if k in ('W_fc', 'W_proj')}
    del _L0_ffn_all

    def _L1_cond_setup():
        import jax, jax.numpy as jnp
        import numpy as np
        B, N, DIM, H, DH = (2, 512, 256, 16, 64)
        INNER = H * DH
        EPS = 1e-05

        def layernorm(x, g):
            mean = jnp.mean(x, axis=-1, keepdims=True)
            var = jnp.var(x, axis=-1, keepdims=True)
            return (x - mean) * jax.lax.rsqrt(var + EPS) * g
        key = jax.random.key(seed)
        ks = jax.random.split(key, 10)
        x = jax.random.normal(ks[0], (B, N, DIM), dtype=jnp.float32)
        attn_bias = jax.random.normal(ks[1], (H, N, N), dtype=jnp.float32)
        mask = jax.random.randint(ks[2], (B, N), 0, 2).astype(bool)
        g_in = jnp.ones((DIM,), dtype=jnp.float32)
        null_attn_bias = jax.random.normal(ks[3], (H,), dtype=jnp.float32)
        null_kv = jax.random.normal(ks[4], (2, DH), dtype=jnp.float32)
        Wq = jax.random.normal(ks[5], (DIM, INNER), dtype=jnp.float32) * 0.02
        Wkv = jax.random.normal(ks[6], (DIM, 2 * DH), dtype=jnp.float32) * 0.02
        Wo = jax.random.normal(ks[7], (INNER, DIM), dtype=jnp.float32) * 0.02
        g_out = jnp.ones((DIM,), dtype=jnp.float32)
        return {'x': x, 'attn_bias': attn_bias, 'mask': mask, 'g_in': g_in, 'null_attn_bias': null_attn_bias, 'null_kv': null_kv, 'Wq': Wq, 'Wkv': Wkv, 'Wo': Wo, 'g_out': g_out}
    _L1_cond_all = _L1_cond_setup()
    _L1_cond_in = {k: v for k, v in _L1_cond_all.items() if k in ('g_in', 'null_attn_bias', 'Wq', 'Wkv', 'Wo', 'g_out')}
    del _L1_cond_all

    def _L1_ffn_setup():
        import jax, jax.numpy as jnp
        import numpy as np
        D_MODEL = 256
        NUM_HEADS = 4
        NUM_EXPERTS = 8
        TOP_K = 2
        D_FF = 256
        EPS = 1e-06

        def _rmsnorm(x, g):
            return x * jax.lax.rsqrt(jnp.mean(x * x, axis=-1, keepdims=True) + EPS) * g

        def _swiglu(x, w1, w2, w3):
            return jax.nn.silu(x @ w1.T) * (x @ w3.T) @ w2.T
        key = jax.random.key(seed)
        ks = jax.random.split(key, 16)
        d, e, f = (D_MODEL, NUM_EXPERTS, D_FF)
        dc = d // 4
        s = 0.02
        return {'X': jax.random.normal(ks[0], (2, 256, d), dtype=jnp.float32), 'g1': jnp.ones((d,), jnp.float32), 'g2': jnp.ones((d,), jnp.float32), 'Wq': jax.random.normal(ks[1], (d, d), jnp.float32) * s, 'Wkc': jax.random.normal(ks[2], (dc, d), jnp.float32) * s, 'Wvc': jax.random.normal(ks[3], (dc, d), jnp.float32) * s, 'Wo': jax.random.normal(ks[4], (d, d), jnp.float32) * s, 'Wr': jax.random.normal(ks[5], (e, d), jnp.float32) * s, 'expert_bias': jnp.zeros((e,), jnp.float32), 'sW1': jax.random.normal(ks[6], (f, d), jnp.float32) * s, 'sW2': jax.random.normal(ks[7], (d, f), jnp.float32) * s, 'sW3': jax.random.normal(ks[8], (f, d), jnp.float32) * s, 'eW1': jax.random.normal(ks[9], (e, f, d), jnp.float32) * s, 'eW2': jax.random.normal(ks[10], (e, d, f), jnp.float32) * s, 'eW3': jax.random.normal(ks[11], (e, f, d), jnp.float32) * s}
    _L1_ffn_all = _L1_ffn_setup()
    _L1_ffn_in = {k: v for k, v in _L1_ffn_all.items() if k in ('g1', 'g2', 'Wq', 'Wkc', 'Wvc', 'Wo', 'Wr', 'expert_bias', 'sW1', 'sW2', 'sW3', 'eW1', 'eW2', 'eW3')}
    del _L1_ffn_all
    return {'x': x, 'cond_64': cond_64, 'fside_16xSxS_0': fside_16xSxS_0, 'mask_BxS_bf1': mask_BxS_bf1, 'mask_BxS_bk0': mask_BxS_bk0, 'L0_cond_g_norm': _L0_cond_in['g_norm'], 'L0_cond_Wq': _L0_cond_in['Wq'], 'L0_cond_Wkv': _L0_cond_in['Wkv'], 'L0_cond_q_scale': _L0_cond_in['q_scale'], 'L0_cond_k_scale': _L0_cond_in['k_scale'], 'L0_cond_null_attn_bias': _L0_cond_in['null_attn_bias'], 'L0_cond_w0': _L0_cond_in['w0'], 'L0_cond_b0': _L0_cond_in['b0'], 'L0_cond_g0': _L0_cond_in['g0'], 'L0_cond_w1': _L0_cond_in['w1'], 'L0_cond_b1': _L0_cond_in['b1'], 'L0_cond_g1': _L0_cond_in['g1'], 'L0_cond_w2': _L0_cond_in['w2'], 'L0_cond_b2': _L0_cond_in['b2'], 'L0_cond_Wout': _L0_cond_in['Wout'], 'L0_cond_g_out': _L0_cond_in['g_out'], 'L0_ffn_W_fc': _L0_ffn_in['W_fc'], 'L0_ffn_W_proj': _L0_ffn_in['W_proj'], 'L1_cond_g_in': _L1_cond_in['g_in'], 'L1_cond_null_attn_bias': _L1_cond_in['null_attn_bias'], 'L1_cond_Wq': _L1_cond_in['Wq'], 'L1_cond_Wkv': _L1_cond_in['Wkv'], 'L1_cond_Wo': _L1_cond_in['Wo'], 'L1_cond_g_out': _L1_cond_in['g_out'], 'L1_ffn_g1': _L1_ffn_in['g1'], 'L1_ffn_g2': _L1_ffn_in['g2'], 'L1_ffn_Wq': _L1_ffn_in['Wq'], 'L1_ffn_Wkc': _L1_ffn_in['Wkc'], 'L1_ffn_Wvc': _L1_ffn_in['Wvc'], 'L1_ffn_Wo': _L1_ffn_in['Wo'], 'L1_ffn_Wr': _L1_ffn_in['Wr'], 'L1_ffn_expert_bias': _L1_ffn_in['expert_bias'], 'L1_ffn_sW1': _L1_ffn_in['sW1'], 'L1_ffn_sW2': _L1_ffn_in['sW2'], 'L1_ffn_sW3': _L1_ffn_in['sW3'], 'L1_ffn_eW1': _L1_ffn_in['eW1'], 'L1_ffn_eW2': _L1_ffn_in['eW2'], 'L1_ffn_eW3': _L1_ffn_in['eW3']}

def reference(x, cond_64, fside_16xSxS_0, mask_BxS_bf1, mask_BxS_bk0, L0_cond_g_norm, L0_cond_Wq, L0_cond_Wkv, L0_cond_q_scale, L0_cond_k_scale, L0_cond_null_attn_bias, L0_cond_w0, L0_cond_b0, L0_cond_g0, L0_cond_w1, L0_cond_b1, L0_cond_g1, L0_cond_w2, L0_cond_b2, L0_cond_Wout, L0_cond_g_out, L0_ffn_W_fc, L0_ffn_W_proj, L1_cond_g_in, L1_cond_null_attn_bias, L1_cond_Wq, L1_cond_Wkv, L1_cond_Wo, L1_cond_g_out, L1_ffn_g1, L1_ffn_g2, L1_ffn_Wq, L1_ffn_Wkc, L1_ffn_Wvc, L1_ffn_Wo, L1_ffn_Wr, L1_ffn_expert_bias, L1_ffn_sW1, L1_ffn_sW2, L1_ffn_sW3, L1_ffn_eW1, L1_ffn_eW2, L1_ffn_eW3):
    import jax
    import jax.numpy as jnp

    def _L0_cond_ref(x, mask, g_norm, Wq, Wkv, q_scale, k_scale, null_kv, null_attn_bias, w0, b0, g0, w1, b1, g1, w2, b2, Wout, g_out):
        import jax, jax.numpy as jnp
        import numpy as np
        DIM = 256
        HEADS = 16
        DIM_HEAD = 64
        SCALE = 8.0

        def ln(x, g, eps=1e-05):
            mean = x.mean(axis=-1, keepdims=True)
            var = ((x - mean) ** 2).mean(axis=-1, keepdims=True)
            return (x - mean) * jax.lax.rsqrt(var + eps) * g

        def l2norm(t):
            n = jnp.maximum(jnp.linalg.norm(t, axis=-1, keepdims=True), 1e-12)
            return t / n

        def rel_pos_bias(n, w0, b0, g0, w1, b1, g1, w2, b2, dtype):
            pos = jnp.arange(-n + 1, n, dtype=dtype)[:, None]
            h = jax.nn.silu(ln(pos @ w0 + b0, g0))
            h = jax.nn.silu(ln(h @ w1 + b1, g1))
            h = h @ w2 + b2
            i = jnp.arange(n)
            idx = i[:, None] - i[None, :] + n - 1
            bias = h[idx]
            return jnp.transpose(bias, (2, 0, 1))
        b, n, _ = x.shape
        xn = ln(x, g_norm)
        q = (xn @ Wq).reshape(b, n, HEADS, DIM_HEAD).transpose(0, 2, 1, 3)
        kv = xn @ Wkv
        k, v = (kv[..., :DIM_HEAD], kv[..., DIM_HEAD:])
        nk = jnp.broadcast_to(null_kv[0], (b, 1, DIM_HEAD))
        nv = jnp.broadcast_to(null_kv[1], (b, 1, DIM_HEAD))
        k = jnp.concatenate([nk, k], axis=1)
        v = jnp.concatenate([nv, v], axis=1)
        q = l2norm(q) * q_scale
        k = l2norm(k) * k_scale
        sim = jnp.einsum('bhid,bjd->bhij', q, k) * SCALE
        bias = rel_pos_bias(n, w0, b0, g0, w1, b1, g1, w2, b2, q.dtype)
        null_bias = jnp.broadcast_to(null_attn_bias[:, None, None], (HEADS, n, 1))
        attn_bias = jnp.concatenate([null_bias, bias], axis=-1)
        sim = sim + attn_bias
        neg = -jnp.finfo(sim.dtype).max
        causal = jnp.triu(jnp.ones((n, n + 1), dtype=bool), k=2)
        sim = jnp.where(causal, neg, sim)
        m = jnp.pad(mask, ((0, 0), (1, 0)), constant_values=True)[:, None, None, :]
        sim = jnp.where(m, sim, neg)
        attn = jax.nn.softmax(sim, axis=-1)
        out = jnp.einsum('bhij,bjd->bhid', attn, v)
        out = out.transpose(0, 2, 1, 3).reshape(b, n, HEADS * DIM_HEAD)
        return ln(out @ Wout, g_out)

    def _L0_ffn_ref(x, W_fc, W_proj):
        import jax, jax.numpy as jnp
        import numpy as np
        import math
        BETA = 0.9
        THRESHOLD = 1.0
        NUM_STEPS = 5
        ALPHA = 2.0

        @jax.custom_vjp
        def spike_fn(u):
            return (u > 0).astype(u.dtype)

        def _spike_fwd(u):
            return (spike_fn(u), u)

        def _spike_bwd(u, g):
            s = jnp.pi / 2.0 * ALPHA * u
            return (g * (ALPHA / 2.0) / (1.0 + s * s),)
        spike_fn.defvjp(_spike_fwd, _spike_bwd)
        h = jnp.square(jax.nn.relu(jnp.einsum('bsd,fd->bsf', x, W_fc)))
        y = jnp.einsum('bsf,df->bsd', h, W_proj)

        def step(mem, _):
            reset = jax.lax.stop_gradient(spike_fn(mem - THRESHOLD))
            mem_new = BETA * mem + y - reset * THRESHOLD
            spk = spike_fn(mem_new - THRESHOLD)
            return (mem_new, spk)
        mem0 = jnp.zeros_like(y)
        _, spks = jax.lax.scan(step, mem0, None, length=NUM_STEPS)
        return jnp.sum(spks, axis=0) / NUM_STEPS

    def _L1_cond_ref(x, attn_bias, mask, g_in, null_attn_bias, null_kv, Wq, Wkv, Wo, g_out):
        import jax, jax.numpy as jnp
        import numpy as np
        B, N, DIM, H, DH = (2, 512, 256, 16, 64)
        INNER = H * DH
        EPS = 1e-05

        def layernorm(x, g):
            mean = jnp.mean(x, axis=-1, keepdims=True)
            var = jnp.var(x, axis=-1, keepdims=True)
            return (x - mean) * jax.lax.rsqrt(var + EPS) * g
        b, n, _ = x.shape
        scale = DH ** (-0.5)
        xn = layernorm(x, g_in)
        q = (xn @ Wq).reshape(b, n, H, DH).transpose(0, 2, 1, 3) * scale
        kv = xn @ Wkv
        k, v = (kv[..., :DH], kv[..., DH:])
        nk = jnp.broadcast_to(null_kv[0], (b, 1, DH))
        nv = jnp.broadcast_to(null_kv[1], (b, 1, DH))
        k = jnp.concatenate([nk, k], axis=1)
        v = jnp.concatenate([nv, v], axis=1)
        sim = jnp.einsum('bhid,bjd->bhij', q, k)
        null_col = jnp.broadcast_to(null_attn_bias[:, None, None], (H, n, 1))
        bias = jnp.concatenate([null_col, attn_bias], axis=-1)
        sim = sim + bias
        neg = -jnp.finfo(sim.dtype).max
        j = n + 1
        causal_mask = jnp.triu(jnp.ones((n, j), dtype=bool), k=j - n + 1)
        sim = jnp.where(causal_mask, neg, sim)
        mask_p = jnp.pad(mask, ((0, 0), (1, 0)), constant_values=True)
        sim = jnp.where(mask_p[:, None, None, :], sim, neg)
        attn = jax.nn.softmax(sim, axis=-1)
        out = jnp.einsum('bhij,bjd->bhid', attn, v)
        out = out.transpose(0, 2, 1, 3).reshape(b, n, INNER)
        out = out @ Wo
        return layernorm(out, g_out)

    def _L1_ffn_ref(X, g1, g2, Wq, Wkc, Wvc, Wo, Wr, expert_bias, sW1, sW2, sW3, eW1, eW2, eW3):
        import jax, jax.numpy as jnp
        import numpy as np
        D_MODEL = 256
        NUM_HEADS = 4
        NUM_EXPERTS = 8
        TOP_K = 2
        D_FF = 256
        EPS = 1e-06

        def _rmsnorm(x, g):
            return x * jax.lax.rsqrt(jnp.mean(x * x, axis=-1, keepdims=True) + EPS) * g

        def _swiglu(x, w1, w2, w3):
            return jax.nn.silu(x @ w1.T) * (x @ w3.T) @ w2.T
        B, S, d = X.shape
        H = NUM_HEADS
        dk = d // H
        scale = 1.0 / jnp.sqrt(jnp.float32(dk))
        nx = _rmsnorm(X, g1)
        Q = (nx @ Wq.T).reshape(B, S, H, dk).transpose(0, 2, 1, 3)
        Kc = nx @ Wkc.T
        Vc = nx @ Wvc.T
        scores = jnp.einsum('bhsd,btd->bhst', Q, Kc) * scale
        attn = jax.nn.softmax(scores, axis=-1)
        out = jnp.einsum('bhst,btd->bhsd', attn, Vc)
        out = out.transpose(0, 2, 1, 3).reshape(B, S, d) @ Wo.T
        X = X + out
        nx = _rmsnorm(X, g2)
        xf = nx.reshape(-1, d)
        logits = xf @ Wr.T + expert_bias
        rw = jax.nn.softmax(logits, axis=-1)
        topw, topi = jax.lax.top_k(rw, TOP_K)
        topw = jax.nn.softmax(topw, axis=-1)
        combine = jnp.sum(jax.nn.one_hot(topi, NUM_EXPERTS, dtype=xf.dtype) * topw[..., None], axis=1)
        shared = _swiglu(xf, sW1, sW2, sW3)
        h = jax.nn.silu(jnp.einsum('td,efd->etf', xf, eW1)) * jnp.einsum('td,efd->etf', xf, eW3)
        eo = jnp.einsum('etf,edf->etd', h, eW2)
        specialist = jnp.einsum('te,etd->td', combine, eo)
        moe_out = (shared + specialist).reshape(B, S, d)
        return X + moe_out
    x = x + _L0_ffn_ref(_L0_cond_ref(x, mask_BxS_bf1, L0_cond_g_norm, L0_cond_Wq, L0_cond_Wkv, L0_cond_q_scale, L0_cond_k_scale, cond_64, L0_cond_null_attn_bias, L0_cond_w0, L0_cond_b0, L0_cond_g0, L0_cond_w1, L0_cond_b1, L0_cond_g1, L0_cond_w2, L0_cond_b2, L0_cond_Wout, L0_cond_g_out), L0_ffn_W_fc, L0_ffn_W_proj)
    x = x + _L1_ffn_ref(_L1_cond_ref(x, fside_16xSxS_0, mask_BxS_bk0, L1_cond_g_in, L1_cond_null_attn_bias, cond_64, L1_cond_Wq, L1_cond_Wkv, L1_cond_Wo, L1_cond_g_out), L1_ffn_g1, L1_ffn_g2, L1_ffn_Wq, L1_ffn_Wkc, L1_ffn_Wvc, L1_ffn_Wo, L1_ffn_Wr, L1_ffn_expert_bias, L1_ffn_sW1, L1_ffn_sW2, L1_ffn_sW3, L1_ffn_eW1, L1_ffn_eW2, L1_ffn_eW3)
    return x

_drawn_inputs = setup_inputs


def setup_inputs(seed=0):
    import zlib

    import numpy as np

    out = dict(_drawn_inputs(seed))
    spreads = {'L0_cond_g_norm': (1.0, 0.2),
     'L0_cond_q_scale': (1.0, 0.2),
     'L0_cond_k_scale': (1.0, 0.2),
     'L0_cond_b0': (0.0, 0.1),
     'L0_cond_g0': (1.0, 0.6),
     'L0_cond_b1': (0.0, 0.268),
     'L0_cond_g1': (1.0, 0.6),
     'L0_cond_b2': (0.0, 0.319),
     'L0_cond_g_out': (1.0, 0.2),
     'L1_cond_g_in': (1.0, 0.6),
     'L1_cond_g_out': (1.0, 0.2),
     'L1_ffn_g1': (1.0, 0.6),
     'L1_ffn_g2': (1.0, 0.6),
     'L1_ffn_expert_bias': (0.0, 0.8)}
    factors = {'L1_ffn_Wq': 8.0,
     'L1_ffn_Wkc': 8.0,
     'L1_ffn_Wr': 8.0,
     'L1_ffn_sW1': 4.429,
     'L1_ffn_sW2': 4.478,
     'L1_ffn_sW3': 5.85,
     'L1_ffn_eW1': 7.494,
     'L1_ffn_eW2': 7.746,
     'L1_ffn_eW3': 6.866}
    for name, (base, spread) in spreads.items():
        noise = np.random.default_rng([zlib.crc32(name.encode()), seed]).standard_normal(out[name].shape)
        drawn = base * np.exp(spread * noise) if base else spread * noise
        out[name] = jnp.asarray(drawn.astype(out[name].dtype))
    for name, factor in factors.items():
        out[name] = (out[name] * factor).astype(out[name].dtype)
    return out
```

```python
from contextlib import ExitStack

import concourse.bass as bass
import numpy as np
from concourse import mybir

F32 = mybir.dt.float32
F32R = mybir.dt.float32r
BF16 = mybir.dt.bfloat16
U8 = mybir.dt.uint8
I32 = mybir.dt.int32
ALU = mybir.AluOpType
ACT = mybir.ActivationFunctionType
AX = mybir.AxisListType

P = 128
SEQS, S, D = 64, 64, 256
TILES = SEQS * S // P
KD = D // P
H, DH = 16, 64
INNER = H * DH
CH = INNER // P
KVN = 2 * DH + H
FF = 4 * D
FC = FF // P
G4 = 4
GROUPS = TILES // G4
GT = G4 * P
HB = 4
CB = HB * DH // P
QKV = D + 2 * DH
E = 8
EP = E + 1
NEG = -1e30
LIF_STEPS, LIF_BETA, LIF_THRESHOLD = 5, 0.9, 1.0

BLK = 2 * TILES

CONSTANTS = 13

PASSES = ((0, 0), (0, 1), (1, 0))


def reach(eng, sem, n):
    if not isinstance(n, int) or n > 0:
        eng.wait_ge(sem, n)


def spread(t, par):
    return 32 * (t - par) + 64


def live(t):
    return not isinstance(t, int) or 0 <= t < TILES


def pipeline(eng, body, ahead, behind):
    first, last = behind + 1, TILES - ahead
    first += first % 2
    last -= last % 2
    for i in range(-ahead, first):
        body(i, i % 2)
    with eng.Fori(first // 2, last // 2) as pair:
        body(2 * pair, 0)
        body(2 * pair + 1, 1)
    for i in range(last, TILES + behind):
        body(i, i % 2)


def build(nc, a, out):
    ctx = ExitStack()
    with ctx:
        base = -(-nc.sbuf_base // 64) * 64
        place = {}

        def region(name, nbytes, at=None):
            nonlocal base
            if at is None:
                at, base = base, base + nbytes
            place[name] = [at, at + nbytes]
            return at

        def sb(where, name, shape, dt):
            n = int(np.prod(shape[1:])) * (1 if dt == U8 else 2 if dt == BF16 else 4)
            at, end = place[where]
            place[where][0] = at + -(-n // 32) * 32
            assert place[where][0] <= end, (where, name, place[where][0] - end)
            return nc.alloc_sbuf_tensor_at(name, shape, dt, offset=at)

        K = 1024
        region("x", 32 * K)
        region("o", 32 * K)
        region("stage", 18 * K)
        region("bias", 4 * K)
        region("const", 13 * K)
        work = region("work", 41 * K)
        attw = region("attw", 35 * K)
        ffw = region("ffw", 32 * K)
        assert base <= 229344, base
        region("ffn_work", 41 * K, at=work)
        region("blk_w", 32 * K, at=ffw)
        region("xft", 75 * K, at=work)
        assert attw == work + 41 * K

        X = sb("x", "X", [P, TILES, D], F32)
        O = sb("o", "O", [P, TILES, D], F32)

        sems = {}

        def sem(name):
            if name not in sems:
                sems[name] = ctx.enter_context(nc.semaphore(name))
            return sems[name]

        def apart(eng, *waits):
            for signal, n in waits:
                reach(eng, signal, n)
                eng.sem_inc(sem("apart"), 1)

        psQ = ctx.enter_context(nc.psum_tensor("psQ", [P, 2, 512], F32))
        psS = ctx.enter_context(nc.psum_tensor("psS", [P, 2, 512], F32))
        psT = ctx.enter_context(nc.psum_tensor("psT", [P, 2, 512], F32))
        psW = ctx.enter_context(nc.psum_tensor("psW", [P, 512], F32))
        psM = ctx.enter_context(nc.psum_tensor("psM", [P, 512], F32))

        ident = sb("const", "ident", [P, P], F32)
        sel_f = sb("const", "sel_f", [P, P], F32)
        sel = sb("const", "sel", [P, P], F32R)
        ind_f = sb("const", "ind_f", [2, P], F32)
        ind = sb("const", "ind", [2, P], BF16)
        rms_eps = sb("const", "rms_eps", [P, 1], F32)
        ln_eps = sb("const", "ln_eps", [P, 1], F32)
        mhalf = sb("const", "mhalf", [P, 32], F32)
        mask_w = sb("const", "mask_w", [2, TILES, S // 4], I32)
        negmask = sb("const", "negmask", [2, TILES, S], BF16)
        bias_t = sb("bias", "bias_t", [P, H, S], F32R)
        gcol = sb("const", "gcol", [P, KD], F32)
        nkb = sb("const", "nkb", [P, DH], F32)
        nvb = sb("const", "nvb", [P, DH], F32)
        nvcol = sb("const", "nvcol", [P, 1], F32)
        nbias = sb("const", "nbias", [P, H], F32)
        ksc = sb("const", "ksc", [P, 1], F32)
        qsc = sb("const", "qsc", [P, 1], F32)
        ksrow = sb("const", "ksrow", [P, DH], F32)
        qsrow = sb("const", "qsrow", [P, DH], F32)
        tiny = sb("const", "tiny", [P, 8], F32)

        wq = [sb("attw", f"wq{i}", [P, KD, INNER], F32R) for i in range(2)]
        wkvn = [sb("attw", f"wkvn{i}", [P, KD, KVN], F32R) for i in range(2)]
        wout = [sb("attw", f"wout{i}", [P, CH, D], F32R) for i in range(2)]
        st6 = sb("work", "st6", [P, 6], F32)
        mv = [sb("work", f"mv{i}", [P, 2], F32) for i in range(2)]
        vareps = sb("work", "vareps", [P, 1], F32)
        rstd = [sb("work", f"rstd{i}", [P, 1], F32) for i in range(2)]
        xn = sb("work", "xn", [P, D], F32)
        xT = [sb("work", f"xT{i}", [P, KD, P], F32R) for i in range(2)]
        kvs = sb("work", "kvs", [P, KVN], F32)
        junk = sb("work", "junk", [P, DH], F32)
        sq = sb("work", "sq", [P, INNER], F32)
        qss = sb("work", "qss", [P, H + 1], F32)
        qmx = sb("work", "qmx", [P, H + 1], F32)
        rq = sb("work", "rq", [P, H + 1], F32)
        qn = sb("work", "qn", [P, INNER], F32)
        kn = sb("work", "kn", [P, 2, DH], F32)
        snr = sb("work", "snr", [P, H], F32)
        sn = [sb("work", f"sn{i}", [P, H], F32) for i in range(2)]
        vp = [sb("work", f"vp{i}", [P, DH], F32) for i in range(2)]
        vv = [sb("work", f"vv{i}", [P, 2, DH], F32) for i in range(2)]
        qT = sb("work", "qT", [P, CH, P], F32)
        kT = sb("work", "kT", [P, P], F32)
        m16 = sb("work", "m16", [P, H], F32)
        mm16 = sb("work", "mm16", [P, H], F32)
        ex = sb("work", "ex", [P, H, S + 1], F32)
        den = sb("work", "den", [P, H], F32)
        rden = sb("work", "rden", [P, H], F32)
        pn = sb("work", "pn", [P, H, S], F32)
        pT = sb("work", "pT", [P, CH, P], F32)
        oT = [sb("work", f"oT{i}", [P, CH, P], F32R) for i in range(2)]

        wfc = [sb("ffw", f"wfc{i}", [P, KD, FF], F32R) for i in range(2)]
        wpr = [sb("ffw", f"wpr{i}", [P, FC, D], F32R) for i in range(2)]
        gout0 = sb("const", "gout0", [P, KD], F32)
        c0 = sb("ffn_work", "c0", [P, G4, D], F32)
        cT = [sb("ffn_work", f"cT{i}", [P, KD, GT], F32R) for i in range(2)]
        hf = [sb("ffn_work", f"hf{i}", [P, GT], F32) for i in range(2)]
        hT = [[sb("ffn_work", f"hT{i}{j}", [P, GT], F32R) for j in range(2)] for i in range(2)]
        cur = sb("ffn_work", "cur", [P, G4 * D], F32)
        mem = sb("ffn_work", "mem", [P, G4 * D], F32)
        spk = [sb("ffn_work", f"spk{i}", [P, G4 * D], BF16) for i in range(2)]
        count = sb("ffn_work", "count", [P, G4 * D], BF16)
        up_bank = (psQ[:, 0, :], psQ[:, 1, :], psW[:], psM[:])
        fst6 = sb("ffn_work", "fst6", [P, G4, 6], F32)
        fmv = sb("ffn_work", "fmv", [P, G4, 2], F32)
        fve = sb("ffn_work", "fve", [P, G4], F32)
        frs = sb("ffn_work", "frs", [P, G4], F32)

        bqkv = [sb("blk_w", f"bqkv{i}", [P, KD, QKV], F32R) for i in range(2)]
        bwo = [sb("blk_w", f"bwo{i}", [P, KD, D], F32R) for i in range(2)]
        bwr = sb("blk_w", "bwr", [P, KD, E], F32)
        gout1 = sb("blk_w", "gout1", [P, D], F32)
        g1col = sb("blk_w", "g1col", [P, KD], F32)
        g2col = sb("const", "g2col", [P, KD], F32)
        ebias = sb("const", "ebias", [P, E], F32)
        dst6 = sb("blk_w", "dst6", [P, 6], F32)
        dmv = [sb("blk_w", f"dmv{i}", [P, 2], F32) for i in range(2)]
        dvar = sb("blk_w", "dvar", [P, 1], F32)
        drs = [sb("blk_w", f"drs{i}", [P, 1], F32) for i in range(2)]
        ss1 = [sb("blk_w", f"ss1{i}", [P, 1], F32) for i in range(2)]
        ms1 = sb("blk_w", "ms1", [P, 1], F32)
        r1 = [sb("blk_w", f"r1{i}", [P, 1], F32) for i in range(2)]
        ss2 = [sb("blk_w", f"ss2{i}", [P, 1], F32) for i in range(2)]
        ms2 = sb("blk_w", "ms2", [P, 1], F32)
        r2 = [sb("blk_w", f"r2{i}", [P, 1], F32) for i in range(2)]
        sqj = [sb("blk_w", f"sqj{i}", [P, D], F32) for i in range(2)]
        nx = sb("blk_w", "nx", [P, D], F32)
        nxT = [sb("blk_w", f"nxT{i}", [P, KD, P], F32R) for i in range(2)]
        bq = sb("blk_w", "bq", [P, D], F32)
        bk = sb("blk_w", "bk", [P, 2, DH], F32)
        bqT = sb("blk_w", "bqT", [P, CB, P], F32)
        bkT = sb("blk_w", "bkT", [P, P], F32)
        bm = sb("blk_w", "bm", [P, HB], F32)
        be = sb("blk_w", "be", [P, HB, S], F32)
        bden = sb("blk_w", "bden", [P, HB], F32)
        brd = sb("blk_w", "brd", [P, HB], F32)
        bpn = sb("blk_w", "bpn", [P, HB, S], F32)
        bpT = sb("blk_w", "bpT", [P, CB, P], F32)
        bvv = [sb("blk_w", f"bvv{i}", [P, 2, DH], F32) for i in range(2)]
        boT = [sb("blk_w", f"boT{i}", [P, CB, P], F32R) for i in range(2)]
        xf = sb("blk_w", "xf", [P, D], F32)
        xff = sb("blk_w", "xff", [P, KD, P], F32)
        xfT = [sb("xft", f"xfT{i}", [P, KD, TILES * P], F32R) for i in range(2)]
        v_all = sb("xft", "v_all", [P, TILES, DH], F32)

        logits = sb("const", "logits", [P, TILES, E], F32)
        comb = sb("const", "comb", [P, TILES, EP], F32)
        iota8 = sb("const", "iota8", [P, E], F32)

        region("moe_w", 32 * K, at=place["o"][1] - 32 * K)
        ew = [[sb("moe_w", f"ew{i}{j}", [P, 3, KD, D], F32R) for j in range(2)] for i in range(2)]
        rt = [sb("moe_w", f"rt{i}", [P, TILES, E], F32) for i in range(4)]
        rc = [sb("moe_w", f"rc{i}", [P, TILES], F32) for i in range(6)]
        region("moe_t", 32 * K, at=place["blk_w"][1] - 32 * K)
        sg = [sb("moe_t", f"sg{i}", [P, GT], F32) for i in range(2)]
        eT = [[sb("moe_t", f"eT{i}{j}", [P, KD, GT], F32R) for j in range(2)] for i in range(2)]
        cw = sb("moe_t", "cw", [P, G4], F32)

        raw_q = nc.alloc_sbuf_tensor_at("raw_q", [P, KD, INNER], F32, offset=place["stage"][0])
        raw_kvn = nc.alloc_sbuf_tensor_at("raw_kvn", [P, KD, KVN], F32, offset=place["stage"][0] + 8 * K)
        raw_o = nc.alloc_sbuf_tensor_at("raw_o", [P, CH, D], F32, offset=place["stage"][0] + 8 * K + 1152)
        raw_bqkv = nc.alloc_sbuf_tensor_at("raw_bqkv", [P, KD, QKV], F32, offset=place["stage"][0])
        raw_bwo = nc.alloc_sbuf_tensor_at("raw_bwo", [P, KD, D], F32, offset=place["stage"][0] + 3 * K)
        raw_e = [nc.alloc_sbuf_tensor_at(f"raw_e{i}", [P, 3, KD, D], F32, offset=place["stage"][0] + 6 * K * i + 5 * K) for i in range(2)]
        rp = place["o"][1] - 32 * K
        NPOS = 2 * S - 1
        region("relpos", 32 * K, at=rp)
        r_w1 = sb("relpos", "r_w1", [P, KD, D], F32)
        r_w2 = sb("relpos", "r_w2", [P, KD, H], F32)
        r_rows = {n: sb("relpos", f"r_{n}", [P, D], F32) for n in ("w0", "b0", "g0", "b1", "g1")}
        r_b2 = sb("relpos", "r_b2", [H, 1], F32)
        r_pos = sb("relpos", "r_pos", [P, 1], F32)
        r_h = sb("relpos", "r_h", [P, D], F32)
        r_hT = sb("relpos", "r_hT", [P, KD, P], F32)
        r_st = sb("relpos", "r_st", [P, 6], F32)
        r_mv = sb("relpos", "r_mv", [P, 2], F32)
        r_rs = sb("relpos", "r_rs", [P, 2], F32)
        r_out = sb("relpos", "r_out", [H, P], F32)
        braw0 = sb("relpos", "braw0", [P, H, S], F32)
        wn_tmp = sb("relpos", "wn_tmp", [P, H, DH], F32)
        rel_dram = nc.dram_tensor("rel_bias", (H, S, P), F32, kind="Internal").ap()

        x_dram = a["x"].rearrange("(t p) d -> p t d", p=P)
        out_dram = out.rearrange("(t p) d -> p t d", p=P)

        LAYERS = (
            dict(n="a", done=0, cosine=True, mask="mask0", g="g_norm", wq="Wq0", wkv="Wkv0", wo="Wout0", nb="nb0"),
            dict(n="c", done=TILES, cosine=False, mask="mask1", g="g_in", wq="Wq1", wkv="Wkv1", wo="Wo1", nb="nb1"),
        )

        LOADED = {"a": 16 * 16, "c": 16 * 10}

        block = ctx.enter_context(nc.Block())

        @block.sync
        def _(sp):
            def load_layer(L):
                ld = sem(L["n"] + "_loaded")
                sp.dma_start(gcol[:], a[L["g"]].rearrange("(k p) -> p k", p=P), allow_slow_non_contiguous=True).then_inc(ld, 16)
                sp.dma_start(nkb[:], a["null"][0:1, :].to_broadcast([P, DH])).then_inc(ld, 16)
                sp.dma_start(nvb[:], a["null"][1:2, :].to_broadcast([P, DH])).then_inc(ld, 16)
                for half in range(2):
                    sp.dma_start(nvcol[half * DH:(half + 1) * DH, :], a["null"][1:2, :].rearrange("o d -> d o"),
                                 allow_slow_non_contiguous=True).then_inc(ld, 16)
                sp.dma_start(nbias[:], a[L["nb"]].rearrange("(o h) -> o h", o=1).to_broadcast([P, H])).then_inc(ld, 16)
                sp.dma_start(mask_w[:], a[L["mask"]].rearrange("(t b) j -> b t j", b=2)).then_inc(ld, 16)
                sp.dma_start(raw_q[:], a[L["wq"]].rearrange("(k p) n -> p k n", p=P)).then_inc(ld, 16)
                sp.dma_start(raw_kvn[:, :, 0:2 * DH], a[L["wkv"]].rearrange("(k p) n -> p k n", p=P)).then_inc(ld, 16)
                sp.dma_start(raw_o[:], a[L["wo"]].rearrange("(k p) n -> p k n", p=P)).then_inc(ld, 16)

            def load_ffn():
                sp.wait_ge(sem("a_wlo"), 2 * KD + 1)
                sp.dma_start(gout0[:], a["g_out0"].rearrange("(k p) -> p k", p=P), allow_slow_non_contiguous=True).then_inc(sem("f_loaded"), 16)
                sp.dma_start(raw_q[:], a["Wfc"].rearrange("(k p) n -> p k n", p=P)).then_inc(sem("f_loaded"), 16)
                sp.dma_start(raw_o[:], a["Wproj"].rearrange("(k p) n -> p k n", p=P)).then_inc(sem("f_loaded"), 16)

            def load_block():
                sp.wait_ge(sem("c_wlo"), 2 * KD + 1)
                ld = sem("d_loaded")
                for col, name in ((g1col, "g1"), (g2col, "g2")):
                    sp.dma_start(col[:], a[name].rearrange("(k p) -> p k", p=P), allow_slow_non_contiguous=True).then_inc(ld, 16)
                sp.dma_start(gout1[:], a["g_out1"].rearrange("(o d) -> o d", o=1).to_broadcast([P, D])).then_inc(ld, 16)
                sp.dma_start(ebias[:], a["ebias"].rearrange("(o e) -> o e", o=1).to_broadcast([P, E])).then_inc(ld, 16)
                sp.dma_start(raw_bqkv[:], a["Wqkv"].rearrange("(k p) n -> p k n", p=P)).then_inc(ld, 16)
                sp.dma_start(raw_bwo[:], a["Wo"].rearrange("(k p) n -> p k n", p=P)).then_inc(ld, 16)
                sp.dma_start(bwr[:], a["Wr"].rearrange("(k p) n -> p k n", p=P)).then_inc(ld, 16)

            def spread_v(L, before_loop):
                n = L["n"]
                done = L["done"]

                def step(t, par):
                    apart(sp, (sem("t_vp"), done + t + 1))
                    reach(sp, sem("t_pv"), done + t - 1)
                    for half in range(2):
                        for b in range(2):
                            sp.dma_start(vv[par][half * DH:(half + 1) * DH, b, :],
                                         vp[par][b * S:(b + 1) * S, :]).then_inc(sem(f"t_vv{par}"), 16)

                for t in range(2):
                    step(t, t)
                before_loop()
                with sp.Fori(1, TILES // 2) as pair:
                    step(2 * pair, 0)
                    step(2 * pair + 1, 1)

            sp.dma_start(X[:, 0:4, :], x_dram[:, 0:4, :]).then_inc(sem("x_in0"), 16)
            load_layer(LAYERS[0])
            for half in range(2):
                for row, name in ((ksc, "k_scale"), (qsc, "q_scale")):
                    sp.dma_start(row[half * DH:(half + 1) * DH, :], a[name].rearrange("(d o) -> d o", o=1),
                                 allow_slow_non_contiguous=True).then_inc(sem("a_loaded"), 16)
            for row, name in ((ksrow, "k_scale"), (qsrow, "q_scale")):
                sp.dma_start(row[:], a[name].rearrange("(o d) -> o d", o=1).to_broadcast([P, DH])).then_inc(sem("a_loaded"), 16)
            for name, key in (("w0", "rw0"), ("b0", "rb0"), ("g0", "rg0"), ("b1", "rb1"), ("g1", "rg1")):
                sp.dma_start(r_rows[name][:], a[key].rearrange("(o d) -> o d", o=1).to_broadcast([P, D])).then_inc(sem("rel_loaded"), 16)
            sp.dma_start(r_w1[:], a["rw1"].rearrange("(k p) n -> p k n", p=P)).then_inc(sem("rel_loaded"), 16)
            sp.dma_start(r_w2[:], a["rw2"].rearrange("(k p) n -> p k n", p=P)).then_inc(sem("rel_loaded"), 16)
            sp.dma_start(r_b2[:], a["rb2"].rearrange("(h o) -> h o", o=1), allow_slow_non_contiguous=True).then_inc(sem("rel_loaded"), 16)
            sp.dma_start(X[:, 4:16, :], x_dram[:, 4:16, :]).then_inc(sem("x_in1"), 16)
            sp.dma_start(X[:, 16:32, :], x_dram[:, 16:32, :]).then_inc(sem("x_in2"), 16)
            sp.wait_ge(sem("rel_out"), 1)
            sp.dma_start(rel_dram, r_out[:].unsqueeze(1).to_broadcast([H, S, P])).then_inc(sem("rel_stored"), 16)
            sp.wait_ge(sem("rel_stored"), 16)
            for half in range(2):
                sp.dma_start(braw0[half * S:(half + 1) * S, :, :],
                             bass.AP(rel_dram.tensor, S - 1, [[P - 1, S], [S * P, H], [1, S]])).then_inc(sem("braw_a"), 16)
            spread_v(LAYERS[0], before_loop=load_ffn)
            sp.wait_ge(sem("f_wlo"), KD + 1)
            sp.wait_ge(sem("t_oev"), TILES)
            load_layer(LAYERS[1])
            sp.wait_ge(sem("f_c0"), GROUPS)
            for half in range(2):
                sp.dma_start(braw0[half * S:(half + 1) * S, :, :], a["fside"].rearrange("h i j -> i h j")).then_inc(sem("braw_c"), 16)
            spread_v(LAYERS[1], before_loop=load_block)
            def load_expert(p, par):
                for j, w in enumerate(("W1", "W3", "W2")):
                    sp.dma_start(raw_e[par][:, j, :, :], a[w][p].rearrange("(k p) n -> p k n", p=P)).then_inc(sem(f"e_loaded{par}"), 16)

            sp.wait_ge(sem("d_wlo"), 2)
            load_expert(0, 0)
            load_expert(1, 1)

            def spread_block_v(t, par):
                apart(sp, (sem("t_vp"), BLK + t + 1))
                reach(sp, sem("t_pv"), BLK + t - 1)
                for half in range(2):
                    for b in range(2):
                        sp.dma_start(bvv[par][half * DH:(half + 1) * DH, b, :],
                                     v_all[b * S:(b + 1) * S, t, :]).then_inc(sem(f"t_vv{par}"), 16)

            for t in range(2):
                spread_block_v(t, t)
            with sp.Fori(1, TILES // 2) as pair:
                spread_block_v(2 * pair, 0)
                spread_block_v(2 * pair + 1, 1)
            with sp.Fori(1, 4) as pair:
                sp.wait_ge(sem("e_wlo"), 2 * pair - 1)
                load_expert(2 * pair, 0)
                sp.wait_ge(sem("e_wlo"), 2 * pair)
                load_expert(2 * pair + 1, 1)
            sp.wait_ge(sem("e_wlo"), EP - 2)
            load_expert(EP - 1, 0)
            for g in range(GROUPS):
                sp.wait_ge(sem("e_acc"), GROUPS * (EP - 1) + g + 1)
                sp.dma_start(out_dram[:, G4 * g:G4 * g + G4, :], X[:, G4 * g:G4 * g + G4, :]).then_inc(sem("stored"), 16)
            sp.wait_ge(sem("stored"), 16 * GROUPS)

        @block.gpsimd
        def _(pool):
            c = sem("const_pool")
            nc.gpsimd.memset(ident[:], 0.0).then_inc(c, 1)
            nc.gpsimd.memset(sel_f[:], 0.0).then_inc(c, 1)
            nc.gpsimd.memset(ind_f[:], 1.0).then_inc(c, 1)
            nc.gpsimd.memset(mhalf[:], -0.5).then_inc(c, 1)
            nc.gpsimd.memset(ln_eps[:], 1e-5).then_inc(c, 1)
            nc.gpsimd.memset(rms_eps[:], 1e-6).then_inc(c, 1)
            nc.gpsimd.iota(r_pos[:], pattern=[[0, 1]], base=S - 1, channel_multiplier=-1,
                           allow_small_or_imprecise_dtypes=True).then_inc(c, 1)
            pool.wait_ge(c, 7)
            nc.gpsimd.affine_select(out=ident[:], in_=ident[:], compare_op=ALU.not_equal, fill=1.0, base=0,
                                    pattern=[[-1, P]], channel_multiplier=1).then_inc(c, 1)
            nc.gpsimd.affine_select(out=ind_f[:], in_=ind_f[:], compare_op=ALU.is_ge, fill=0.0, base=0,
                                    pattern=[[1, P]], channel_multiplier=-S).then_inc(c, 1)
            for n, off in enumerate((0, S, -S)):
                pool.wait_ge(c, 9 + n)
                nc.gpsimd.affine_select(out=sel_f[:], in_=sel_f[:], compare_op=ALU.not_equal, fill=1.0, base=off,
                                        pattern=[[-1, P]], channel_multiplier=1).then_inc(c, 1)
            nc.gpsimd.affine_select(out=ind_f[:], in_=ind_f[:], compare_op=ALU.is_ge, fill=0.0, base=S - 1,
                                    pattern=[[-1, P]], channel_multiplier=S).then_inc(c, 1)


            pool.wait_ge(sem("nk_ss"), 1)
            nc.gpsimd.tensor_tensor(tiny[:, 2:3], tiny[:, 1:2], mhalf[:, 0:1], ALU.pow).then_inc(sem("nk_r"), 1)
            for k in range(2):
                pool.wait_ge(sem("rel_mv"), k + 1)
                nc.gpsimd.tensor_scalar(r_rs[:, 0:1], r_mv[:, 1:2], 1.0, 1e-5, ALU.mult, ALU.add).then_inc(sem("rel_ve"), 1)
                pool.wait_ge(sem("rel_ve"), k + 1)
                nc.gpsimd.tensor_tensor(r_rs[:, 1:2], r_rs[:, 0:1], mhalf[:, 0:1], ALU.pow).then_inc(sem("rel_rstd"), 1)

            def causal(table, wait, done):
                pool.wait_ge(*wait)
                for half in range(2):
                    v = table[half * S:(half + 1) * S, :, :]
                    nc.gpsimd.affine_select(out=v, in_=v, compare_op=ALU.is_ge, fill=NEG, base=0,
                                            pattern=[[0, H], [-1, S]], channel_multiplier=1).then_inc(done, 1)

            causal(braw0, (sem("braw_a"), 32), sem("a_causal"))

            def attention(L):
                n = L["n"]
                done = L["done"]

                def step(i, par):
                    t = i - 2
                    if live(t):
                        pool.wait_ge(sem("t_rden"), done + t + 1)
                        reach(pool, sem("t_pTp"), done + t)
                        nc.gpsimd.tensor_tensor(pn[:], ex[:, :, 0:S], rden[:].unsqueeze(2).to_broadcast([P, H, S]),
                                                ALU.mult).then_inc(sem("t_pn"), 1)
                    t = i
                    if live(t) and L["cosine"]:
                        pool.wait_ge(sem("t_qmx"), done + t + 1)
                        reach(pool, sem("t_sn"), done + t)
                        nc.gpsimd.tensor_tensor(rq[:], qmx[:], mhalf[:, 0:H + 1], ALU.pow).then_inc(sem("t_rq"), 1)
                    t = i + 2
                    if live(t):
                        pool.wait_ge(sem("t_mv"), done + t + 1)
                        reach(pool, sem("t_rstd"), done + t)
                        nc.gpsimd.tensor_tensor(vareps[:], mv[par][:, 1:2], ln_eps[:], ALU.add).then_inc(sem("t_ve"), 1)
                        pool.wait_ge(sem("t_ve"), done + t + 1)
                        reach(pool, sem("t_xn"), done + t - 1)
                        nc.gpsimd.tensor_tensor(rstd[par][:], vareps[:], mhalf[:, 0:1], ALU.pow).then_inc(sem("t_rstd"), 1)

                pipeline(pool, step, 2, 3)

            attention(LAYERS[0])
            def ffn_norm(g):
                pool.wait_ge(sem("f_mv"), G4 * g + G4)
                nc.gpsimd.tensor_tensor(fve[:], fmv[:, :, 1], ln_eps[:].to_broadcast([P, G4]), ALU.add).then_inc(sem("f_ve"), 1)
                pool.wait_ge(sem("f_ve"), g + 1)
                nc.gpsimd.tensor_tensor(frs[:], fve[:], mhalf[:, 0:G4], ALU.pow).then_inc(sem("f_rs"), 1)

            def ffn_lo(s, par):
                pool.wait_ge(sem("f_hi"), s + 1)
                nc.gpsimd.tensor_tensor(hT[par][1][:], hf[par][:], hT[par][0][:].bitcast(F32), ALU.subtract).then_inc(sem("f_lo"), 1)

            def add_spikes(g, k):
                pool.wait_ge(sem("f_lif"), 13 * g + 3 * k + 4)
                if k == 0:
                    reach(pool, sem("f_x1"), g)
                    nc.gpsimd.tensor_tensor(count[:], spk[0][:], spk[1][:], ALU.add).then_inc(sem("f_count"), 1)
                else:
                    pool.wait_ge(sem("f_count"), 4 * g + k)
                    nc.gpsimd.tensor_tensor(count[:], count[:], spk[(k + 1) % 2][:], ALU.add).then_inc(sem("f_count"), 1)

            def ffn(g, first=False, last=False):
                for f in range(FC):
                    ffn_lo(FC * g + f, f % 2)
                    if not last and f == 0:
                        ffn_norm(g + 1)
                    if not first and f in (2, 4, 5, 7):
                        add_spikes(g - 1, (2, 4, 5, 7).index(f))

            ffn_norm(0)
            ffn(0, first=True)
            ffn(1)
            with pool.Fori(2, GROUPS - 1) as g:
                ffn(g)
            ffn(GROUPS - 1, last=True)
            for k in range(4):
                add_spikes(GROUPS - 1, k)
            pool.wait_ge(sem("f_count"), 4 * GROUPS)
            causal(braw0, (sem("braw_c"), 32), sem("c_causal"))
            attention(LAYERS[1])
            def mean_root(n, t, par, ss, ms, r, used):
                pool.wait_ge(sem(f"d_ss{n}"), t + 1)
                reach(pool, sem(f"d_r{n}"), t)
                nc.gpsimd.tensor_tensor(ms[:], ss[par][:], rms_eps[:], ALU.add).then_inc(sem(f"d_ms{n}"), 1)
                pool.wait_ge(sem(f"d_ms{n}"), t + 1)
                reach(pool, sem(used), t - 1)
                nc.gpsimd.tensor_tensor(r[par][:], ms[:], mhalf[:, 0:1], ALU.pow).then_inc(sem(f"d_r{n}"), 1)

            def block_step(i, par):
                other = (par + 1) % 2
                t = i - 4
                if live(t):
                    pool.wait_ge(sem("t_rden"), BLK + t + 1)
                    reach(pool, sem("t_pTp"), BLK + t)
                    nc.gpsimd.tensor_tensor(bpn[:], be[:], brd[:].unsqueeze(2).to_broadcast([P, HB, S]), ALU.mult).then_inc(sem("t_pn"), 1)
                t = i - 7
                if live(t):
                    pool.wait_ge(sem("d_X1"), t + 1)
                    nc.gpsimd.tensor_tensor(X[:, t, :], X[:, t, :], O[:, t, :], ALU.add).then_inc(sem("d_R"), 1)
                t = i - 7
                if live(t):
                    mean_root(2, t, other, ss2, ms2, r2, "d_xf")
                t = i + 4
                if live(t):
                    pool.wait_ge(sem("t_mv"), BLK + t + 1)
                    reach(pool, sem("t_rstd"), BLK + t)
                    nc.gpsimd.tensor_tensor(dvar[:], dmv[par][:, 1:2], ln_eps[:], ALU.add).then_inc(sem("t_ve"), 1)
                    pool.wait_ge(sem("t_ve"), BLK + t + 1)
                    reach(pool, sem("d_X0"), t - 1)
                    nc.gpsimd.tensor_tensor(drs[par][:], dvar[:], mhalf[:, 0:1], ALU.pow).then_inc(sem("t_rstd"), 1)
                t = i + 2
                if live(t):
                    mean_root(1, t, par, ss1, ms1, r1, "d_nx")
                t = i + 3
                if live(t):
                    pool.wait_ge(sem("d_X0"), t + 1)
                    nc.gpsimd.tensor_tensor(O[:, t, :], O[:, t, :], gout1[:], ALU.mult).then_inc(sem("d_X"), 1)

            nc.gpsimd.iota(iota8[:], pattern=[[1, E]], base=0, channel_multiplier=0,
                           allow_small_or_imprecise_dtypes=True).then_inc(sem("d_iota"), 1)
            pipeline(pool, block_step, 4, 10)
            def expert_lo(s, par):
                for c in range(KD):
                    pool.wait_ge(sem(f"e_hi{c}"), s + 1)
                    nc.gpsimd.tensor_tensor(eT[par][1][:, c, :], sg[c][:], eT[par][0][:, c, :].bitcast(F32),
                                            ALU.subtract).then_inc(sem(f"e_lo{c}"), 1)

            with pool.Fori(0, EP * GROUPS // 2) as pair:
                expert_lo(2 * pair, 0)
                expert_lo(2 * pair + 1, 1)

        @block.scalar
        def _(act):
            def split_hi(L):
                n = L["n"]
                act.wait_ge(sem(n + "_loaded"), LOADED[n])
                act.wait_ge(sem(n + "_wn"), KD)
                for k in range(KD):
                    nc.scalar.activation(wkvn[0][:, k, :], raw_kvn[:, k, :], ACT.Copy, scale=gcol[:, k:k + 1]).then_inc(sem(n + "_whi"), 1)
                for k in range(KD):
                    nc.scalar.activation(wq[0][:, k, :], raw_q[:, k, :], ACT.Copy, scale=gcol[:, k:k + 1]).then_inc(sem(n + "_whi"), 1)
                nc.scalar.activation(wout[0][:], raw_o[:], ACT.Copy).then_inc(sem(n + "_whi"), 1)

            def rel_silu(k):
                act.wait_ge(sem("rel_ln"), k + 1)
                nc.scalar.activation(r_h[:], r_h[:], ACT.Silu).then_inc(sem("rel_act"), 1)
                act.wait_ge(sem("rel_Tp"), k + 1)
                nc.scalar.activation(r_hT[:], psW[:, 0:D], ACT.Copy).then_inc(sem("rel_T"), 1)

            def attention(L):
                n = L["n"]
                done = L["done"]

                def step(i, par):
                    t = i - 1
                    if live(t):
                        act.wait_ge(sem("t_kTp"), done + t + 1)
                        reach(act, sem("t_sp"), done + t)
                        nc.scalar.activation(kT[:], psM[:, 0:P], ACT.Copy, scale=ksc[:, 0:1]).then_inc(sem("t_kT"), 1)
                    t = i - 3
                    if live(t):
                        act.wait_ge(sem("t_pTp"), done + t + 1)
                        reach(act, sem("t_pv"), done + t)
                        nc.scalar.activation(pT[:], psT[:].rearrange("p a (c q) -> p (a c) q", q=P), ACT.Copy).then_inc(sem("t_pT"), 1)
                    t = i
                    if live(t):
                        act.wait_ge(sem("t_kvp"), done + t + 1)
                        reach(act, sem("t_sn"), done + t)
                        nc.scalar.activation(kvs[:], psM[:, 0:KVN], ACT.Copy).then_inc(sem("t_kvs"), 1)
                        if L["cosine"]:
                            act.wait_ge(sem("t_kvs"), done + t + 1)
                            reach(act, sem("t_qmx"), done + t)
                            nc.scalar.activation(junk[:], kvs[:, 0:DH], ACT.Square, accum_out=qss[:, H:H + 1]).then_inc(sem("t_kss"), 1)
                    t = i - 2
                    if live(t):
                        act.wait_ge(sem("t_sub"), done + t + 1)
                        nc.scalar.activation(ex[:], ex[:], ACT.Exp).then_inc(sem("t_ex"), 1)
                    t = i
                    if live(t) and L["cosine"]:
                        act.wait_ge(sem("t_qp"), done + t + 1)
                        reach(act, sem("t_ssq"), done + t)
                        nc.scalar.activation(sq[:], psQ[:].rearrange("p a n -> p (a n)"), ACT.Square).then_inc(sem("t_sq"), 1)
                    t = i - 3
                    if live(t):
                        act.wait_ge(sem("t_pv"), done + t + 1)
                        reach(act, sem("t_wo"), done + t)
                        nc.scalar.activation(oT[0][:], psS[:].rearrange("p a (c q) -> p (a c) q", q=P), ACT.Identity,
                                             bias=nvcol[:, 0:1]).then_inc(sem("t_ohi"), 1)
                    t = i - 1
                    if live(t):
                        act.wait_ge(sem("t_qTp"), done + t + 1)
                        nc.scalar.activation(qT[:], psT[:].rearrange("p a (c q) -> p (a c) q", q=P), ACT.Copy).then_inc(sem("t_qT"), 1)
                    t = i + 1
                    if live(t):
                        act.wait_ge(sem("t_xTp"), done + t + 1)
                        nc.scalar.activation(xT[0][:], psM[:, 0:D].rearrange("p (k q) -> p k q", q=P), ACT.Copy).then_inc(sem("t_xhi"), 1)
                    t = i
                    if live(t) and not L["cosine"]:
                        act.wait_ge(sem("t_qp"), done + t + 1)
                        nc.scalar.activation(qn[:], psQ[:].rearrange("p a n -> p (a n)"), ACT.Copy).then_inc(sem("t_qn"), 1)
                    t = i - 3
                    if live(t):
                        act.wait_ge(sem("t_wo"), done + t + 1)
                        nc.scalar.activation(O[:, t, :], psW[:, 0:D], ACT.Copy).then_inc(sem("t_oev"), 1)

                pipeline(act, step, 2, 3)

            split_hi(LAYERS[0])
            for k in range(2):
                rel_silu(k)
            act.wait_ge(sem("rel_outp"), 1)
            nc.scalar.activation(r_out[:], psW[0:H, 0:P], ACT.Identity, bias=r_b2[:, 0:1]).then_inc(sem("rel_out"), 1)
            act.wait_ge(sem("a_causal"), 2)
            nc.scalar.activation(bias_t[0:S, :, :], braw0[0:S, :, :], ACT.Copy).then_inc(sem("a_bias"), 1)
            nc.scalar.activation(bias_t[S:P, :, :], braw0[S:P, :, :], ACT.Copy).then_inc(sem("a_bhi"), 1)
            attention(LAYERS[0])
            act.wait_ge(sem("f_loaded"), 48)
            for k in range(KD):
                nc.scalar.activation(wfc[0][:, k, :], raw_q[:, k, :], ACT.Copy, scale=gout0[:, k:k + 1]).then_inc(sem("f_whi"), 1)
            nc.scalar.activation(wpr[0][:], raw_o[:], ACT.Copy).then_inc(sem("f_whi"), 1)

            def ffn_in_hi(g):
                act.wait_ge(sem("f_cTp"), g + 1)
                nc.scalar.activation(cT[0][:], psT[:], ACT.Copy).then_inc(sem("f_chi"), 1)

            def ffn_relu(s, f):
                act.wait_ge(sem("f_up"), s + 1)
                reach(act, sem("f_lo"), s - 1)
                nc.scalar.activation(hf[f % 2][:], up_bank[f % 4], ACT.Relu).then_inc(sem("f_relu"), 1)

            def ffn_hi(s, par):
                act.wait_ge(sem("f_relu"), s + 1)
                nc.scalar.activation(hf[par][:], hf[par][:], ACT.Square).then_inc(sem("f_h"), 1)
                act.wait_ge(sem("f_h"), s + 1)
                reach(act, sem("f_dn"), s - 1)
                nc.scalar.activation(hT[par][0][:], hf[par][:], ACT.Copy).then_inc(sem("f_hi"), 1)

            def ffn_out(g):
                act.wait_ge(sem("f_dn"), FC * g + FC)
                reach(act, sem("f_lif"), 13 * g)
                nc.scalar.activation(cur[:].rearrange("p (a n) -> p a n", a=2), psS[:], ACT.Copy).then_inc(sem("f_y"), 1)

            def ffn(g, first=False, last=False):
                for f in range(FC):
                    if f == FC - 1 and not last:
                        act.wait_ge(sem("f_up"), FC * g + FC)
                        ffn_in_hi(g + 1)
                    ffn_relu(FC * g + f, f)
                    ffn_hi(FC * g + f, f % 2)
                    if f == 0 and not first:
                        ffn_out(g - 1)

            ffn_in_hi(0)
            ffn(0, first=True)
            ffn(1)
            with act.Fori(2, GROUPS - 1) as g:
                ffn(g)
            ffn(GROUPS - 1, last=True)
            ffn_out(GROUPS - 1)
            split_hi(LAYERS[1])
            act.wait_ge(sem("c_causal"), 2)
            nc.scalar.activation(bias_t[0:S, :, :], braw0[0:S, :, :], ACT.Copy).then_inc(sem("c_bias"), 1)
            nc.scalar.activation(bias_t[S:P, :, :], braw0[S:P, :, :], ACT.Copy).then_inc(sem("c_bhi"), 1)
            attention(LAYERS[1])
            act.wait_ge(sem("d_loaded"), 16 * 7)
            for k in range(KD):
                nc.scalar.activation(bqkv[0][:, k, :], raw_bqkv[:, k, :], ACT.Copy, scale=g1col[:, k:k + 1]).then_inc(sem("d_whi"), 1)
            nc.scalar.activation(bwo[0][:], raw_bwo[:], ACT.Copy).then_inc(sem("d_whi"), 1)
            act.wait_ge(sem("t_oev"), 2 * TILES)

            def block_step(i, par):
                t = i + 2
                if live(t):
                    act.wait_ge(sem("d_X"), t + 1)
                    reach(act, sem("d_ms1"), t - 1)
                    reach(act, sem("d_ss1"), t)
                    nc.scalar.activation(sqj[0][:], O[:, t, :], ACT.Square, scale=float(D) ** -0.5, accum_out=ss1[par][:]).then_inc(sem("d_ss1"), 1)
                t = i - 5
                if live(t):
                    act.wait_ge(sem("t_pv"), BLK + t + 1)
                    reach(act, sem("t_wo"), BLK + t)
                    nc.scalar.activation(boT[0][:], psM[:, 0:D].rearrange("p (k q) -> p k q", q=P), ACT.Copy).then_inc(sem("t_ohi"), 1)
                t = i - 6
                if live(t):
                    act.wait_ge(sem("d_X1"), t + 1)
                    reach(act, sem("d_ms2"), t - 1)
                    reach(act, sem("d_ss2"), t)
                    nc.scalar.activation(sqj[1][:], O[:, t, :], ACT.Square, scale=float(D) ** -0.5, accum_out=ss2[par][:]).then_inc(sem("d_ss2"), 1)
                t = i - 4
                if live(t):
                    act.wait_ge(sem("t_pTp"), BLK + t + 1)
                    reach(act, sem("t_pv"), BLK + t)
                    nc.scalar.activation(bpT[:], psT[:, 1, 0:D].rearrange("p (k q) -> p k q", q=P), ACT.Copy).then_inc(sem("t_pT"), 1)
                t = i - 9
                if live(t):
                    act.wait_ge(sem("d_xfTp"), t + 1)
                    reach(act, sem("d_lgp"), t)
                    reach(act, sem("d_xflo"), t)
                    nc.scalar.activation(xff[:], psQ[:, 0, D:2 * D].rearrange("p (k q) -> p k q", q=P), ACT.Copy).then_inc(sem("d_xff"), 1)
                t = i - 9
                if live(t):
                    act.wait_ge(sem("d_xff"), t + 1)
                    nc.scalar.activation(xfT[0][:, :, bass.ts(t, P)], xff[:], ACT.Copy).then_inc(sem("d_xfhi"), 1)
                t = i - 3
                if live(t):
                    act.wait_ge(sem("t_sub"), BLK + t + 1)
                    nc.scalar.activation(be[:], be[:], ACT.Exp).then_inc(sem("t_ex"), 1)
                t = i - 2
                if live(t):
                    act.wait_ge(sem("t_qTp"), BLK + t + 1)
                    reach(act, sem("t_sp"), BLK + t)
                    nc.scalar.activation(bqT[:], psT[:, 0, 0:D].rearrange("p (k q) -> p k q", q=P), ACT.Copy).then_inc(sem("t_qT"), 1)
                    nc.scalar.activation(bkT[:], psT[:, 0, D:D + P], ACT.Copy, scale=float(DH) ** -0.5).then_inc(sem("t_kT"), 1)
                t = i - 1
                if live(t):
                    act.wait_ge(sem("t_qp"), BLK + t + 1)
                    reach(act, sem("t_qTp"), BLK + t)
                    nc.scalar.activation(bq[:], psQ[:, 1, 0:D], ACT.Copy).then_inc(sem("t_qn"), 1)
                    nc.scalar.activation(bk[:], psQ[:, 1, D:D + DH].unsqueeze(1).to_broadcast([P, 2, DH]), ACT.Copy).then_inc(sem("t_kn"), 1)
                    nc.scalar.activation(v_all[:, t, :], psQ[:, 1, D + DH:QKV], ACT.Copy).then_inc(sem("t_vp"), 1)
                t = i
                if live(t):
                    act.wait_ge(sem("t_xTp"), BLK + t + 1)
                    reach(act, sem("t_qp"), BLK + t)
                    nc.scalar.activation(nxT[0][:], psQ[:, 0, 0:D].rearrange("p (k q) -> p k q", q=P), ACT.Copy).then_inc(sem("t_xhi"), 1)

            pipeline(act, block_step, 4, 10)
            def expert_weights(p, par):
                act.wait_ge(sem(f"e_loaded{par}"), 24 * (p - par) + 48)
                reach(act, sem("e_dn"), GROUPS * (p - 1))
                for j in range(2):
                    for k in range(KD):
                        nc.scalar.activation(ew[par][0][:, j, k, :], raw_e[par][:, j, k, :], ACT.Copy,
                                             scale=g2col[:, k:k + 1]).then_inc(sem("e_whi"), 1)
                nc.scalar.activation(ew[par][0][:, 2, :, :], raw_e[par][:, 2, :, :], ACT.Copy).then_inc(sem("e_whi"), 1)

            def expert(s, par):
                for c in range(KD):
                    act.wait_ge(sem(f"e_up{c}"), s + 1)
                    reach(act, sem(f"e_lo{c}"), s)
                    nc.scalar.activation(sg[c][:], psQ[:, c, :], ACT.Silu).then_inc(sem(f"e_sg{c}"), 1)
                for c in range(KD):
                    act.wait_ge(sem(f"e_h{c}"), s + 1)
                    reach(act, sem("e_dn"), s - 1)
                    nc.scalar.activation(eT[par][0][:, c, :], sg[c][:], ACT.Copy).then_inc(sem(f"e_hi{c}"), 1)

            def all_groups(p, next_weights):
                expert(GROUPS * p, 0)
                expert(GROUPS * p + 1, 1)
                next_weights()
                with act.Fori(1, GROUPS // 2) as pair:
                    expert(GROUPS * p + 2 * pair, 0)
                    expert(GROUPS * p + 2 * pair + 1, 1)

            act.wait_ge(sem("d_xflo"), TILES)
            act.wait_ge(sem("d_R"), TILES)
            expert_weights(0, 0)
            act.wait_ge(sem("r_shift"), 1)
            nc.scalar.activation(rt[0][:], rt[0][:], ACT.Exp).then_inc(sem("r_exp"), 1)
            act.wait_ge(sem("r_gap"), 1)
            nc.scalar.activation(rc[4][:], rc[4][:], ACT.Exp).then_inc(sem("r_exp"), 1)
            all_groups(0, lambda: expert_weights(1, 1))
            with act.Fori(0, (E - 1) // 2) as pair:
                all_groups(2 * pair + 1, lambda: expert_weights(2 * pair + 2, 0))
                all_groups(2 * pair + 2, lambda: expert_weights(2 * pair + 3, 1))
            all_groups(E - 1, lambda: expert_weights(E, 0))
            all_groups(E, lambda: None)

        @block.vector
        def _(dve):
            def null_key(L):
                n = L["n"]
                dve.wait_ge(sem(n + "_loaded"), LOADED[n])
                nk = sem(n + "_nk")
                if L["cosine"]:
                    nc.vector.tensor_tensor(junk[:], nkb[:], nkb[:], ALU.mult).then_inc(nk, 1)
                    nc.vector.tensor_tensor(qsrow[:], qsrow[:], ksrow[:], ALU.mult).then_inc(nk, 1)
                    nc.vector.tensor_tensor(ksc[:], ksc[:], qsc[:], ALU.mult).then_inc(nk, 1)
                    dve.wait_ge(nk, 3)
                    nc.vector.tensor_reduce(tiny[:, 0:1], junk[:], AX.X, ALU.add).then_inc(nk, 1)
                    nc.vector.tensor_scalar(ksc[:], ksc[:], float(DH) ** 0.5, None, ALU.mult).then_inc(sem(n + "_ksc"), 1)
                    dve.wait_ge(nk, 4)
                    nc.vector.tensor_scalar(tiny[:, 1:2], tiny[:, 0:1], 1e-24, None, ALU.max).then_inc(sem("nk_ss"), 1)
                    dve.wait_ge(sem("nk_r"), 1)
                    nc.vector.tensor_scalar(nkb[:], nkb[:], tiny[:, 2:3], float(DH) ** 0.5, ALU.mult, ALU.mult).then_inc(nk, 1)
                    dve.wait_ge(nk, 5)
                    nc.vector.tensor_tensor(nkb[:], nkb[:], qsrow[:], ALU.mult).then_inc(nk, 1)
                    dve.wait_ge(nk, 6)
                else:
                    nc.vector.tensor_scalar(nkb[:], nkb[:], float(DH) ** -0.5, None, ALU.mult).then_inc(nk, 1)
                    nc.vector.memset(ksc[:], float(DH) ** -0.5).then_inc(sem(n + "_ksc"), 1)
                    dve.wait_ge(nk, 1)
                for k in range(KD):
                    prod = wn_tmp[:]
                    if k:
                        dve.wait_ge(sem(n + "_wn"), k)
                    nc.vector.tensor_tensor(prod, raw_q[:, k, :].rearrange("p (h d) -> p h d", h=H),
                                            nkb[:].unsqueeze(1).to_broadcast([P, H, DH]), ALU.mult).then_inc(sem(n + "_wnp"), 1)
                    dve.wait_ge(sem(n + "_wnp"), k + 1)
                    nc.vector.tensor_reduce(raw_kvn[:, k, 2 * DH:KVN], prod, AX.X, ALU.add).then_inc(sem(n + "_wn"), 1)

            def split_lo(L):
                n = L["n"]
                lo = sem(n + "_wlo")
                for k in range(KD):
                    dve.wait_ge(sem(n + "_whi"), k + 1)
                    nc.vector.scalar_tensor_tensor(wkvn[1][:, k, :], raw_kvn[:, k, :], gcol[:, k:k + 1],
                                                   wkvn[0][:, k, :].bitcast(F32), ALU.mult, ALU.subtract).then_inc(lo, 1)
                for k in range(KD):
                    dve.wait_ge(sem(n + "_whi"), KD + k + 1)
                    nc.vector.scalar_tensor_tensor(wq[1][:, k, :], raw_q[:, k, :], gcol[:, k:k + 1],
                                                   wq[0][:, k, :].bitcast(F32), ALU.mult, ALU.subtract).then_inc(lo, 1)
                dve.wait_ge(sem(n + "_whi"), 2 * KD + 1)
                nc.vector.tensor_tensor(wout[1][:], raw_o[:], wout[0][:].bitcast(F32), ALU.subtract).then_inc(lo, 1)
                nc.vector.tensor_scalar(negmask[:], mask_w[:].bitcast(U8), -1.0, -NEG, ALU.add, ALU.mult).then_inc(sem(n + "_mask"), 1)

            def rel_norm(k, src):
                c = sem("rel_chain")
                nc.vector.bn_stats(r_st[:], src).then_inc(c, 1)
                dve.wait_ge(c, 4 * k + 2)
                nc.vector.bn_aggr(r_mv[:], r_st[:]).then_inc(sem("rel_mv"), 1)
                dve.wait_ge(sem("rel_rstd"), k + 1)
                nc.vector.tensor_scalar(r_h[:], src, r_mv[:, 0:1], r_rs[:, 1:2], ALU.subtract, ALU.mult).then_inc(c, 1)
                dve.wait_ge(c, 4 * k + 3)
                nc.vector.tensor_tensor(r_h[:], r_h[:], r_rows[f"g{k}"][:], ALU.mult).then_inc(sem("rel_ln"), 1)

            def attention(L, start):
                n = L["n"]
                done = L["done"]

                def step(i, par):
                    t = i - 2
                    if live(t):
                        dve.wait_ge(sem("t_sp"), done + t + 1)
                        scores = psS[:].rearrange("p a (c j) -> p c a j", j=S)
                        by_head = lambda v: v.rearrange("p (c a) -> p c a", a=2)
                        nc.vector.tensor_reduce(by_head(m16[:]), scores, AX.X, ALU.max).then_inc(sem("t_m0"), 1)
                        dve.wait_ge(sem("t_m0"), done + t + 1)
                        nc.vector.tensor_tensor(mm16[:], m16[:], sn[par][:], ALU.max).then_inc(sem("t_m1"), 1)
                        dve.wait_ge(sem("t_m1"), done + t + 1)
                        reach(dve, sem("t_pn"), done + t)
                        nc.vector.tensor_tensor(ex[:, :, 0:S].rearrange("p (c a) j -> p c a j", a=2), scores,
                                                by_head(mm16[:]).unsqueeze(3).to_broadcast([P, CH, 2, S]),
                                                ALU.subtract).then_inc(sem("t_sub0"), 1)
                        nc.vector.tensor_tensor(ex[:, :, S], sn[par][:], mm16[:], ALU.subtract).then_inc(sem("t_sub"), 1)
                    t = i
                    if live(t):
                        dve.wait_ge(sem("t_kvs"), done + t + 1)
                        reach(dve, sem(f"t_vv{par}"), 32 * done + spread(t - 2, par))
                        nc.vector.tensor_tensor(vp[par][:], kvs[:, DH:2 * DH], nvb[:], ALU.subtract).then_inc(sem("t_vp"), 1)
                    t = i + 1
                    if live(t):
                        dve.wait_ge(sem("t_rstd"), done + t + 1)
                        reach(dve, sem("t_xTp"), done + t)
                        q = (par + 1) % 2
                        nc.vector.tensor_scalar(xn[:], X[:, t, :], mv[q][:, 0:1], rstd[q][:, 0:1], ALU.subtract,
                                                ALU.mult).then_inc(sem("t_xn"), 1)
                    t = i + 2
                    if live(t):
                        start(t)
                        reach(dve, sem("t_mv"), done + t)
                        nc.vector.bn_stats(st6[:], X[:, t, :]).then_inc(sem("t_st"), 1)
                    t = i - 2
                    if live(t):
                        dve.wait_ge(sem("t_ex"), done + t + 1)
                        nc.vector.tensor_reduce(den[:], ex[:], AX.X, ALU.add).then_inc(sem("t_den"), 1)
                        dve.wait_ge(sem("t_den"), done + t + 1)
                        nc.vector.reciprocal(rden[:], den[:]).then_inc(sem("t_rden"), 1)
                    t = i
                    if live(t) and L["cosine"]:
                        dve.wait_ge(sem("t_sq"), done + t + 1)
                        nc.vector.tensor_reduce(qss[:, 0:H], sq[:].rearrange("p (h d) -> p h d", h=H), AX.X,
                                                ALU.add).then_inc(sem("t_ssq"), 1)
                        dve.wait_ge(sem("t_ssq"), done + t + 1)
                        dve.wait_ge(sem("t_kss"), done + t + 1)
                        reach(dve, sem("t_rq"), done + t)
                        nc.vector.tensor_scalar(qmx[:], qss[:], 1e-24, None, ALU.max).then_inc(sem("t_qmx"), 1)
                    t = i + 2
                    if live(t):
                        apart(dve, (sem("t_st"), done + t + 1))
                        nc.vector.bn_aggr(mv[par][:], st6[:]).then_inc(sem("t_mv"), 1)
                    t = i - 3
                    if live(t):
                        dve.wait_ge(sem("t_ohi"), done + t + 1)
                        nc.vector.scalar_tensor_tensor(oT[1][:], psS[:].rearrange("p a (c q) -> p (a c) q", q=P), nvcol[:, 0:1],
                                                       oT[0][:].bitcast(F32), ALU.add, ALU.subtract).then_inc(sem("t_olo"), 1)
                    t = i + 1
                    if live(t):
                        dve.wait_ge(sem("t_xhi"), done + t + 1)
                        nc.vector.tensor_tensor(xT[1][:], psM[:, 0:D].rearrange("p (k q) -> p k q", q=P),
                                                xT[0][:].bitcast(F32), ALU.subtract).then_inc(sem("t_xlo"), 1)
                    t = i
                    if live(t):
                        reach(dve, sem("t_kTp"), done + t)
                        if L["cosine"]:
                            dve.wait_ge(sem("t_rq"), done + t + 1)
                            nc.vector.tensor_scalar(kn[:], kvs[:, 0:DH].unsqueeze(1).to_broadcast([P, 2, DH]), rq[:, H:H + 1],
                                                    None, ALU.mult).then_inc(sem("t_kn"), 1)
                            nc.vector.tensor_tensor(snr[:], kvs[:, 2 * DH:KVN], rq[:, 0:H], ALU.mult).then_inc(sem("t_snr"), 1)
                            reach(dve, sem("t_qTp"), done + t)
                            nc.vector.tensor_tensor(qn[:].rearrange("p (h d) -> p h d", h=H),
                                                    psQ[:].rearrange("p a (h d) -> p (a h) d", d=DH),
                                                    rq[:, 0:H].unsqueeze(2).to_broadcast([P, H, DH]), ALU.mult).then_inc(sem("t_qn"), 1)
                            dve.wait_ge(sem("t_snr"), done + t + 1)
                            reach(dve, sem("t_sub"), done + t - 1)
                            nc.vector.tensor_tensor(sn[par][:], snr[:], nbias[:], ALU.add).then_inc(sem("t_sn"), 1)
                        else:
                            nc.vector.tensor_copy(kn[:], kvs[:, 0:DH].unsqueeze(1).to_broadcast([P, 2, DH])).then_inc(sem("t_kn"), 1)
                            reach(dve, sem("t_sub"), done + t - 1)
                            nc.vector.tensor_tensor(sn[par][:], kvs[:, 2 * DH:KVN], nbias[:], ALU.add).then_inc(sem("t_sn"), 1)

                pipeline(dve, step, 2, 3)

            dve.wait_ge(sem("const_pool"), CONSTANTS)
            nc.vector.tensor_copy(sel[:], sel_f[:]).then_inc(sem("const_dve"), 1)
            nc.vector.tensor_copy(ind[:], ind_f[:]).then_inc(sem("const_dve"), 1)
            null_key(LAYERS[0])
            dve.wait_ge(sem("rel_loaded"), 16 * 8)
            nc.vector.scalar_tensor_tensor(r_h[:], r_rows["w0"][:], r_pos[:, 0:1], r_rows["b0"][:], ALU.mult,
                                           ALU.add).then_inc(sem("rel_chain"), 1)
            dve.wait_ge(sem("rel_chain"), 1)
            rel_norm(0, r_h[:])
            split_lo(LAYERS[0])
            dve.wait_ge(sem("rel_mm"), 1)
            nc.vector.tensor_tensor(r_h[:], psS[:, 0, 0:D], r_rows["b1"][:], ALU.add).then_inc(sem("rel_chain"), 2)
            dve.wait_ge(sem("rel_chain"), 5)
            rel_norm(1, r_h[:])
            dve.wait_ge(sem("a_bhi"), 1)
            nc.vector.tensor_tensor(bias_t[S:P, :, :], braw0[S:P, :, :], bias_t[S:P, :, :].bitcast(F32),
                                    ALU.subtract).then_inc(sem("a_bias"), 1)

            def x_there(t):
                if isinstance(t, int) and t < 4:
                    dve.wait_ge(sem("x_in0"), 16)
                else:
                    dve.wait_ge(sem("x_in1"), 16)
                    dve.wait_ge(sem("x_in2"), 16)

            attention(LAYERS[0], x_there)
            for k in range(KD):
                dve.wait_ge(sem("f_whi"), k + 1)
                nc.vector.scalar_tensor_tensor(wfc[1][:, k, :], raw_q[:, k, :], gout0[:, k:k + 1], wfc[0][:, k, :].bitcast(F32),
                                               ALU.mult, ALU.subtract).then_inc(sem("f_wlo"), 1)
            dve.wait_ge(sem("f_whi"), KD + 1)
            nc.vector.tensor_tensor(wpr[1][:], raw_o[:], wpr[0][:].bitcast(F32), ALU.subtract).then_inc(sem("f_wlo"), 1)

            def ffn_stats(g):
                for j in range(G4):
                    reach(dve, sem("f_mv"), G4 * g)
                    nc.vector.bn_stats(fst6[:, j, :], O[:, G4 * g + j, :]).then_inc(sem("f_st"), 1)
                for j in range(G4):
                    apart(dve, (sem("f_st"), G4 * g + j + 1),
                               (sem("f_c0"), g))
                    nc.vector.bn_aggr(fmv[:, j, :], fst6[:, j, :]).then_inc(sem("f_mv"), 1)

            def ffn_normalise(g):
                dve.wait_ge(sem("f_rs"), g + 1)
                reach(dve, sem("f_cTp"), g)
                for j in range(G4):
                    ins = nc.vector.tensor_scalar(c0[:, j, :], O[:, G4 * g + j, :], fmv[:, j, 0:1], frs[:, j:j + 1],
                                                  ALU.subtract, ALU.mult)
                ins.then_inc(sem("f_c0"), 1)

            def ffn_in_lo(g):
                dve.wait_ge(sem("f_chi"), g + 1)
                nc.vector.tensor_tensor(cT[1][:], psT[:], cT[0][:].bitcast(F32), ALU.subtract).then_inc(sem("f_clo"), 1)

            def add_to_x(g):
                dve.wait_ge(sem("f_count"), 4 * g + 4)
                rows = X[:, bass.ts(g, G4), :]
                nc.vector.scalar_tensor_tensor(rows, count[:].rearrange("p (t d) -> p t d", d=D), 1.0 / LIF_STEPS, rows,
                                               ALU.mult, ALU.add).then_inc(sem("f_x1"), 1)

            def fire(g, n):
                done = sem("f_lif")
                reach(dve, done, 13 * g + n)
                if n == 0:
                    dve.wait_ge(sem("f_y"), g + 1)
                    reach(dve, sem("f_count"), 4 * g)
                kind, k = (2, 0) if n == 0 else ((n - 1) % 3, (n - 1) // 3 + 1)
                if kind == 2 and k >= 2:
                    dve.wait_ge(sem("f_count"), 4 * g + k - 1)
                if kind == 0:
                    src = cur if k == 1 else mem
                    ins = nc.vector.scalar_tensor_tensor(mem[:], src[:], LIF_BETA, cur[:], ALU.mult, ALU.add)
                elif kind == 1:
                    ins = nc.vector.tensor_tensor(mem[:], mem[:], spk[(k + 1) % 2][:], ALU.subtract)
                else:
                    src = cur if n == 0 else mem
                    ins = nc.vector.tensor_scalar(spk[k % 2][:], src[:], LIF_THRESHOLD, None, ALU.is_gt)
                ins.then_inc(done, 1)

            def ffn(g, first=False, last=False):
                if not last:
                    ffn_stats(g + 1)
                for f in range(FC):
                    if not first:
                        for n in (2 * f, 2 * f + 1):
                            if n < 13:
                                fire(g - 1, n)
                    if not last and f == 2:
                        ffn_normalise(g + 1)
                if not last:
                    ffn_in_lo(g + 1)
                if not first:
                    add_to_x(g - 1)

            dve.wait_ge(sem("t_oev"), TILES)
            ffn_stats(0)
            ffn_normalise(0)
            ffn_in_lo(0)
            ffn(0, first=True)
            ffn(1)
            with dve.Fori(2, GROUPS - 1) as g:
                ffn(g)
            ffn(GROUPS - 1, last=True)
            for n in range(13):
                fire(GROUPS - 1, n)
            add_to_x(GROUPS - 1)
            dve.wait_ge(sem("f_x1"), GROUPS)
            null_key(LAYERS[1])
            split_lo(LAYERS[1])
            dve.wait_ge(sem("c_bhi"), 1)
            nc.vector.tensor_tensor(bias_t[S:P, :, :], braw0[S:P, :, :], bias_t[S:P, :, :].bitcast(F32),
                                    ALU.subtract).then_inc(sem("c_bias"), 1)
            attention(LAYERS[1], lambda t: None)
            for k in range(KD):
                dve.wait_ge(sem("d_whi"), k + 1)
                nc.vector.scalar_tensor_tensor(bqkv[1][:, k, :], raw_bqkv[:, k, :], g1col[:, k:k + 1], bqkv[0][:, k, :].bitcast(F32),
                                               ALU.mult, ALU.subtract).then_inc(sem("d_wlo0"), 1)
            for k in range(KD):
                nc.vector.tensor_scalar(bwr[:, k, :], bwr[:, k, :], g2col[:, k:k + 1], None, ALU.mult).then_inc(sem("d_wr"), 1)
            dve.wait_ge(sem("d_whi"), KD + 1)
            nc.vector.tensor_tensor(bwo[1][:], raw_bwo[:], bwo[0][:].bitcast(F32), ALU.subtract).then_inc(sem("d_wlo"), 2)
            dve.wait_ge(sem("t_oev"), 2 * TILES)

            def block_step(i, par):
                other = (par + 1) % 2
                t = i - 1
                if live(t):
                    dve.wait_ge(sem("t_xhi"), BLK + t + 1)
                    nc.vector.tensor_tensor(nxT[1][:], psQ[:, 0, 0:D].rearrange("p (k q) -> p k q", q=P),
                                            nxT[0][:].bitcast(F32), ALU.subtract).then_inc(sem("t_xlo"), 1)
                t = i
                if live(t):
                    dve.wait_ge(sem("d_r1"), t + 1)
                    reach(dve, sem("t_xTp"), BLK + t)
                    nc.vector.tensor_scalar(nx[:], O[:, t, :], r1[par][:, 0:1], None, ALU.mult).then_inc(sem("d_nx"), 1)
                t = i + 4
                if live(t):
                    reach(dve, sem("t_mv"), BLK + t)
                    nc.vector.bn_stats(dst6[:], O[:, t, :]).then_inc(sem("t_st"), 1)
                t = i - 6
                if live(t):
                    dve.wait_ge(sem("t_wo"), BLK + t + 1)
                    nc.vector.tensor_tensor(O[:, t, :], psW[:, 0:D], O[:, t, :], ALU.add).then_inc(sem("d_X1"), 1)
                t = i + 4
                if live(t):
                    apart(dve, (sem("t_st"), BLK + t + 1))
                    nc.vector.bn_aggr(dmv[par][:], dst6[:]).then_inc(sem("t_mv"), 1)
                t = i - 5
                if live(t):
                    dve.wait_ge(sem("t_ohi"), BLK + t + 1)
                    nc.vector.tensor_tensor(boT[1][:], psM[:, 0:D].rearrange("p (k q) -> p k q", q=P),
                                            boT[0][:].bitcast(F32), ALU.subtract).then_inc(sem("t_olo"), 1)
                t = i - 3
                if live(t):
                    dve.wait_ge(sem("t_sp"), BLK + t + 1)
                    scores = psS[:, :, 0:CB * S].rearrange("p a (c j) -> p c a j", j=S)
                    nc.vector.tensor_reduce(bm[:].rearrange("p (c a) -> p c a", a=2), scores, AX.X, ALU.max).then_inc(sem("t_m0"), 1)
                    dve.wait_ge(sem("t_m0"), BLK + t + 1)
                    reach(dve, sem("t_pn"), BLK + t)
                    nc.vector.tensor_tensor(be[:].rearrange("p (c a) j -> p c a j", a=2), scores,
                                            bm[:].rearrange("p (c a) -> p c a", a=2).unsqueeze(3).to_broadcast([P, CB, 2, S]),
                                            ALU.subtract).then_inc(sem("t_sub"), 1)
                t = i + 3
                if live(t):
                    dve.wait_ge(sem("t_rstd"), BLK + t + 1)
                    nc.vector.tensor_scalar(O[:, t, :], O[:, t, :], dmv[other][:, 0:1], drs[other][:, 0:1], ALU.subtract,
                                            ALU.mult).then_inc(sem("d_X0"), 1)
                t = i - 8
                if live(t):
                    dve.wait_ge(sem("d_r2"), t + 1)
                    reach(dve, sem("d_xfTp"), t)
                    nc.vector.tensor_scalar(xf[:], O[:, t, :], r2[par][:, 0:1], None, ALU.mult).then_inc(sem("d_xf"), 1)
                t = i - 10
                if live(t):
                    dve.wait_ge(sem("d_lgp"), t + 1)
                    nc.vector.tensor_tensor(logits[:, t, :], psW[:, D:D + E], ebias[:], ALU.add).then_inc(sem("d_lg"), 1)
                t = i - 9
                if live(t):
                    dve.wait_ge(sem("d_xfhi"), t + 1)
                    nc.vector.tensor_tensor(xfT[1][:, :, bass.ts(t, P)], xff[:], xfT[0][:, :, bass.ts(t, P)].bitcast(F32),
                                            ALU.subtract).then_inc(sem("d_xflo"), 1)
                t = i - 3
                if live(t):
                    dve.wait_ge(sem("t_ex"), BLK + t + 1)
                    nc.vector.tensor_reduce(bden[:], be[:], AX.X, ALU.add).then_inc(sem("t_den"), 1)
                    dve.wait_ge(sem("t_den"), BLK + t + 1)
                    nc.vector.reciprocal(brd[:], bden[:]).then_inc(sem("t_rden"), 1)

            pipeline(dve, block_step, 4, 10)
            def expert_weights(p, par):
                for j in range(2):
                    for k in range(KD):
                        dve.wait_ge(sem("e_whi"), 5 * p + 2 * j + k + 1)
                        nc.vector.scalar_tensor_tensor(ew[par][1][:, j, k, :], raw_e[par][:, j, k, :], g2col[:, k:k + 1],
                                                       ew[par][0][:, j, k, :].bitcast(F32), ALU.mult, ALU.subtract)
                dve.wait_ge(sem("e_whi"), 5 * p + 5)
                nc.vector.tensor_tensor(ew[par][1][:, 2, :, :], raw_e[par][:, 2, :, :], ew[par][0][:, 2, :, :].bitcast(F32),
                                        ALU.subtract).then_inc(sem("e_wlo"), 1)

            def route():
                c = sem("r_chain")
                done = 0

                def then(ins):
                    nonlocal done
                    done += 1
                    ins.then_inc(c, 1)
                    dve.wait_ge(c, done)

                wide = lambda v: v.unsqueeze(2).to_broadcast([P, TILES, E])
                index = iota8[:].unsqueeze(1).to_broadcast([P, TILES, E])
                dve.wait_ge(sem("d_lg"), TILES)
                dve.wait_ge(sem("d_R"), TILES)
                dve.wait_ge(sem("d_iota"), 1)
                nc.vector.memset(comb[:, :, 0], 1.0).then_inc(sem("r_shared"), 1)
                then(nc.vector.tensor_reduce(rc[0][:], logits[:], AX.X, ALU.max))
                nc.vector.tensor_tensor(rt[0][:], logits[:], wide(rc[0][:]), ALU.subtract).then_inc(sem("r_shift"), 1)
                dve.wait_ge(sem("r_exp"), 1)
                then(nc.vector.tensor_reduce(rc[0][:], rt[0][:], AX.X, ALU.add))
                then(nc.vector.reciprocal(rc[1][:], rc[0][:]))
                then(nc.vector.tensor_tensor(rt[0][:], rt[0][:], wide(rc[1][:]), ALU.mult))
                for n in range(2):
                    then(nc.vector.tensor_reduce(rc[2 + n][:], rt[0][:], AX.X, ALU.max))
                    then(nc.vector.tensor_tensor(rt[3][:], rt[0][:], wide(rc[2 + n][:]), ALU.is_lt))
                    then(nc.vector.scalar_tensor_tensor(rt[3][:], rt[3][:], float(E), index, ALU.mult, ALU.add))
                    then(nc.vector.tensor_reduce(rc[0][:], rt[3][:], AX.X, ALU.min))
                    then(nc.vector.tensor_tensor(rt[1 + n][:], index, wide(rc[0][:]), ALU.is_equal))
                    if n == 0:
                        then(nc.vector.scalar_tensor_tensor(rt[0][:], rt[1][:], -2.0, rt[0][:], ALU.mult, ALU.add))
                nc.vector.tensor_tensor(rc[4][:], rc[3][:], rc[2][:], ALU.subtract).then_inc(sem("r_gap"), 1)
                dve.wait_ge(sem("r_exp"), 2)
                then(nc.vector.tensor_scalar(rc[0][:], rc[4][:], 1.0, None, ALU.add))
                then(nc.vector.reciprocal(rc[1][:], rc[0][:]))
                then(nc.vector.tensor_tensor(rc[5][:], rc[4][:], rc[1][:], ALU.mult))
                then(nc.vector.tensor_tensor(rt[1][:], rt[1][:], wide(rc[1][:]), ALU.mult))
                then(nc.vector.tensor_tensor(rt[2][:], rt[2][:], wide(rc[5][:]), ALU.mult))
                then(nc.vector.tensor_tensor(comb[:, :, 1:EP], rt[1][:], rt[2][:], ALU.add))

            def expert_h(s):
                for c in range(KD):
                    dve.wait_ge(sem(f"e_sg{c}"), s + 1)
                    nc.vector.tensor_tensor(sg[c][:], sg[c][:], psS[:, c, :], ALU.mult).then_inc(sem(f"e_h{c}"), 1)

            def add_up(p, g):
                s = GROUPS * p + g
                dve.wait_ge(sem("e_dn"), s + 1)
                nc.vector.tensor_copy(cw[:], comb[:, bass.ts(g, G4), p]).then_inc(sem("e_cw"), 1)
                dve.wait_ge(sem("e_cw"), s + 1)
                for j in range(G4):
                    row = X[:, G4 * g + j, :]
                    ins = nc.vector.scalar_tensor_tensor(row, psT[:, j // 2, j % 2 * D:j % 2 * D + D], cw[:, j:j + 1], row,
                                                         ALU.mult, ALU.add)
                ins.then_inc(sem("e_acc"), 1)

            def all_groups(p, next_weights, first=False):
                expert_h(GROUPS * p)
                if not first:
                    add_up(p - 1, GROUPS - 1)
                expert_h(GROUPS * p + 1)
                add_up(p, 0)
                next_weights()
                with dve.Fori(1, GROUPS // 2) as pair:
                    expert_h(GROUPS * p + 2 * pair)
                    add_up(p, 2 * pair - 1)
                    expert_h(GROUPS * p + 2 * pair + 1)
                    add_up(p, 2 * pair)

            expert_weights(0, 0)
            route()
            all_groups(0, lambda: expert_weights(1, 1), first=True)
            with dve.Fori(0, (E - 1) // 2) as pair:
                all_groups(2 * pair + 1, lambda: expert_weights(2 * pair + 2, 0))
                all_groups(2 * pair + 2, lambda: expert_weights(2 * pair + 3, 1))
            all_groups(E - 1, lambda: expert_weights(E, 0))
            all_groups(E, lambda: None)
            add_up(E, GROUPS - 1)

        @block.tensor
        def _(pe):
            def attention(L):
                n = L["n"]
                done = L["done"]

                def step(i, par):
                    t = i - 1
                    if live(t):
                        pe.wait_ge(sem("t_kn"), done + t + 1)
                        if live(t + 1):
                            pe.wait_ge(sem("t_xlo"), done + t + 2)
                        nc.tensor.transpose(psM[:, 0:P], kn[:].rearrange("p a d -> p (a d)"), ident[:]).then_inc(sem("t_kTp"), 1)
                    t = i - 3
                    if live(t):
                        pe.wait_ge(sem("t_pn"), done + t + 1)
                        if live(t + 1):
                            pe.wait_ge(sem("t_qT"), done + t + 2)
                        for c in range(CH):
                            mm = nc.tensor.transpose(psT[:, c // 4, c % 4 * P:c % 4 * P + P],
                                                     pn[:, 2 * c:2 * c + 2, :].rearrange("p a j -> p (a j)"), ident[:])
                        mm.then_inc(sem("t_pTp"), 1)
                    t = i
                    if live(t):
                        pe.wait_ge(sem("t_xlo"), done + t + 1)
                        reach(pe, sem("t_kT"), done + t)
                        if isinstance(t, int) and t == 0:
                            pe.wait_ge(sem(n + "_wlo"), 2 * KD + 1)
                        for k in range(KD):
                            for j, (u, w) in enumerate(PASSES):
                                mm = nc.tensor.matmul(psM[:, 0:KVN], xT[u][:, k, :], wkvn[w][:, k, :],
                                                      start=(k == 0 and j == 0), stop=(k == KD - 1 and j == 2))
                        mm.then_inc(sem("t_kvp"), 1)
                        reach(pe, sem("t_qn"), done + t)
                        for half in range(2):
                            for k in range(KD):
                                for j, (u, w) in enumerate(PASSES):
                                    if live(i - 3) and half == 1 and k == KD - 1 and j == 2:
                                        pe.wait_ge(sem("t_pT"), done + i - 2)
                                        pe.wait_ge(sem("t_sub"), done + i - 1)
                                        pe.wait_ge(sem(f"t_vv{(par + 1) % 2}"), 32 * done + spread(i - 3, (par + 1) % 2))
                                    mm = nc.tensor.matmul(psQ[:, half, :], xT[u][:, k, :], wq[w][:, k, half * 512:half * 512 + 512],
                                                          start=(k == 0 and j == 0), stop=(k == KD - 1 and j == 2))
                        mm.then_inc(sem("t_qp"), 1)
                    t = i - 3
                    if live(t):
                        vpar = (par + 1) % 2
                        if not live(i):
                            pe.wait_ge(sem("t_pT"), done + t + 1)
                            pe.wait_ge(sem(f"t_vv{vpar}"), 32 * done + spread(t, vpar))
                            if live(t + 1):
                                pe.wait_ge(sem("t_sub"), done + t + 2)
                        for c4 in range(2):
                            out4 = psS[:, c4, :].rearrange("p (c b q) -> p c b q", b=2, q=S)
                            for b in range(2):
                                for half in range(2):
                                    f = slice(half * S, half * S + S)
                                    mm = nc.tensor.matmul(out4[f, :, b, :], vv[vpar][f, b, :],
                                                          pT[f, 4 * c4:4 * c4 + 4, b * S:b * S + S],
                                                          start=(b == 0), stop=(b == 1), skip_group_check=True)
                        mm.then_inc(sem("t_pv"), 1)
                    t = i - 1
                    if live(t):
                        pe.wait_ge(sem("t_qn"), done + t + 1)
                        reach(pe, sem("t_pT"), done + t - 1)
                        for c in range(CH):
                            mm = nc.tensor.transpose(psT[:, c // 4, c % 4 * P:c % 4 * P + P], qn[:, c * P:c * P + P], ident[:])
                        mm.then_inc(sem("t_qTp"), 1)
                    t = i + 1
                    if live(t):
                        pe.wait_ge(sem("t_xn"), done + t + 1)
                        reach(pe, sem("t_kvs"), done + t)
                        for k in range(KD):
                            mm = nc.tensor.transpose(psM[:, k * P:k * P + P], xn[:, k * P:k * P + P], ident[:])
                        mm.then_inc(sem("t_xTp"), 1)
                    t = i - 3
                    if live(t):
                        pe.wait_ge(sem("t_ohi"), done + t + 1)
                        reach(pe, sem("t_oev"), done + t)
                        for u in range(2):
                            if u:
                                pe.wait_ge(sem("t_olo"), done + t + 1)
                            for c in range(CH):
                                for w in range(2 - u):
                                    mm = nc.tensor.matmul(psW[:, 0:D], oT[u][:, c, :], wout[w][:, c, :],
                                                          start=(u == 0 and c == 0 and w == 0), stop=(u == 1 and c == CH - 1))
                        mm.then_inc(sem("t_wo"), 1)
                    t = i - 1
                    if live(t):
                        reach(pe, sem("t_olo"), done + t - 1)
                        reach(pe, sem("t_sub"), done + t)
                        if isinstance(t, int) and t == 0:
                            pe.wait_ge(sem(n + "_bias"), 2)
                            pe.wait_ge(sem(n + "_mask"), 1)
                        for half in range(2):
                            nc.tensor.matmul(psS[:, half, :], sel[:], bias_t[:].rearrange("p (c a) j -> p a c j", a=2)[:, half],
                                             start=True, stop=False, skip_group_check=True)
                        pe.wait_ge(sem("t_qT"), done + t + 1)
                        pe.wait_ge(sem("t_kT"), done + t + 1)
                        for half in range(2):
                            nc.tensor.matmul(psS[:, half, :], ind[:], negmask[:, t, :].unsqueeze(1).to_broadcast([2, CH, S]),
                                             start=False, stop=False, skip_group_check=True)
                        for c in range(CH):
                            for half in range(2):
                                for b in range(2):
                                    f = slice(half * DH, half * DH + DH)
                                    q = slice(b * S, b * S + S)
                                    mm = nc.tensor.matmul(psS[q, half, c * S:c * S + S], qT[f, c, q], kT[f, q],
                                                          start=False, stop=True, skip_group_check=True)
                        mm.then_inc(sem("t_sp"), 1)

                pipeline(pe, step, 2, 3)

            pe.wait_ge(sem("const_pool"), CONSTANTS)
            for k in range(2):
                pe.wait_ge(sem("rel_act"), k + 1)
                for c in range(KD):
                    mm = nc.tensor.transpose(psW[:, c * P:c * P + P], r_h[:, c * P:c * P + P], ident[:])
                mm.then_inc(sem("rel_Tp"), 1)
                pe.wait_ge(sem("rel_T"), k + 1)
                if k == 0:
                    for c in range(KD):
                        mm = nc.tensor.matmul(psS[:, 0, 0:D], r_hT[:, c, :], r_w1[:, c, :], start=(c == 0), stop=(c == KD - 1))
                    mm.then_inc(sem("rel_mm"), 1)
                else:
                    for c in range(KD):
                        mm = nc.tensor.matmul(psW[0:H, 0:P], r_w2[:, c, :], r_hT[:, c, :], start=(c == 0), stop=(c == KD - 1))
                    mm.then_inc(sem("rel_outp"), 1)
            pe.wait_ge(sem("const_dve"), 2)
            attention(LAYERS[0])
            def ffn_in(g):
                pe.wait_ge(sem("f_c0"), g + 1)
                reach(pe, sem("f_clo"), g)
                for k in range(KD):
                    for j in range(G4):
                        mm = nc.tensor.transpose(psT[:, k, j * P:j * P + P], c0[:, j, k * P:k * P + P], ident[:])
                mm.then_inc(sem("f_cTp"), 1)

            def ffn_up(g, f):
                s = FC * g + f
                if f % FC == 0:
                    pe.wait_ge(sem("f_clo"), g + f // FC + 1)
                reach(pe, sem("f_relu"), s - 3)
                for k in range(KD):
                    for j, (u, w) in enumerate(PASSES):
                        mm = nc.tensor.matmul(up_bank[f % 4], wfc[u][:, k, f % FC * P:f % FC * P + P], cT[w][:, k, :],
                                              start=(k == 0 and j == 0), stop=(k == KD - 1 and j == 2))
                mm.then_inc(sem("f_up"), 1)

            def ffn_down(g, f):
                s = FC * g + f
                pe.wait_ge(sem("f_lo"), s + 1)
                if f == 0:
                    reach(pe, sem("f_y"), g)
                for t in range(G4):
                    for j, (u, w) in enumerate(PASSES):
                        mm = nc.tensor.matmul(psS[:, t // 2, t % 2 * D:t % 2 * D + D], hT[f % 2][u][:, t * P:t * P + P], wpr[w][:, f, :],
                                              start=(f == 0 and j == 0 and t % 2 == 0), stop=(f == FC - 1 and j == 2),
                                              skip_group_check=True)
                mm.then_inc(sem("f_dn"), 1)

            def ffn(g, last=False):
                for f in range(FC - 2):
                    ffn_up(g, f + 2)
                    ffn_down(g, f)
                    if f == FC - 4 and not last:
                        ffn_in(g + 1)
                ffn_down(g, FC - 2)
                if not last:
                    ffn_up(g, FC)
                ffn_down(g, FC - 1)
                if not last:
                    ffn_up(g, FC + 1)

            pe.wait_ge(sem("f_wlo"), KD + 1)
            ffn_in(0)
            ffn_up(0, 0)
            ffn_up(0, 1)
            ffn(0)
            with pe.Fori(1, GROUPS - 1) as g:
                ffn(g)
            ffn(GROUPS - 1, last=True)
            attention(LAYERS[1])
            def block_step(i, par):
                t = i - 6
                if live(t):
                    pe.wait_ge(sem("t_olo"), BLK + t + 1)
                    reach(pe, sem("d_X1"), t)
                    if live(i - 11):
                        pe.wait_ge(sem("d_lg"), i - 10)
                    for c in range(CB):
                        for j, (u, w) in enumerate(PASSES):
                            mm = nc.tensor.matmul(psW[:, 0:D], boT[u][:, c, :], bwo[w][:, c, :],
                                                  start=(c == 0 and j == 0), stop=(c == CB - 1 and j == 2))
                    mm.then_inc(sem("t_wo"), 1)
                t = i - 5
                if live(t):
                    vpar = (par + 1) % 2
                    apart(pe, (sem("t_pT"), BLK + t + 1),
                              (sem(f"t_vv{vpar}"), 32 * BLK + spread(t, vpar)),
                              (sem("t_olo"), BLK + t))
                    o = psM[:, 0:D].rearrange("p (c b q) -> p c b q", b=2, q=S)
                    for b in range(2):
                        for half in range(2):
                            f = slice(half * S, half * S + S)
                            mm = nc.tensor.matmul(o[f, :, b, :], bvv[vpar][f, b, :], bpT[f, :, b * S:b * S + S],
                                                  start=True, stop=True, skip_group_check=True)
                    mm.then_inc(sem("t_pv"), 1)
                t = i - 3
                if live(t):
                    apart(pe, (sem("t_kT"), BLK + t + 1),
                              (sem("t_sub"), BLK + t))
                    for c in range(CB):
                        for half in range(2):
                            for b in range(2):
                                f = slice(half * DH, half * DH + DH)
                                q = slice(b * S, b * S + S)
                                mm = nc.tensor.matmul(psS[q, half, c * S:c * S + S], bqT[f, c, q], bkT[f, q],
                                                      start=True, stop=True, skip_group_check=True)
                    mm.then_inc(sem("t_sp"), 1)
                t = i - 4
                if live(t):
                    pe.wait_ge(sem("t_pn"), BLK + t + 1)
                    reach(pe, sem("t_pT"), BLK + t)
                    for c in range(CB):
                        mm = nc.tensor.transpose(psT[:, 1, c * P:c * P + P],
                                                 bpn[:, 2 * c:2 * c + 2, :].rearrange("p a j -> p (a j)"), ident[:])
                    mm.then_inc(sem("t_pTp"), 1)
                t = i - 9
                if live(t):
                    pe.wait_ge(sem("d_xf"), t + 1)
                    if live(i - 1):
                        pe.wait_ge(sem("t_xlo"), BLK + i)
                    reach(pe, sem("d_xff"), t)
                    for k in range(KD):
                        mm = nc.tensor.transpose(psQ[:, 0, D + k * P:D + k * P + P], xf[:, k * P:k * P + P], ident[:])
                    mm.then_inc(sem("d_xfTp"), 1)
                t = i - 10
                if live(t):
                    pe.wait_ge(sem("d_xff"), t + 1)
                    if live(i - 6):
                        pe.wait_ge(sem("d_X1"), i - 5)
                    reach(pe, sem("d_lg"), t)
                    for k in range(KD):
                        mm = nc.tensor.matmul(psW[:, D:D + E], xff[:, k, :], bwr[:, k, :], start=(k == 0), stop=(k == KD - 1))
                    mm.then_inc(sem("d_lgp"), 1)
                t = i - 2
                if live(t):
                    pe.wait_ge(sem("t_kn"), BLK + t + 1)
                    reach(pe, sem("t_kT"), BLK + t)
                    for c in range(CB):
                        nc.tensor.transpose(psT[:, 0, c * P:c * P + P], bq[:, c * P:c * P + P], ident[:])
                    nc.tensor.transpose(psT[:, 0, D:D + P], bk[:].rearrange("p a d -> p (a d)"), ident[:]).then_inc(sem("t_qTp"), 1)
                t = i - 1
                if live(t):
                    pe.wait_ge(sem("t_xlo"), BLK + t + 1)
                    reach(pe, sem("t_vp"), BLK + t)
                    for k in range(KD):
                        for j, (u, w) in enumerate(PASSES):
                            mm = nc.tensor.matmul(psQ[:, 1, 0:QKV], nxT[u][:, k, :], bqkv[w][:, k, :],
                                                  start=(k == 0 and j == 0), stop=(k == KD - 1 and j == 2))
                    mm.then_inc(sem("t_qp"), 1)
                t = i
                if live(t):
                    pe.wait_ge(sem("d_nx"), t + 1)
                    reach(pe, sem("t_xlo"), BLK + t)
                    if live(i - 9):
                        pe.wait_ge(sem("d_xff"), i - 8)
                    for k in range(KD):
                        mm = nc.tensor.transpose(psQ[:, 0, k * P:k * P + P], nx[:, k * P:k * P + P], ident[:])
                    mm.then_inc(sem("t_xTp"), 1)

            pe.wait_ge(sem("d_wlo"), 2)
            pe.wait_ge(sem("d_wr"), KD)
            pipeline(pe, block_step, 4, 10)
            def expert_up(p, g, par):
                s = GROUPS * p + g
                for c in range(KD):
                    reach(pe, sem(f"e_h{c}"), s)
                    for bank, w13 in ((psQ, 0), (psS, 1)):
                        for k in range(KD):
                            for j, (u, w) in enumerate(PASSES):
                                mm = nc.tensor.matmul(bank[:, c, :], ew[par][u][:, w13, k, c * P:c * P + P], xfT[w][:, k, bass.ts(g, GT)],
                                                      start=(k == 0 and j == 0), stop=(k == KD - 1 and j == 2))
                    mm.then_inc(sem(f"e_up{c}"), 1)

            def expert_down(p, g, par, gpar):
                s = GROUPS * p + g
                for c in range(KD):
                    pe.wait_ge(sem(f"e_lo{c}"), s + 1)
                reach(pe, sem("e_acc"), s)
                for t in range(G4):
                    for c in range(KD):
                        for j, (u, w) in enumerate(PASSES):
                            mm = nc.tensor.matmul(psT[:, t // 2, t % 2 * D:t % 2 * D + D], eT[gpar][u][:, c, t * P:t * P + P],
                                                  ew[par][w][:, 2, c, :], start=(c == 0 and j == 0 and t % 2 == 0),
                                                  stop=(c == KD - 1 and j == 2), skip_group_check=True)
                mm.then_inc(sem("e_dn"), 1)

            def all_groups(p, par, first=False):
                pe.wait_ge(sem("e_wlo"), p + 1)
                expert_up(p, 0, par)
                if not first:
                    expert_down(p - 1, GROUPS - 1, (par + 1) % 2, 1)
                expert_up(p, 1, par)
                expert_down(p, 0, par, 0)
                with pe.Fori(1, GROUPS // 2) as pair:
                    expert_up(p, 2 * pair, par)
                    expert_down(p, 2 * pair - 1, par, 1)
                    expert_up(p, 2 * pair + 1, par)
                    expert_down(p, 2 * pair, par, 0)

            pe.wait_ge(sem("d_xflo"), TILES)
            all_groups(0, 0, first=True)
            with pe.Fori(0, E // 2) as pair:
                all_groups(2 * pair + 1, 1)
                all_groups(2 * pair + 2, 0)
            expert_down(E, GROUPS - 1, 0, 1)


def layout(inputs):
    c = np.ascontiguousarray
    i = {k: np.asarray(v) for k, v in inputs.items()}
    first = lambda name, s: c(np.concatenate([i[s][None], i[name]], axis=0).transpose(0, 2, 1))
    return {
        "x": c(i["x"].reshape(SEQS * S, D)), "null": c(i["cond_64"]), "fside": c(i["fside_16xSxS_0"]),
        "mask0": c(i["mask_BxS_bf1"]).view(np.int32), "mask1": c(i["mask_BxS_bk0"]).view(np.int32),
        "g_norm": c(i["L0_cond_g_norm"]), "Wq0": c(i["L0_cond_Wq"]), "Wkv0": c(i["L0_cond_Wkv"]),
        "q_scale": c(i["L0_cond_q_scale"]), "k_scale": c(i["L0_cond_k_scale"]), "nb0": c(i["L0_cond_null_attn_bias"]),
        "rw0": c(i["L0_cond_w0"].reshape(D)), "rb0": c(i["L0_cond_b0"]), "rg0": c(i["L0_cond_g0"]),
        "rw1": c(i["L0_cond_w1"]), "rb1": c(i["L0_cond_b1"]), "rg1": c(i["L0_cond_g1"]),
        "rw2": c(i["L0_cond_w2"]), "rb2": c(i["L0_cond_b2"]), "Wout0": c(i["L0_cond_Wout"]),
        "g_out0": c(i["L0_cond_g_out"]), "Wfc": c(i["L0_ffn_W_fc"].T), "Wproj": c(i["L0_ffn_W_proj"].T),
        "g_in": c(i["L1_cond_g_in"]), "nb1": c(i["L1_cond_null_attn_bias"]), "Wq1": c(i["L1_cond_Wq"]),
        "Wkv1": c(i["L1_cond_Wkv"]), "Wo1": c(i["L1_cond_Wo"]), "g_out1": c(i["L1_cond_g_out"]),
        "g1": c(i["L1_ffn_g1"]), "g2": c(i["L1_ffn_g2"]),
        "Wqkv": c(np.concatenate([i["L1_ffn_Wq"], i["L1_ffn_Wkc"], i["L1_ffn_Wvc"]], axis=0).T),
        "Wo": c(i["L1_ffn_Wo"].T), "Wr": c(i["L1_ffn_Wr"].T), "ebias": c(i["L1_ffn_expert_bias"]),
        "W1": first("L1_ffn_eW1", "L1_ffn_sW1"), "W2": first("L1_ffn_eW2", "L1_ffn_sW2"),
        "W3": first("L1_ffn_eW3", "L1_ffn_sW3"),
    }


def kernel(**inputs):
    import concourse.bacc as bacc
    from concourse.bass_utils import run_bass_kernel_spmd

    nc = bacc.Bacc("TRN2", target_bir_lowering=False, num_devices=1)
    arrays = layout(inputs)
    args = {n: nc.dram_tensor(n, v.shape, mybir.dt.from_np(v.dtype), kind="ExternalInput").ap() for n, v in arrays.items()}
    out = nc.dram_tensor("out", (SEQS * S, D), F32, kind="ExternalOutput").ap()
    build(nc, args, out)
    r = run_bass_kernel_spmd(nc, [arrays], core_ids=[0])
    return np.asarray(r.results[0]["out"]).reshape(SEQS, S, D)
```

```python
from contextlib import ExitStack

import concourse.bass as bass
import numpy as np
from concourse import mybir

F32 = mybir.dt.float32
F32R = mybir.dt.float32r
BF16 = mybir.dt.bfloat16
U8 = mybir.dt.uint8
I32 = mybir.dt.int32
ALU = mybir.AluOpType
ACT = mybir.ActivationFunctionType
AX = mybir.AxisListType

P = 128
SEQS, S, D = 64, 64, 256
TILES = SEQS * S // P
KD = D // P
H, DH = 16, 64
INNER = H * DH
CH = INNER // P
KVN = 2 * DH + H
FF = 4 * D
FC = FF // P
G4 = 4
GROUPS = TILES // G4
GT = G4 * P
HB = 4
CB = HB * DH // P
QKV = D + 2 * DH
E = 8
EP = E + 1
TOP_K = 2
ROUTED = TOP_K * TILES + E
SLOTS = ROUTED * P
SHARED_SLOT = 1
ROW = D + 1
NOWHERE = 1 << 20
EW = 3 * KD * D
NEG = -1e30
LIF_STEPS, LIF_BETA, LIF_THRESHOLD = 5, 0.9, 1.0

BLK = 2 * TILES

CONSTANTS = 11

PASSES = ((0, 0), (0, 1), (1, 0))


def reach(eng, sem, n):
    if not isinstance(n, int) or n > 0:
        eng.wait_ge(sem, n)


def spread(t, par):
    return 32 * (t - par) + 64


def live(t):
    return not isinstance(t, int) or 0 <= t < TILES


def pipeline(eng, body, ahead, behind, between=None):
    first, last = behind + 1, TILES - ahead
    first += first % 2
    last -= last % 2
    for i in range(-ahead, first):
        body(i, i % 2)
        if between:
            between(i)
    with eng.Fori(first // 2, last // 2) as pair:
        body(2 * pair, 0)
        body(2 * pair + 1, 1)
    for i in range(last, TILES + behind):
        body(i, i % 2)
        if between:
            between(i)


def expert_steps(eng, step, splits=None):
    end = TILES + ROUTED

    def four(quad, shared):
        for m in range(4):
            step(4 * quad + m, m, shared)
            if splits and shared == "splits" and m % 2:
                splits(2 * quad - 3 + m // 2)

    for i in range(0, 8):
        step(i, i % 4)
    with eng.Fori(2, 3) as quad:
        four(quad, "shared")
    with eng.Fori(3, 6) as quad:
        four(quad, "splits")
    for i in range(24, TILES + 8):
        step(i, i % 4)
        if i == 24 and splits:
            splits(EP)
    with eng.Fori((TILES + 8) // 4, (end - 1) // 4) as quad:
        four(quad, None)
    for i in range((end - 1) // 4 * 4, end + 4):
        step(i, i % 4)


def kind(t, shared):
    if not isinstance(t, int):
        return "shared" if shared else "routed"
    return "shared" if 0 <= t < TILES else "routed" if TILES <= t < TILES + ROUTED else None


def loaded(t, m):
    return 4 * (t - m) + 16


def stored(r, par):
    return 8 * (r - par)


def build(nc, a, out):
    ctx = ExitStack()
    with ctx:
        base = -(-nc.sbuf_base // 64) * 64
        place = {}

        def region(name, nbytes, at=None):
            nonlocal base
            if at is None:
                at, base = base, base + nbytes
            place[name] = [at, at + nbytes]
            return at

        def sb(where, name, shape, dt):
            n = int(np.prod(shape[1:])) * (1 if dt == U8 else 2 if dt == BF16 else 4)
            at, end = place[where]
            place[where][0] = at + -(-n // 32) * 32
            assert place[where][0] <= end, (where, name, place[where][0] - end)
            return nc.alloc_sbuf_tensor_at(name, shape, dt, offset=at)

        K = 1024
        region("x", 32 * K)
        region("stage", 18 * K)
        region("bias", 4 * K)
        region("const", 12 * K)
        work = region("work", 41 * K)
        attw = region("attw", 35 * K)
        ffw = region("ffw", 32 * K)
        region("o", 32 * K)
        assert base <= 229344, base
        region("ffn_work", 41 * K, at=work)
        region("blk_w", 32 * K, at=ffw)
        region("xf_all", 41 * K, at=work)
        assert attw == work + 41 * K

        X = sb("x", "X", [P, TILES, D], F32)
        O = sb("o", "O", [P, TILES, D], F32)

        sems = {}

        def sem(name):
            if name not in sems:
                sems[name] = ctx.enter_context(nc.semaphore(name))
            return sems[name]

        def apart(eng, *waits):
            for signal, n in waits:
                reach(eng, signal, n)
                eng.sem_inc(sem("apart"), 1)

        psQ = ctx.enter_context(nc.psum_tensor("psQ", [P, 2, 512], F32))
        psS = ctx.enter_context(nc.psum_tensor("psS", [P, 2, 512], F32))
        psT = ctx.enter_context(nc.psum_tensor("psT", [P, 2, 512], F32))
        psW = ctx.enter_context(nc.psum_tensor("psW", [P, 512], F32))
        psM = ctx.enter_context(nc.psum_tensor("psM", [P, 512], F32))

        ident = sb("const", "ident", [P, P], F32)
        rms_eps = sb("const", "rms_eps", [P, 1], F32)
        ln_eps = sb("const", "ln_eps", [P, 1], F32)
        mhalf = sb("const", "mhalf", [P, 32], F32)
        route_at = place["const"][0]
        mask_w = sb("const", "mask_w", [P, TILES, S // 4], I32)
        negmask = sb("const", "negmask", [P, TILES, S], BF16)
        assert place["const"][0] >= route_at + 6 * K
        bias_t = sb("bias", "bias_t", [P, H, S], F32)
        region("masked", 4 * K, at=ffw + 28 * K)
        masked = sb("masked", "masked_bias", [P, H, S], F32)
        gcol = sb("const", "gcol", [P, KD], F32)
        nkb = sb("const", "nkb", [P, DH], F32)
        nvb = sb("const", "nvb", [P, DH], F32)
        nvcol = sb("const", "nvcol", [P, 1], F32)
        nbias = sb("const", "nbias", [P, H], F32)
        ksc = sb("const", "ksc", [P, 1], F32)
        qsc = sb("const", "qsc", [P, 1], F32)
        ksrow = sb("const", "ksrow", [P, DH], F32)
        qsrow = sb("const", "qsrow", [P, DH], F32)
        tiny = sb("const", "tiny", [P, 8], F32)

        wq = [sb("attw", f"wq{i}", [P, KD, INNER], F32R) for i in range(2)]
        wkvn = [sb("attw", f"wkvn{i}", [P, KD, KVN], F32R) for i in range(2)]
        wout = [sb("attw", f"wout{i}", [P, CH, D], F32R) for i in range(2)]
        st6 = sb("work", "st6", [P, 6], F32)
        mv = [sb("work", f"mv{i}", [P, 2], F32) for i in range(2)]
        vareps = sb("work", "vareps", [P, 1], F32)
        rstd = [sb("work", f"rstd{i}", [P, 1], F32) for i in range(2)]
        xn = sb("work", "xn", [P, D], F32)
        xT = [sb("work", f"xT{i}", [P, KD, P], F32R) for i in range(2)]
        kvs = sb("work", "kvs", [P, KVN], F32)
        junk = sb("work", "junk", [P, DH], F32)
        sq = sb("work", "sq", [P, INNER], F32)
        qss = sb("work", "qss", [P, H + 1], F32)
        qmx = sb("work", "qmx", [P, H + 1], F32)
        rq = [sb("work", f"rq{i}", [P, H], F32) for i in range(2)]
        rk = sb("work", "rk", [P, 1], F32)
        qn = sb("work", "qn", [P, INNER], F32)
        kn = sb("work", "kn", [P, 2, DH], F32)
        sn = [sb("work", f"sn{i}", [P, H], F32) for i in range(2)]
        vp = [sb("work", f"vp{i}", [P, DH], F32) for i in range(2)]
        vv = [sb("work", f"vv{i}", [P, 2, DH], F32) for i in range(2)]
        qT = sb("work", "qT", [P, CH, P], F32)
        kT = sb("work", "kT", [P, P], F32)
        m16 = sb("work", "m16", [P, H], F32)
        mm16 = sb("work", "mm16", [P, H], F32)
        ex = sb("work", "ex", [P, H, S + 1], F32)
        den = sb("work", "den", [P, H], F32)
        rden = sb("work", "rden", [P, H], F32)
        pn = sb("work", "pn", [P, H, S], F32)
        pT = sb("work", "pT", [P, CH, P], F32)
        oT = [sb("work", f"oT{i}", [P, CH, P], F32R) for i in range(2)]

        wfc = [sb("ffw", f"wfc{i}", [P, KD, FF], F32R) for i in range(2)]
        wpr = [sb("ffw", f"wpr{i}", [P, FC, D], F32R) for i in range(2)]
        gout0 = sb("const", "gout0", [P, KD], F32)
        c0 = sb("ffn_work", "c0", [P, G4, D], F32)
        cT = [sb("ffn_work", f"cT{i}", [P, KD, GT], F32R) for i in range(2)]
        hf = [sb("ffn_work", f"hf{i}", [P, GT], F32) for i in range(2)]
        hT = [[sb("ffn_work", f"hT{i}{j}", [P, GT], F32R) for j in range(2)] for i in range(2)]
        cur = sb("ffn_work", "cur", [P, G4 * D], F32)
        mem = sb("ffn_work", "mem", [P, G4 * D], F32)
        spk = [sb("ffn_work", f"spk{i}", [P, G4 * D], BF16) for i in range(2)]
        count = sb("ffn_work", "count", [P, G4 * D], BF16)
        up_bank = (psQ[:, 0, :], psQ[:, 1, :], psW[:], psM[:])
        fst6 = sb("ffn_work", "fst6", [P, G4, 6], F32)
        fmv = sb("ffn_work", "fmv", [P, G4, 2], F32)
        fve = sb("ffn_work", "fve", [P, G4], F32)
        frs = sb("ffn_work", "frs", [P, G4], F32)

        bqkv = [sb("blk_w", f"bqkv{i}", [P, KD, QKV], F32R) for i in range(2)]
        bwo = [sb("blk_w", f"bwo{i}", [P, KD, D], F32R) for i in range(2)]
        bwr = sb("blk_w", "bwr", [P, KD, E], F32)
        gout1 = sb("blk_w", "gout1", [P, D], F32)
        g1col = sb("blk_w", "g1col", [P, KD], F32)
        g2col = sb("const", "g2col", [P, KD], F32)
        ebias = sb("const", "ebias", [P, E], F32)
        dst6 = sb("blk_w", "dst6", [P, 6], F32)
        dmv = [sb("blk_w", f"dmv{i}", [P, 2], F32) for i in range(2)]
        dvar = sb("blk_w", "dvar", [P, 1], F32)
        drs = [sb("blk_w", f"drs{i}", [P, 1], F32) for i in range(2)]
        ss1 = [sb("blk_w", f"ss1{i}", [P, 1], F32) for i in range(2)]
        ms1 = sb("blk_w", "ms1", [P, 1], F32)
        r1 = [sb("blk_w", f"r1{i}", [P, 1], F32) for i in range(2)]
        ss2 = [sb("blk_w", f"ss2{i}", [P, 1], F32) for i in range(2)]
        ms2 = sb("blk_w", "ms2", [P, 1], F32)
        r2 = [sb("blk_w", f"r2{i}", [P, 1], F32) for i in range(2)]
        sqj = [sb("blk_w", f"sqj{i}", [P, D], F32) for i in range(2)]
        nx = sb("blk_w", "nx", [P, D], F32)
        nxT = [sb("blk_w", f"nxT{i}", [P, KD, P], F32R) for i in range(2)]
        bq = sb("blk_w", "bq", [P, D], F32)
        bk = sb("blk_w", "bk", [P, 2, DH], F32)
        bqT = sb("blk_w", "bqT", [P, CB, P], F32)
        bkT = sb("blk_w", "bkT", [P, P], F32)
        bm = sb("blk_w", "bm", [P, HB], F32)
        be = sb("blk_w", "be", [P, HB, S], F32)
        bden = sb("blk_w", "bden", [P, HB], F32)
        brd = sb("blk_w", "brd", [P, HB], F32)
        bpn = sb("blk_w", "bpn", [P, HB, S], F32)
        bpT = sb("blk_w", "bpT", [P, CB, P], F32)
        bvv = [sb("blk_w", f"bvv{i}", [P, 2, DH], F32) for i in range(2)]
        boT = [sb("blk_w", f"boT{i}", [P, CB, P], F32R) for i in range(2)]
        xf = sb("blk_w", "xf", [P, D], F32)
        xff = sb("blk_w", "xff", [P, KD, P], F32)
        xf_at = place["xf_all"][0]
        xf_all = sb("xf_all", "xf_all", [P, TILES, ROW], F32)
        w_at = place["xf_all"][0]
        W = nc.alloc_sbuf_tensor_at("W", [P, EP, 2, EW], F32R, offset=w_at)
        raw_w = nc.alloc_sbuf_tensor_at("raw_w", [P, EP, 2, EW], F32, offset=w_at)
        assert w_at + 12 * K * SHARED_SLOT >= attw and w_at + 12 * K * EP <= 229344
        v_all = sb("xf_all", "v_all", [P, TILES, DH], F32)

        logits_at = place["const"][0]
        logits = sb("const", "logits", [P, TILES, E], F32)
        iota8 = sb("const", "iota8", [P, E], F32)
        before_f = sb("const", "before_f", [P, P], F32)
        before = sb("const", "before", [P, P], BF16)
        ones = sb("const", "ones", [P, P], BF16)
        top_w = [sb("const", f"top_w{i}", [P, TILES], F32) for i in range(TOP_K)]
        pos = [sb("const", f"pos{i}", [P, TILES], I32) for i in range(TOP_K)]
        slots = sb("const", "slots", [1, ROUTED], I32)
        region("route", 6 * K, at=route_at)
        region("route2", 4 * K, at=place["bias"][0] - 4 * K)
        rt = [sb("route2", f"rt{i}", [P, TILES, E], F32) for i in range(4)]
        rc = [sb("route", f"rc{i}", [P, TILES], F32) for i in range(5)]
        chosen = sb("route", "chosen", [P, TILES, E], BF16)
        upto = [sb("route", f"upto{i}", [P, TILES, E], F32) for i in range(2)]
        iota_rows = sb("route", "iota_rows", [P, TILES], F32)
        iota_tile = sb("route", "iota_tile", [1, ROUTED], F32)
        n_tiles = sb("route", "n_tiles", [P, E], F32)
        end_tile = [sb("route", f"end_tile{i}", [P, E], F32) for i in range(2)]

        region("tile", 18 * K, at=place["stage"][0])
        rows = sb("tile", "rows", [P, 4, ROW], F32)
        exT = [[sb("tile", f"exT{i}{j}", [P, KD, P], F32R) for j in range(2)] for i in range(2)]
        sg = sb("tile", "sg", [P, D], F32)
        eh = [sb("tile", f"eh{i}", [P, D], F32) for i in range(2)]
        ehT = [sb("tile", f"ehT{j}", [P, KD, P], F32R) for j in range(2)]
        result = [sb("tile", f"result{i}", [P, D], F32) for i in range(2)]
        ids = sb("tile", "ids", [P, ROUTED], I32)
        idx = [sb("tile", f"idx{i}", [P, 1], I32) for i in range(2)]
        by_end = sb("tile", "by_end", [1, ROUTED, E], F32)
        slot_f = [sb("route", f"slot_f{i}", [1, ROUTED], F32) for i in range(2)]
        YS = (0, 0, 0, 1, 1, 2, 2, 3)
        both = [nc.alloc_sbuf_tensor_at(f"both{i}", [P, G4, TOP_K, D], F32, offset=xf_at + 8 * K * i) for i in range(GROUPS)]
        blank = nc.alloc_sbuf_tensor_at("blank", [P, ROW], F32, offset=logits_at)
        sorted_rows = nc.dram_tensor("sorted_rows", (SLOTS, ROW), F32, kind="Internal").ap()
        results = nc.dram_tensor("results", (SEQS * S * TOP_K, D), F32, kind="Internal").ap()

        raw_q = nc.alloc_sbuf_tensor_at("raw_q", [P, KD, INNER], F32, offset=place["stage"][0])
        raw_kvn = nc.alloc_sbuf_tensor_at("raw_kvn", [P, KD, KVN], F32, offset=place["stage"][0] + 8 * K)
        raw_o = nc.alloc_sbuf_tensor_at("raw_o", [P, CH, D], F32, offset=place["stage"][0] + 8 * K + 1152)
        raw_bqkv = nc.alloc_sbuf_tensor_at("raw_bqkv", [P, KD, QKV], F32, offset=place["stage"][0])
        raw_bwo = nc.alloc_sbuf_tensor_at("raw_bwo", [P, KD, D], F32, offset=place["stage"][0] + 3 * K)
        rp = place["o"][1] - 32 * K
        NPOS = 2 * S - 1
        region("relpos", 32 * K, at=rp)
        r_w1 = sb("relpos", "r_w1", [P, KD, D], F32)
        r_w2 = sb("relpos", "r_w2", [P, KD, H], F32)
        r_rows = {n: sb("relpos", f"r_{n}", [P, D], F32) for n in ("w0", "b0", "g0", "b1", "g1")}
        r_b2 = sb("relpos", "r_b2", [H, 1], F32)
        r_pos = sb("relpos", "r_pos", [P, 1], F32)
        r_h = sb("relpos", "r_h", [P, D], F32)
        r_hT = sb("relpos", "r_hT", [P, KD, P], F32)
        r_st = sb("relpos", "r_st", [P, 6], F32)
        r_mv = sb("relpos", "r_mv", [P, 2], F32)
        r_rs = sb("relpos", "r_rs", [P, 2], F32)
        r_out = sb("relpos", "r_out", [H, P], F32)
        wn_tmp = sb("relpos", "wn_tmp", [P, H, DH], F32)
        rel_dram = nc.dram_tensor("rel_bias", (H, S, P), F32, kind="Internal").ap()

        x_dram = a["x"].rearrange("(t p) d -> p t d", p=P)
        out_dram = out.rearrange("(t p) d -> p t d", p=P)

        LAYERS = (
            dict(n="a", done=0, cosine=True, mask="mask0", g="g_norm", wq="Wq0", wkv="Wkv0", wo="Wout0", nb="nb0"),
            dict(n="c", done=TILES, cosine=False, mask="mask1", g="g_in", wq="Wq1", wkv="Wkv1", wo="Wo1", nb="nb1"),
        )

        LOADED = {"a": 16 * 17, "c": 16 * 11}
        FIRST = dict(loaded=LOADED["a"], braw=32, causal=2, nk=6, wnp=KD, wn=KD, whi=2 * KD + 1,
                     wlo=2 * KD + 1, mask=1)

        def nth(L, name, n):
            return n + FIRST[name] if L["done"] else n

        block = ctx.enter_context(nc.Block())

        @block.sync
        def _(sp):
            def load_layer(L):
                ld = sem("l_loaded")
                sp.dma_start(gcol[:], a[L["g"]].rearrange("(k p) -> p k", p=P), allow_slow_non_contiguous=True).then_inc(ld, 16)
                sp.dma_start(nkb[:], a["null"][0:1, :].to_broadcast([P, DH])).then_inc(ld, 16)
                sp.dma_start(nvb[:], a["null"][1:2, :].to_broadcast([P, DH])).then_inc(ld, 16)
                for half in range(2):
                    sp.dma_start(nvcol[half * DH:(half + 1) * DH, :], a["null"][1:2, :].rearrange("o d -> d o"),
                                 allow_slow_non_contiguous=True).then_inc(ld, 16)
                sp.dma_start(nbias[:], a[L["nb"]].rearrange("(o h) -> o h", o=1).to_broadcast([P, H])).then_inc(ld, 16)
                for b in range(2):
                    sp.dma_start(mask_w[b * S:(b + 1) * S, :, :], a[L["mask"]].rearrange("(t b) j -> b t j", b=2)[b:b + 1]
                                 .to_broadcast([S, TILES, S // 4])).then_inc(ld, 16)
                sp.dma_start(raw_q[:], a[L["wq"]].rearrange("(k p) n -> p k n", p=P)).then_inc(ld, 16)
                sp.dma_start(raw_kvn[:, :, 0:2 * DH], a[L["wkv"]].rearrange("(k p) n -> p k n", p=P)).then_inc(ld, 16)
                sp.dma_start(raw_o[:], a[L["wo"]].rearrange("(k p) n -> p k n", p=P)).then_inc(ld, 16)

            def load_ffn():
                sp.wait_ge(sem("l_wlo"), 2 * KD + 1)
                sp.dma_start(gout0[:], a["g_out0"].rearrange("(k p) -> p k", p=P), allow_slow_non_contiguous=True).then_inc(sem("f_loaded"), 16)
                sp.dma_start(raw_q[:], a["Wfc"].rearrange("(k p) n -> p k n", p=P)).then_inc(sem("f_loaded"), 16)
                sp.dma_start(raw_o[:], a["Wproj"].rearrange("(k p) n -> p k n", p=P)).then_inc(sem("f_loaded"), 16)

            def load_block():
                sp.wait_ge(sem("l_wlo"), nth(LAYERS[1], "wlo", 2 * KD + 1))
                ld = sem("d_loaded")
                for col, name in ((g1col, "g1"), (g2col, "g2")):
                    sp.dma_start(col[:], a[name].rearrange("(k p) -> p k", p=P), allow_slow_non_contiguous=True).then_inc(ld, 16)
                sp.dma_start(gout1[:], a["g_out1"].rearrange("(o d) -> o d", o=1).to_broadcast([P, D])).then_inc(ld, 16)
                sp.dma_start(ebias[:], a["ebias"].rearrange("(o e) -> o e", o=1).to_broadcast([P, E])).then_inc(ld, 16)
                sp.dma_start(raw_bqkv[:], a["Wqkv"].rearrange("(k p) n -> p k n", p=P)).then_inc(ld, 16)
                sp.dma_start(raw_bwo[:], a["Wo"].rearrange("(k p) n -> p k n", p=P)).then_inc(ld, 16)
                sp.dma_start(bwr[:], a["Wr"].rearrange("(k p) n -> p k n", p=P)).then_inc(ld, 16)

            def spread_v(L, before_loop):
                n = L["n"]
                done = L["done"]

                def step(t, par):
                    apart(sp, (sem("t_vp"), done + t + 1))
                    reach(sp, sem("t_pv"), done + t - 1)
                    for half in range(2):
                        for b in range(2):
                            sp.dma_start(vv[par][half * DH:(half + 1) * DH, b, :],
                                         vp[par][b * S:(b + 1) * S, :]).then_inc(sem(f"t_vv{par}"), 16)

                for t in range(2):
                    step(t, t)
                before_loop()
                with sp.Fori(1, TILES // 2) as pair:
                    step(2 * pair, 0)
                    step(2 * pair + 1, 1)

            sp.dma_start(X[:, 0:4, :], x_dram[:, 0:4, :]).then_inc(sem("x_in0"), 16)
            load_layer(LAYERS[0])
            for half in range(2):
                for row, name in ((ksc, "k_scale"), (qsc, "q_scale")):
                    sp.dma_start(row[half * DH:(half + 1) * DH, :], a[name].rearrange("(d o) -> d o", o=1),
                                 allow_slow_non_contiguous=True).then_inc(sem("l_loaded"), 16)
            for row, name in ((ksrow, "k_scale"), (qsrow, "q_scale")):
                sp.dma_start(row[:], a[name].rearrange("(o d) -> o d", o=1).to_broadcast([P, DH])).then_inc(sem("l_loaded"), 16)
            for name, key in (("w0", "rw0"), ("b0", "rb0"), ("g0", "rg0"), ("b1", "rb1"), ("g1", "rg1")):
                sp.dma_start(r_rows[name][:], a[key].rearrange("(o d) -> o d", o=1).to_broadcast([P, D])).then_inc(sem("rel_loaded"), 16)
            sp.dma_start(r_w1[:], a["rw1"].rearrange("(k p) n -> p k n", p=P)).then_inc(sem("rel_loaded"), 16)
            sp.dma_start(r_w2[:], a["rw2"].rearrange("(k p) n -> p k n", p=P)).then_inc(sem("rel_loaded"), 16)
            sp.dma_start(r_b2[:], a["rb2"].rearrange("(h o) -> h o", o=1), allow_slow_non_contiguous=True).then_inc(sem("rel_loaded"), 16)
            sp.dma_start(X[:, 4:TILES, :], x_dram[:, 4:TILES, :]).then_inc(sem("x_in1"), 16)
            sp.wait_ge(sem("rel_out"), 1)
            sp.dma_start(rel_dram, r_out[:].unsqueeze(1).to_broadcast([H, S, P])).then_inc(sem("rel_stored"), 16)
            sp.wait_ge(sem("rel_stored"), 16)
            for half in range(2):
                sp.dma_start(bias_t[half * S:(half + 1) * S, :, :],
                             bass.AP(rel_dram.tensor, S - 1, [[P - 1, S], [S * P, H], [1, S]])).then_inc(sem("l_braw"), 16)
            spread_v(LAYERS[0], before_loop=load_ffn)
            sp.wait_ge(sem("const_pool"), CONSTANTS)
            sp.dma_start(sorted_rows.rearrange("(i p) d -> p i d", p=P),
                         blank[:].unsqueeze(1).to_broadcast([P, ROUTED, ROW])).then_inc(sem("emptied"), 16)
            sp.wait_ge(sem("f_wlo"), KD + 1)
            sp.wait_ge(sem("t_oev"), TILES)
            load_layer(LAYERS[1])
            sp.wait_ge(sem("t_bm"), TILES)
            for half in range(2):
                sp.dma_start(bias_t[half * S:(half + 1) * S, :, :], a["fside"].rearrange("h i j -> i h j")).then_inc(sem("l_braw"), 16)
            spread_v(LAYERS[1], before_loop=load_block)
            def load_expert(p, slot, done):
                w13 = raw_w[:, slot, 1, 0:2 * KD * D].rearrange("p (k w n) -> p k w n", k=KD, w=2)
                for j, w in enumerate(("W1", "W3")):
                    sp.dma_start(w13[:, :, j, :], a[w][p].rearrange("(k p) n -> p k n", p=P)).then_inc(done, 16)
                sp.dma_start(raw_w[:, slot, 1, 2 * KD * D:EW].rearrange("p (k n) -> p k n", k=KD),
                             a["W2"][p].rearrange("(k p) n -> p k n", p=P)).then_inc(done, 16)

            sp.wait_ge(sem("t_oev"), 2 * TILES)
            for p in range(2):
                load_expert(p, SHARED_SLOT + p, sem("e_first"))

            def spread_block_v(t, par):
                apart(sp, (sem("t_vp"), BLK + t + 1))
                reach(sp, sem("t_pv"), BLK + t - 1)
                for half in range(2):
                    for b in range(2):
                        sp.dma_start(bvv[par][half * DH:(half + 1) * DH, b, :],
                                     v_all[b * S:(b + 1) * S, t, :]).then_inc(sem(f"t_vv{par}"), 16)

            for t in range(2):
                spread_block_v(t, t)
            with sp.Fori(1, TILES // 2) as pair:
                spread_block_v(2 * pair, 0)
                spread_block_v(2 * pair + 1, 1)
            sp.wait_ge(sem("d_R"), TILES)
            sp.wait_ge(sem("d_lg"), TILES)
            sp.wait_ge(sem("d_xfa"), TILES)
            for p in range(2, EP):
                load_expert(p, (p + 1) % EP, sem("e_rest"))

            def load_rows(pair, b, routed):
                if not isinstance(pair, int) or pair > 1:
                    apart(sp, (sem("e_xTp"), 2 * pair - 2))
                if routed and (not isinstance(pair, int) or pair > TILES // 2 + 1):
                    sp.wait_ge(sem("e_id"), 2 * pair - TILES - 2)
                if routed:
                    tiles = sorted_rows.rearrange("(q j p) d -> q p j d", j=2, p=P)[pair - TILES // 2]
                else:
                    tiles = xf_all[:, bass.ds(2 * pair, 2), 0:D]
                sp.dma_start(rows[:, 2 * b:2 * b + 2, 0:ROW if routed else D], tiles).then_inc(sem(f"e_rows{b}"), 16)

            for pair in range(2):
                load_rows(pair, pair, False)
            with sp.Fori(1, TILES // 4) as quad:
                load_rows(2 * quad, 0, False)
                load_rows(2 * quad + 1, 1, False)
            sp.wait_ge(sem("sorted"), 16 * TILES * TOP_K)
            for pair in range(2):
                load_rows(TILES // 2 + pair, pair, True)
            with sp.Fori(TILES // 4 + 1, (TILES + ROUTED) // 4) as quad:
                load_rows(2 * quad, 0, True)
                load_rows(2 * quad + 1, 1, True)
            for par in range(2):
                sp.wait_ge(sem(f"e_stored{par}"), 16 * ROUTED // 2)
            for g in range(GROUPS):
                sp.dma_start(both[g][:], results.rearrange("(g j p k) d -> g p j k d", j=G4, p=P, k=TOP_K)[g]
                             ).then_inc(sem(f"y_in{YS[g]}"), 16)
            for g in range(GROUPS):
                sp.wait_ge(sem("y_acc"), g + 1)
                sp.dma_start(out_dram[:, G4 * g:G4 * g + G4, :], X[:, G4 * g:G4 * g + G4, :]).then_inc(sem("stored"), 16)
            sp.wait_ge(sem("stored"), 16 * GROUPS)

        @block.gpsimd
        def _(pool):
            c = sem("const_pool")
            nc.gpsimd.memset(ident[:], 0.0).then_inc(c, 1)
            nc.gpsimd.memset(mhalf[:], -0.5).then_inc(c, 1)
            nc.gpsimd.memset(ln_eps[:], 1e-5).then_inc(c, 1)
            nc.gpsimd.memset(rms_eps[:], 1e-6).then_inc(c, 1)
            nc.gpsimd.iota(r_pos[:], pattern=[[0, 1]], base=S - 1, channel_multiplier=-1,
                           allow_small_or_imprecise_dtypes=True).then_inc(c, 1)
            nc.gpsimd.memset(before_f[:], 1.0).then_inc(c, 1)
            nc.gpsimd.memset(ones[:], 1.0).then_inc(c, 1)
            nc.gpsimd.memset(blank[:], 0.0).then_inc(c, 1)
            pool.wait_ge(c, 8)
            nc.gpsimd.memset(blank[:, D:ROW].bitcast(I32), NOWHERE).then_inc(c, 1)
            nc.gpsimd.affine_select(out=before_f[:], in_=before_f[:], compare_op=ALU.is_gt, fill=0.0, base=0,
                                    pattern=[[1, P]], channel_multiplier=-1).then_inc(c, 1)
            nc.gpsimd.affine_select(out=ident[:], in_=ident[:], compare_op=ALU.not_equal, fill=1.0, base=0,
                                    pattern=[[-1, P]], channel_multiplier=1).then_inc(c, 1)

            pool.wait_ge(sem("nk_ss"), 1)
            nc.gpsimd.tensor_tensor(tiny[:, 2:3], tiny[:, 1:2], mhalf[:, 0:1], ALU.pow).then_inc(sem("nk_r"), 1)
            def rel_rstd(k):
                pool.wait_ge(sem("rel_mv"), k + 1)
                nc.gpsimd.tensor_scalar(r_rs[:, 0:1], r_mv[:, 1:2], 1.0, 1e-5, ALU.mult, ALU.add).then_inc(sem("rel_rstd"), 1)
                pool.wait_ge(sem("rel_rstd"), 2 * k + 1)
                nc.gpsimd.tensor_tensor(r_rs[:, 1:2], r_rs[:, 0:1], mhalf[:, 0:1], ALU.pow).then_inc(sem("rel_rstd"), 1)

            def causal(L):
                pool.wait_ge(sem("l_braw"), nth(L, "braw", 32))
                pool.wait_ge(sem("t_rstd"), L["done"] + 3)
                if L["cosine"]:
                    pool.wait_ge(sem("t_rk"), 2)
                    pool.wait_ge(sem("t_rq"), 1)
                else:
                    pool.wait_ge(sem("f_lo"), FC * GROUPS)
                for half in range(2):
                    v = bias_t[half * S:(half + 1) * S, :, :]
                    nc.gpsimd.affine_select(out=v, in_=v, compare_op=ALU.is_ge, fill=NEG, base=0,
                                            pattern=[[0, H], [-1, S]], channel_multiplier=1).then_inc(sem("l_causal"), 1)
                pool.wait_ge(sem("l_causal"), nth(L, "causal", 2))

            rel_rstd(0)

            def attention(L, between):
                n = L["n"]
                done = L["done"]

                def step(i, par):
                    t = i - 2
                    if live(t):
                        pool.wait_ge(sem("t_rden"), done + t + 1)
                        reach(pool, sem("t_pTp"), done + t)
                        nc.gpsimd.tensor_tensor(pn[:], ex[:, :, 0:S], rden[:].unsqueeze(2).to_broadcast([P, H, S]),
                                                ALU.mult).then_inc(sem("t_pn"), 1)
                    t = i
                    if live(t) and L["cosine"]:
                        pool.wait_ge(sem("t_kmx"), done + t + 1)
                        reach(pool, sem("t_kn"), done + t)
                        nc.gpsimd.tensor_tensor(rk[:], qmx[:, H:H + 1], mhalf[:, 0:1], ALU.pow).then_inc(sem("t_rk"), 1)
                    t = i - 1
                    if live(t):
                        if isinstance(t, int) and t == 0:
                            causal(L)
                            pool.wait_ge(sem("l_mask"), nth(L, "mask", 1))
                        reach(pool, sem("t_m0"), done + t)
                        nc.gpsimd.tensor_tensor(masked[:], bias_t[:], negmask[:, bass.ds(t, 1), :].to_broadcast([P, H, S]),
                                                ALU.add).then_inc(sem("t_bm"), 1)
                    t = i + 2
                    if live(t):
                        pool.wait_ge(sem("t_mv"), done + t + 1)
                        reach(pool, sem("t_rstd"), done + t)
                        nc.gpsimd.tensor_tensor(vareps[:], mv[par][:, 1:2], ln_eps[:], ALU.add).then_inc(sem("t_ve"), 1)
                        pool.wait_ge(sem("t_ve"), done + t + 1)
                        reach(pool, sem("t_xn"), done + t - 1)
                        nc.gpsimd.tensor_tensor(rstd[par][:], vareps[:], mhalf[:, 0:1], ALU.pow).then_inc(sem("t_rstd"), 1)
                    t = i
                    if live(t) and L["cosine"]:
                        pool.wait_ge(sem("t_qmx"), done + t + 1)
                        reach(pool, sem("t_snr"), 2 * t - 2)
                        nc.gpsimd.tensor_tensor(rq[par][:], qmx[:, 0:H], mhalf[:, 0:H], ALU.pow).then_inc(sem("t_rq"), 1)
                        pool.wait_ge(sem("t_rq"), done + t + 1)
                        by_head = qn[:].rearrange("p (h d) -> p h d", h=H)
                        nc.gpsimd.tensor_tensor(by_head, by_head, rq[par][:].unsqueeze(2).to_broadcast([P, H, DH]),
                                                ALU.mult).then_inc(sem("t_qs"), 1)

                pipeline(pool, step, 2, 3, between)

            def second_layer(i):
                if i == -1:
                    rel_rstd(1)

            attention(LAYERS[0], second_layer)
            def ffn_norm(g):
                pool.wait_ge(sem("f_mv"), G4 * g + G4)
                nc.gpsimd.tensor_tensor(fve[:], fmv[:, :, 1], ln_eps[:].to_broadcast([P, G4]), ALU.add).then_inc(sem("f_ve"), 1)
                pool.wait_ge(sem("f_ve"), g + 1)
                nc.gpsimd.tensor_tensor(frs[:], fve[:], mhalf[:, 0:G4], ALU.pow).then_inc(sem("f_rs"), 1)

            def ffn_lo(s, par):
                pool.wait_ge(sem("f_hi"), s + 1)
                nc.gpsimd.tensor_tensor(hT[par][1][:], hf[par][:], hT[par][0][:].bitcast(F32), ALU.subtract).then_inc(sem("f_lo"), 1)

            def ffn(g, first=False, last=False):
                for f in range(FC):
                    ffn_lo(FC * g + f, f % 2)
                    if not last and f == 0:
                        ffn_norm(g + 1)

            ffn_norm(0)
            ffn(0, first=True)
            ffn(1)
            with pool.Fori(2, GROUPS - 1) as g:
                ffn(g)
            ffn(GROUPS - 1, last=True)
            pool.wait_ge(sem("f_dn"), FC * GROUPS)

            attention(LAYERS[1], None)
            def mean_root(n, t, par, ss, ms, r, used):
                pool.wait_ge(sem(f"d_ss{n}"), t + 1)
                reach(pool, sem(f"d_r{n}"), t)
                nc.gpsimd.tensor_tensor(ms[:], ss[par][:], rms_eps[:], ALU.add).then_inc(sem(f"d_ms{n}"), 1)
                pool.wait_ge(sem(f"d_ms{n}"), t + 1)
                reach(pool, sem(used), t - 1)
                nc.gpsimd.tensor_tensor(r[par][:], ms[:], mhalf[:, 0:1], ALU.pow).then_inc(sem(f"d_r{n}"), 1)

            def block_step(i, par):
                other = (par + 1) % 2
                t = i - 4
                if live(t):
                    pool.wait_ge(sem("t_rden"), BLK + t + 1)
                    reach(pool, sem("t_pTp"), BLK + t)
                    nc.gpsimd.tensor_tensor(bpn[:], be[:], brd[:].unsqueeze(2).to_broadcast([P, HB, S]), ALU.mult).then_inc(sem("t_pn"), 1)
                t = i - 7
                if live(t):
                    pool.wait_ge(sem("d_X1"), t + 1)
                    nc.gpsimd.tensor_tensor(X[:, t, :], X[:, t, :], O[:, t, :], ALU.add).then_inc(sem("d_R"), 1)
                t = i - 7
                if live(t):
                    mean_root(2, t, other, ss2, ms2, r2, "d_xf")
                t = i + 4
                if live(t):
                    pool.wait_ge(sem("t_mv"), BLK + t + 1)
                    reach(pool, sem("t_rstd"), BLK + t)
                    nc.gpsimd.tensor_tensor(dvar[:], dmv[par][:, 1:2], ln_eps[:], ALU.add).then_inc(sem("t_ve"), 1)
                    pool.wait_ge(sem("t_ve"), BLK + t + 1)
                    reach(pool, sem("d_X0"), t - 1)
                    nc.gpsimd.tensor_tensor(drs[par][:], dvar[:], mhalf[:, 0:1], ALU.pow).then_inc(sem("t_rstd"), 1)
                t = i + 2
                if live(t):
                    mean_root(1, t, par, ss1, ms1, r1, "d_nx")
                t = i + 3
                if live(t):
                    pool.wait_ge(sem("d_X0"), t + 1)
                    nc.gpsimd.tensor_tensor(O[:, t, :], O[:, t, :], gout1[:], ALU.mult).then_inc(sem("d_X"), 1)

            pool.wait_ge(sem("emptied"), 16)
            nc.gpsimd.iota(iota8[:], pattern=[[1, E]], base=0, channel_multiplier=0,
                           allow_small_or_imprecise_dtypes=True).then_inc(sem("d_iota"), 1)
            pool.wait_ge(sem("t_oev"), 2 * TILES)
            nc.gpsimd.iota(iota_rows[:], pattern=[[P, TILES]], base=0, channel_multiplier=0,
                           allow_small_or_imprecise_dtypes=True).then_inc(sem("d_iota"), 1)
            nc.gpsimd.iota(iota_tile[:], pattern=[[1, ROUTED]], base=0, channel_multiplier=0,
                           allow_small_or_imprecise_dtypes=True).then_inc(sem("d_iota"), 1)
            pipeline(pool, block_step, 4, 10)
            pool.wait_ge(sem("d_xfa"), TILES)
            pool.wait_ge(sem("emptied"), 16)
            for k in range(TOP_K):
                if k:
                    pool.wait_ge(sem("sorted"), 16 * TILES)
                nc.gpsimd.iota(xf_all[:, :, D].bitcast(I32), pattern=[[TOP_K * P, TILES]], base=k, channel_multiplier=TOP_K).then_inc(sem("r_ids"), 1)
                pool.wait_ge(sem("r_ids"), k + 1)
                pool.wait_ge(sem("r_pos"), k + 1)
                for t in range(TILES):
                    nc.gpsimd.indirect_dma_start(out=sorted_rows, out_offset=bass.IndirectOffsetOnAxis(ap=pos[k][:, t:t + 1], axis=0),
                                                 in_=xf_all[:, t, :], in_offset=None).then_inc(sem("sorted"), 16)

            def store_result(r, par):
                apart(pool, (sem("e_idx"), r + 1),
                            (sem("e_out"), TILES + r + 1))
                nc.gpsimd.indirect_dma_start(out=results, out_offset=bass.IndirectOffsetOnAxis(ap=idx[par][:], axis=0),
                                             in_=result[par][:], in_offset=None, bounds_check=SEQS * S * TOP_K - 1,
                                             oob_is_err=False).then_inc(sem(f"e_stored{par}"), 16)

            with pool.Fori(0, ROUTED // 2) as pair:
                store_result(2 * pair, 0)
                store_result(2 * pair + 1, 1)
            pool.wait_ge(sem("e_out"), TILES)
            for g in range(GROUPS):
                pool.wait_ge(sem("y_both"), g + 1)
                x = X[:, G4 * g:G4 * g + G4, :]
                nc.gpsimd.tensor_tensor(x, x, both[g][:, :, 1, :], ALU.add).then_inc(sem("y_acc"), 1)

        @block.scalar
        def _(act):
            def split_hi(L):
                n = L["n"]
                act.wait_ge(sem("l_loaded"), nth(L, "loaded", LOADED[n]))
                act.wait_ge(sem("l_wn"), nth(L, "wn", KD))
                for k in range(KD):
                    nc.scalar.activation(wkvn[0][:, k, :], raw_kvn[:, k, :], ACT.Copy, scale=gcol[:, k:k + 1]).then_inc(sem("l_whi"), 1)

            def split_q_hi(k):
                nc.scalar.activation(wq[0][:, k, :], raw_q[:, k, :], ACT.Copy, scale=gcol[:, k:k + 1]).then_inc(sem("l_whi"), 1)

            def split_out_hi():
                nc.scalar.activation(wout[0][:], raw_o[:], ACT.Copy).then_inc(sem("l_whi"), 1)

            def rel_silu(k):
                act.wait_ge(sem("rel_ln"), k + 1)
                nc.scalar.activation(r_h[:], r_h[:], ACT.Silu).then_inc(sem("rel_act"), 1)

            def rel_transposed(k):
                act.wait_ge(sem("rel_Tp"), k + 1)
                nc.scalar.activation(r_hT[:], psW[:, 0:D], ACT.Copy).then_inc(sem("rel_T"), 1)

            def attention(L, between):
                n = L["n"]
                done = L["done"]

                def step(i, par):
                    t = i - 1
                    if live(t):
                        act.wait_ge(sem("t_kTp"), done + t + 1)
                        reach(act, sem("t_sp"), done + t)
                        nc.scalar.activation(kT[:], psM[:, 0:P], ACT.Copy, scale=ksc[:, 0:1]).then_inc(sem("t_kT"), 1)
                    t = i - 3
                    if live(t):
                        act.wait_ge(sem("t_pTp"), done + t + 1)
                        reach(act, sem("t_pv"), done + t)
                        nc.scalar.activation(pT[:], psT[:].rearrange("p a (c q) -> p (a c) q", q=P), ACT.Copy).then_inc(sem("t_pT"), 1)
                    t = i
                    if live(t):
                        act.wait_ge(sem("t_kvp"), done + t + 1)
                        reach(act, sem("t_sn"), done + t)
                        nc.scalar.activation(kvs[:], psM[:, 0:KVN], ACT.Copy).then_inc(sem("t_kvs"), 1)
                        if L["cosine"]:
                            act.wait_ge(sem("t_kvs"), done + t + 1)
                            reach(act, sem("t_kmx"), done + t)
                            nc.scalar.activation(junk[:], kvs[:, 0:DH], ACT.Square, accum_out=qss[:, H:H + 1]).then_inc(sem("t_kss"), 1)
                    t = i - 2
                    if live(t):
                        act.wait_ge(sem("t_sub"), done + t + 1)
                        nc.scalar.activation(ex[:], ex[:], ACT.Exp).then_inc(sem("t_ex"), 1)
                    t = i - 3
                    if live(t):
                        reach(act, sem("t_wo"), done + t)
                        for half, pv, ohi in ((0, "t_pv0", "t_ohi0"), (1, "t_pv", "t_ohi")):
                            act.wait_ge(sem(pv), done + t + 1)
                            nc.scalar.activation(oT[0][:, CH // 2 * half:CH // 2 * (half + 1), :],
                                                 psS[:, half, :].rearrange("p (c q) -> p c q", q=P), ACT.Identity,
                                                 bias=nvcol[:, 0:1]).then_inc(sem(ohi), 1)
                    t = i - 1
                    if live(t):
                        act.wait_ge(sem("t_qTp"), done + t + 1)
                        nc.scalar.activation(qT[:], psT[:].rearrange("p a (c q) -> p (a c) q", q=P), ACT.Copy).then_inc(sem("t_qT"), 1)
                    t = i + 1
                    if live(t):
                        act.wait_ge(sem("t_xTp"), done + t + 1)
                        nc.scalar.activation(xT[0][:], psM[:, 0:D].rearrange("p (k q) -> p k q", q=P), ACT.Copy).then_inc(sem("t_xhi"), 1)
                    t = i
                    if live(t):
                        act.wait_ge(sem("t_qp"), done + t + 1)
                        nc.scalar.activation(qn[:], psQ[:].rearrange("p a n -> p (a n)"), ACT.Copy).then_inc(sem("t_qn"), 1)
                        if L["cosine"]:
                            act.wait_ge(sem("t_qn"), done + t + 1)
                            reach(act, sem("t_ssq"), done + t)
                            nc.scalar.activation(sq[:], qn[:], ACT.Square).then_inc(sem("t_sq"), 1)
                    t = i - 3
                    if live(t):
                        act.wait_ge(sem("t_wo"), done + t + 1)
                        nc.scalar.activation(O[:, t, :], psW[:, 0:D], ACT.Copy).then_inc(sem("t_oev"), 1)

                pipeline(act, step, 2, 3, between)

            split_hi(LAYERS[0])
            for k in range(KD):
                split_q_hi(k)
            rel_silu(0)
            rel_transposed(0)

            def second_layer(i):
                if i == -1:
                    rel_silu(1)
                elif i == 0:
                    rel_transposed(1)
                    act.wait_ge(sem("rel_outp"), 1)
                    nc.scalar.activation(r_out[:], psW[0:H, 0:P], ACT.Identity, bias=r_b2[:, 0:1]).then_inc(sem("rel_out"), 1)
                    split_out_hi()
                elif i == TILES - 2:
                    act.wait_ge(sem("f_loaded"), 48)
                    for k in range(KD):
                        nc.scalar.activation(wfc[0][:, k, :], raw_q[:, k, :], ACT.Copy, scale=gout0[:, k:k + 1]).then_inc(sem("f_whi"), 1)
                    nc.scalar.activation(wpr[0][:], raw_o[:], ACT.Copy).then_inc(sem("f_whi"), 1)

            attention(LAYERS[0], second_layer)
            def ffn_in_hi(g):
                act.wait_ge(sem("f_cTp"), g + 1)
                nc.scalar.activation(cT[0][:], psT[:], ACT.Copy).then_inc(sem("f_chi"), 1)

            def ffn_relu(s, f):
                act.wait_ge(sem("f_up"), s + 1)
                reach(act, sem("f_lo"), s - 1)
                nc.scalar.activation(hf[f % 2][:], up_bank[f % 4], ACT.Relu).then_inc(sem("f_relu"), 1)

            def ffn_hi(s, par):
                act.wait_ge(sem("f_relu"), s + 1)
                nc.scalar.activation(hf[par][:], hf[par][:], ACT.Square).then_inc(sem("f_h"), 1)
                act.wait_ge(sem("f_h"), s + 1)
                reach(act, sem("f_dn"), s - 1)
                nc.scalar.activation(hT[par][0][:], hf[par][:], ACT.Copy).then_inc(sem("f_hi"), 1)

            def ffn_out(g):
                act.wait_ge(sem("f_dn"), FC * g + FC)
                reach(act, sem("f_lif"), 13 * g)
                nc.scalar.activation(cur[:].rearrange("p (a n) -> p a n", a=2), psS[:], ACT.Copy).then_inc(sem("f_y"), 1)

            def ffn(g, first=False, last=False):
                for f in range(FC):
                    if f == FC - 1 and not last:
                        act.wait_ge(sem("f_up"), FC * g + FC)
                        ffn_in_hi(g + 1)
                    ffn_relu(FC * g + f, f)
                    ffn_hi(FC * g + f, f % 2)
                    if f == 0 and not first:
                        ffn_out(g - 1)
                    if last and f == 2:
                        split_hi(LAYERS[1])
                    elif last and f in (3, 4):
                        split_q_hi(f - 3)
                    elif last and f == 5:
                        split_out_hi()

            ffn_in_hi(0)
            ffn(0, first=True)
            ffn(1)
            with act.Fori(2, GROUPS - 1) as g:
                ffn(g)
            ffn(GROUPS - 1, last=True)
            ffn_out(GROUPS - 1)
            def block_weights(i):
                if i == TILES - 2:
                    act.wait_ge(sem("d_loaded"), 16 * 7)
                    for k in range(KD):
                        nc.scalar.activation(bqkv[0][:, k, :], raw_bqkv[:, k, :], ACT.Copy, scale=g1col[:, k:k + 1]).then_inc(sem("d_whi"), 1)
                    nc.scalar.activation(bwo[0][:], raw_bwo[:], ACT.Copy).then_inc(sem("d_whi"), 1)

            attention(LAYERS[1], block_weights)
            act.wait_ge(sem("t_oev"), 2 * TILES)

            def block_step(i, par):
                t = i + 2
                if live(t):
                    act.wait_ge(sem("d_X"), t + 1)
                    reach(act, sem("d_ms1"), t - 1)
                    reach(act, sem("d_ss1"), t)
                    nc.scalar.activation(sqj[0][:], O[:, t, :], ACT.Square, scale=float(D) ** -0.5, accum_out=ss1[par][:]).then_inc(sem("d_ss1"), 1)
                t = i - 5
                if live(t):
                    act.wait_ge(sem("t_pv"), BLK + t + 1)
                    reach(act, sem("t_wo"), BLK + t)
                    nc.scalar.activation(boT[0][:], psM[:, 0:D].rearrange("p (k q) -> p k q", q=P), ACT.Copy).then_inc(sem("t_ohi"), 1)
                t = i - 4
                if live(t):
                    act.wait_ge(sem("t_pTp"), BLK + t + 1)
                    reach(act, sem("t_pv"), BLK + t)
                    nc.scalar.activation(bpT[:], psT[:, 1, 0:D].rearrange("p (k q) -> p k q", q=P), ACT.Copy).then_inc(sem("t_pT"), 1)
                t = i - 9
                if live(t):
                    act.wait_ge(sem("d_xfTp"), t + 1)
                    reach(act, sem("d_lgp"), t)
                    nc.scalar.activation(xff[:], psQ[:, 0, D:2 * D].rearrange("p (k q) -> p k q", q=P), ACT.Copy).then_inc(sem("d_xff"), 1)
                t = i - 9
                if live(t):
                    nc.scalar.activation(xf_all[:, t, 0:D], xf[:], ACT.Copy).then_inc(sem("d_xfa"), 1)
                t = i - 3
                if live(t):
                    act.wait_ge(sem("t_sub"), BLK + t + 1)
                    nc.scalar.activation(be[:], be[:], ACT.Exp).then_inc(sem("t_ex"), 1)
                t = i - 2
                if live(t):
                    act.wait_ge(sem("t_qTp"), BLK + t + 1)
                    reach(act, sem("t_sp"), BLK + t)
                    nc.scalar.activation(bqT[:], psT[:, 0, 0:D].rearrange("p (k q) -> p k q", q=P), ACT.Copy).then_inc(sem("t_qT"), 1)
                    nc.scalar.activation(bkT[:], psT[:, 0, D:D + P], ACT.Copy, scale=float(DH) ** -0.5).then_inc(sem("t_kT"), 1)
                t = i - 1
                if live(t):
                    act.wait_ge(sem("t_qp"), BLK + t + 1)
                    reach(act, sem("t_qTp"), BLK + t)
                    nc.scalar.activation(bq[:], psQ[:, 1, 0:D], ACT.Copy).then_inc(sem("t_qn"), 1)
                    nc.scalar.activation(bk[:], psQ[:, 1, D:D + DH].unsqueeze(1).to_broadcast([P, 2, DH]), ACT.Copy).then_inc(sem("t_kn"), 1)
                    nc.scalar.activation(v_all[:, t, :], psQ[:, 1, D + DH:QKV], ACT.Copy).then_inc(sem("t_vp"), 1)
                t = i
                if live(t):
                    act.wait_ge(sem("t_xTp"), BLK + t + 1)
                    reach(act, sem("t_qp"), BLK + t)
                    nc.scalar.activation(nxT[0][:], psQ[:, 0, 0:D].rearrange("p (k q) -> p k q", q=P), ACT.Copy).then_inc(sem("t_xhi"), 1)

                t = i - 6
                if live(t):
                    act.wait_ge(sem("d_X1"), t + 1)
                    reach(act, sem("d_ms2"), t - 1)
                    reach(act, sem("d_ss2"), t)
                    nc.scalar.activation(sqj[1][:], O[:, t, :], ACT.Square, scale=float(D) ** -0.5, accum_out=ss2[par][:]).then_inc(sem("d_ss2"), 1)

            pipeline(act, block_step, 4, 10)
            def split_expert(n):
                if isinstance(n, int) and n == 1:
                    act.wait_ge(sem("e_first"), 2 * 48)
                if isinstance(n, int) and n == 3 or not isinstance(n, int):
                    act.wait_ge(sem("e_rest"), (EP - 2) * 48)
                slot = n % EP if isinstance(n, int) else n
                for k in range(KD):
                    w13 = slice(2 * k * D, 2 * k * D + 2 * D)
                    nc.scalar.activation(W[:, slot, 0, w13], raw_w[:, slot, 1, w13], ACT.Copy, scale=g2col[:, k:k + 1])
                nc.scalar.activation(W[:, slot, 0, 2 * KD * D:EW], raw_w[:, slot, 1, 2 * KD * D:EW], ACT.Copy).then_inc(sem("e_whi"), 1)

            def expert_step(i, m, shared=None):
                par = m % 2
                t = i - 2
                if kind(t, shared):
                    act.wait_ge(sem("e_up"), t + 1)
                    reach(act, sem("e_h"), t)
                    nc.scalar.activation(sg[:], psQ[:, par, 0:D], ACT.Silu).then_inc(sem("e_sg"), 1)
                t = i
                if kind(t, shared):
                    act.wait_ge(sem("e_xTp"), t + 1)
                    reach(act, sem("e_up"), t - 1)
                    nc.scalar.activation(exT[par][0][:], psM[:, 0:D].rearrange("p (k q) -> p k q", q=P), ACT.Copy).then_inc(sem("e_xhi"), 1)
                t = i - 4
                if kind(t, shared) == "routed":
                    act.wait_ge(sem("e_dn"), t + 1)
                    reach(act, sem(f"e_stored{par}"), stored(t - TILES, par))
                    nc.scalar.activation(result[par][:], psW[:, 0:D], ACT.Copy).then_inc(sem("e_out"), 1)
                t = i - 3
                if kind(t, shared):
                    act.wait_ge(sem("e_hTp"), t + 1)
                    reach(act, sem("e_dn"), t)
                    nc.scalar.activation(ehT[0][:], psT[:, 0, 0:D].rearrange("p (k q) -> p k q", q=P), ACT.Copy).then_inc(sem("e_hhi"), 1)

            act.wait_ge(sem("d_xfa"), TILES)
            act.wait_ge(sem("d_R"), TILES)
            split_expert(1)
            act.wait_ge(sem("r_exp_in"), 1)
            nc.scalar.activation(rt[0][:], rt[0][:], ACT.Exp).then_inc(sem("r_exp"), 1)
            act.wait_ge(sem("r_exp_in"), 2)
            nc.scalar.activation(rc[4][:], rc[4][:], ACT.Exp).then_inc(sem("r_exp"), 1)
            split_expert(2)
            expert_steps(act, expert_step, split_expert)
            for g in range(GROUPS):
                act.wait_ge(sem(f"y_in{YS[g]}"), 16 * YS.count(YS[g]))
                for j in range(G4):
                    t = G4 * g + j
                    ins = nc.scalar.activation(both[g][:, j, 1, :], both[g][:, j, 1, :], ACT.Copy, scale=top_w[1][:, t:t + 1])
                ins.then_inc(sem("y_second"), 1)

        @block.vector
        def _(dve):
            def null_key(L):
                n = L["n"]
                dve.wait_ge(sem("l_loaded"), nth(L, "loaded", LOADED[n]))
                nk = sem("l_nk")
                if L["cosine"]:
                    nc.vector.tensor_tensor(junk[:], nkb[:], nkb[:], ALU.mult).then_inc(nk, 1)
                    nc.vector.tensor_tensor(qsrow[:], qsrow[:], ksrow[:], ALU.mult).then_inc(nk, 1)
                    nc.vector.tensor_tensor(ksc[:], ksc[:], qsc[:], ALU.mult).then_inc(nk, 1)
                    dve.wait_ge(nk, nth(L, "nk", 3))
                    nc.vector.tensor_reduce(tiny[:, 0:1], junk[:], AX.X, ALU.add).then_inc(nk, 1)
                    nc.vector.tensor_scalar(ksc[:], ksc[:], float(DH) ** 0.5, None, ALU.mult)
                    dve.wait_ge(nk, nth(L, "nk", 4))
                    nc.vector.tensor_scalar(tiny[:, 1:2], tiny[:, 0:1], 1e-24, None, ALU.max).then_inc(sem("nk_ss"), 1)
                    dve.wait_ge(sem("nk_r"), 1)
                    nc.vector.tensor_scalar(nkb[:], nkb[:], tiny[:, 2:3], float(DH) ** 0.5, ALU.mult, ALU.mult).then_inc(nk, 1)
                    dve.wait_ge(nk, nth(L, "nk", 5))
                    nc.vector.tensor_tensor(nkb[:], nkb[:], qsrow[:], ALU.mult).then_inc(nk, 1)
                    dve.wait_ge(nk, nth(L, "nk", 6))
                else:
                    nc.vector.tensor_scalar(nkb[:], nkb[:], float(DH) ** -0.5, None, ALU.mult).then_inc(nk, 1)
                    nc.vector.memset(ksc[:], float(DH) ** -0.5)
                    dve.wait_ge(nk, nth(L, "nk", 1))
                for k in range(KD):
                    prod = wn_tmp[:]
                    if k:
                        dve.wait_ge(sem("l_wn"), nth(L, "wn", k))
                    nc.vector.tensor_tensor(prod, raw_q[:, k, :].rearrange("p (h d) -> p h d", h=H),
                                            nkb[:].unsqueeze(1).to_broadcast([P, H, DH]), ALU.mult).then_inc(sem("l_wnp"), 1)
                    dve.wait_ge(sem("l_wnp"), nth(L, "wnp", k + 1))
                    nc.vector.tensor_reduce(raw_kvn[:, k, 2 * DH:KVN], prod, AX.X, ALU.add).then_inc(sem("l_wn"), 1)

            def split_lo(L):
                n = L["n"]
                lo = sem("l_wlo")
                for k in range(KD):
                    dve.wait_ge(sem("l_whi"), nth(L, "whi", k + 1))
                    nc.vector.scalar_tensor_tensor(wkvn[1][:, k, :], raw_kvn[:, k, :], gcol[:, k:k + 1],
                                                   wkvn[0][:, k, :].bitcast(F32), ALU.mult, ALU.subtract).then_inc(lo, 1)
                for k in range(KD):
                    dve.wait_ge(sem("l_whi"), nth(L, "whi", KD + k + 1))
                    nc.vector.scalar_tensor_tensor(wq[1][:, k, :], raw_q[:, k, :], gcol[:, k:k + 1],
                                                   wq[0][:, k, :].bitcast(F32), ALU.mult, ALU.subtract).then_inc(lo, 1)

            def split_out_lo(L):
                dve.wait_ge(sem("l_whi"), nth(L, "whi", 2 * KD + 1))
                nc.vector.tensor_tensor(wout[1][:], raw_o[:], wout[0][:].bitcast(F32), ALU.subtract).then_inc(sem("l_wlo"), 1)

            def masks(L):
                nc.vector.tensor_scalar(negmask[:], mask_w[:].bitcast(U8), -1.0, -NEG, ALU.add, ALU.mult).then_inc(sem("l_mask"), 1)

            def rel_norm(k, src):
                c = sem("rel_chain")
                nc.vector.bn_stats(r_st[:], src).then_inc(c, 1)
                dve.wait_ge(c, 4 * k + 2)
                nc.vector.bn_aggr(r_mv[:], r_st[:]).then_inc(sem("rel_mv"), 1)
                dve.wait_ge(sem("rel_rstd"), 2 * k + 2)
                nc.vector.tensor_scalar(r_h[:], src, r_mv[:, 0:1], r_rs[:, 1:2], ALU.subtract, ALU.mult).then_inc(c, 1)
                dve.wait_ge(c, 4 * k + 3)
                nc.vector.tensor_tensor(r_h[:], r_h[:], r_rows[f"g{k}"][:], ALU.mult).then_inc(sem("rel_ln"), 1)

            def attention(L, start, between):
                n = L["n"]
                done = L["done"]

                def step(i, par):
                    t = i - 2
                    if live(t):
                        dve.wait_ge(sem("t_sp"), done + t + 1)
                        dve.wait_ge(sem("t_bm"), done + t + 1)
                        reach(dve, sem("t_pn"), done + t)
                        keys = ex[:, :, 0:S]
                        keys4 = keys.rearrange("p (c a) j -> p c a j", a=2)
                        scores = psS[:].rearrange("p a (c j) -> p c a j", j=S)
                        nc.vector.tensor_tensor(keys4, scores, masked[:].rearrange("p (c a) j -> p c a j", a=2),
                                                ALU.add).then_inc(sem("t_left"), 1)
                        if L["cosine"]:
                            dve.wait_ge(sem("t_rq"), done + t + 1)
                            nc.vector.tensor_tensor(sn[par][:], sn[par][:], rq[par][:], ALU.mult).then_inc(sem("t_snr"), 1)
                            dve.wait_ge(sem("t_snr"), 2 * t + 1)
                            nc.vector.tensor_tensor(sn[par][:], sn[par][:], nbias[:], ALU.add).then_inc(sem("t_snr"), 1)
                            dve.wait_ge(sem("t_snr"), 2 * t + 2)
                        dve.wait_ge(sem("t_left"), done + t + 1)
                        nc.vector.tensor_reduce(m16[:], keys, AX.X, ALU.max).then_inc(sem("t_m0"), 1)
                        dve.wait_ge(sem("t_m0"), done + t + 1)
                        nc.vector.tensor_tensor(mm16[:], m16[:], sn[par][:], ALU.max).then_inc(sem("t_m1"), 1)
                        dve.wait_ge(sem("t_m1"), done + t + 1)
                        nc.vector.tensor_tensor(keys, keys, mm16[:].unsqueeze(2).to_broadcast([P, H, S]), ALU.subtract)
                        nc.vector.tensor_tensor(ex[:, :, S], sn[par][:], mm16[:], ALU.subtract).then_inc(sem("t_sub"), 1)
                    t = i
                    if live(t) and L["cosine"]:
                        dve.wait_ge(sem("t_kss"), done + t + 1)
                        reach(dve, sem("t_rk"), done + t)
                        nc.vector.tensor_scalar(qmx[:, H:H + 1], qss[:, H:H + 1], 1e-24, None, ALU.max).then_inc(sem("t_kmx"), 1)
                    t = i
                    if live(t):
                        dve.wait_ge(sem("t_kvs"), done + t + 1)
                        reach(dve, sem(f"t_vv{par}"), 32 * done + spread(t - 2, par))
                        nc.vector.tensor_tensor(vp[par][:], kvs[:, DH:2 * DH], nvb[:], ALU.subtract).then_inc(sem("t_vp"), 1)
                    t = i + 1
                    if live(t):
                        dve.wait_ge(sem("t_rstd"), done + t + 1)
                        reach(dve, sem("t_xTp"), done + t)
                        q = (par + 1) % 2
                        nc.vector.tensor_scalar(xn[:], X[:, t, :], mv[q][:, 0:1], rstd[q][:, 0:1], ALU.subtract,
                                                ALU.mult).then_inc(sem("t_xn"), 1)
                    t = i + 2
                    if live(t):
                        start(t)
                        reach(dve, sem("t_mv"), done + t)
                        nc.vector.bn_stats(st6[:], X[:, t, :]).then_inc(sem("t_st"), 1)
                    t = i - 2
                    if live(t):
                        dve.wait_ge(sem("t_ex"), done + t + 1)
                        nc.vector.tensor_reduce(den[:], ex[:], AX.X, ALU.add).then_inc(sem("t_den"), 1)
                        dve.wait_ge(sem("t_den"), done + t + 1)
                        nc.vector.reciprocal(rden[:], den[:]).then_inc(sem("t_rden"), 1)
                    t = i + 2
                    if live(t):
                        apart(dve, (sem("t_st"), done + t + 1))
                        nc.vector.bn_aggr(mv[par][:], st6[:]).then_inc(sem("t_mv"), 1)
                    t = i - 3
                    if live(t):
                        dve.wait_ge(sem("t_ohi"), done + t + 1)
                        nc.vector.scalar_tensor_tensor(oT[1][:], psS[:].rearrange("p a (c q) -> p (a c) q", q=P), nvcol[:, 0:1],
                                                       oT[0][:].bitcast(F32), ALU.add, ALU.subtract).then_inc(sem("t_olo"), 1)
                    t = i + 1
                    if live(t):
                        dve.wait_ge(sem("t_xhi"), done + t + 1)
                        nc.vector.tensor_tensor(xT[1][:], psM[:, 0:D].rearrange("p (k q) -> p k q", q=P),
                                                xT[0][:].bitcast(F32), ALU.subtract).then_inc(sem("t_xlo"), 1)
                    t = i
                    if live(t):
                        reach(dve, sem("t_kTp"), done + t)
                        if L["cosine"]:
                            dve.wait_ge(sem("t_rk"), done + t + 1)
                            nc.vector.tensor_scalar(kn[:], kvs[:, 0:DH].unsqueeze(1).to_broadcast([P, 2, DH]), rk[:, 0:1],
                                                    None, ALU.mult).then_inc(sem("t_kn"), 1)
                            reach(dve, sem("t_sub"), done + t - 1)
                            nc.vector.tensor_copy(sn[par][:], kvs[:, 2 * DH:KVN]).then_inc(sem("t_sn"), 1)
                            dve.wait_ge(sem("t_sq"), done + t + 1)
                            nc.vector.tensor_reduce(qss[:, 0:H], sq[:].rearrange("p (h d) -> p h d", h=H), AX.X,
                                                    ALU.add).then_inc(sem("t_ssq"), 1)
                            dve.wait_ge(sem("t_ssq"), done + t + 1)
                            reach(dve, sem("t_rq"), done + t)
                            nc.vector.tensor_scalar(qmx[:, 0:H], qss[:, 0:H], 1e-24, None, ALU.max).then_inc(sem("t_qmx"), 1)
                        else:
                            nc.vector.tensor_copy(kn[:], kvs[:, 0:DH].unsqueeze(1).to_broadcast([P, 2, DH])).then_inc(sem("t_kn"), 1)
                            reach(dve, sem("t_sub"), done + t - 1)
                            nc.vector.tensor_tensor(sn[par][:], kvs[:, 2 * DH:KVN], nbias[:], ALU.add).then_inc(sem("t_sn"), 1)

                pipeline(dve, step, 2, 3, between)

            dve.wait_ge(sem("const_pool"), CONSTANTS)
            null_key(LAYERS[0])
            dve.wait_ge(sem("rel_loaded"), 16 * 8)
            nc.vector.scalar_tensor_tensor(r_h[:], r_rows["w0"][:], r_pos[:, 0:1], r_rows["b0"][:], ALU.mult,
                                           ALU.add).then_inc(sem("rel_chain"), 1)
            dve.wait_ge(sem("rel_chain"), 1)
            rel_norm(0, r_h[:])
            split_lo(LAYERS[0])

            def second_layer(i):
                if i == -1:
                    dve.wait_ge(sem("rel_mm"), 1)
                    nc.vector.tensor_tensor(r_h[:], psS[:, 0, 0:D], r_rows["b1"][:], ALU.add).then_inc(sem("rel_chain"), 2)
                    dve.wait_ge(sem("rel_chain"), 5)
                    rel_norm(1, r_h[:])
                    masks(LAYERS[0])
                elif i == 1:
                    split_out_lo(LAYERS[0])
                elif i == TILES - 2:
                    for k in range(KD):
                        dve.wait_ge(sem("f_whi"), k + 1)
                        nc.vector.scalar_tensor_tensor(wfc[1][:, k, :], raw_q[:, k, :], gout0[:, k:k + 1], wfc[0][:, k, :].bitcast(F32),
                                                       ALU.mult, ALU.subtract).then_inc(sem("f_wlo"), 1)
                elif i == TILES + 1:
                    dve.wait_ge(sem("f_whi"), KD + 1)
                    nc.vector.tensor_tensor(wpr[1][:], raw_o[:], wpr[0][:].bitcast(F32), ALU.subtract).then_inc(sem("f_wlo"), 1)

            def x_there(t):
                if isinstance(t, int) and t < 4:
                    dve.wait_ge(sem("x_in0"), 16)
                else:
                    dve.wait_ge(sem("x_in1"), 16)

            attention(LAYERS[0], x_there, second_layer)
            def ffn_stats(g):
                for j in range(G4):
                    reach(dve, sem("f_mv"), G4 * g)
                    nc.vector.bn_stats(fst6[:, j, :], O[:, G4 * g + j, :]).then_inc(sem("f_st"), 1)
                for j in range(G4):
                    apart(dve, (sem("f_st"), G4 * g + j + 1),
                               (sem("f_c0"), g))
                    nc.vector.bn_aggr(fmv[:, j, :], fst6[:, j, :]).then_inc(sem("f_mv"), 1)

            def ffn_normalise(g):
                dve.wait_ge(sem("f_rs"), g + 1)
                reach(dve, sem("f_cTp"), g)
                for j in range(G4):
                    ins = nc.vector.tensor_scalar(c0[:, j, :], O[:, G4 * g + j, :], fmv[:, j, 0:1], frs[:, j:j + 1],
                                                  ALU.subtract, ALU.mult)
                ins.then_inc(sem("f_c0"), 1)

            def ffn_in_lo(g):
                dve.wait_ge(sem("f_chi"), g + 1)
                nc.vector.tensor_tensor(cT[1][:], psT[:], cT[0][:].bitcast(F32), ALU.subtract).then_inc(sem("f_clo"), 1)

            def add_to_x(g):
                dve.wait_ge(sem("f_count"), 4 * g + 4)
                rows = X[:, bass.ts(g, G4), :]
                nc.vector.scalar_tensor_tensor(rows, count[:].rearrange("p (t d) -> p t d", d=D), 1.0 / LIF_STEPS, rows,
                                               ALU.mult, ALU.add).then_inc(sem("f_x1"), 1)

            def fire(g, n):
                done = sem("f_lif")
                reach(dve, done, 13 * g + n)
                if n == 0:
                    dve.wait_ge(sem("f_y"), g + 1)
                    reach(dve, sem("f_count"), 4 * g)
                kind, k = (2, 0) if n == 0 else ((n - 1) % 3, (n - 1) // 3 + 1)
                if kind == 2 and k >= 2:
                    dve.wait_ge(sem("f_count"), 4 * g + k - 1)
                if kind == 0:
                    src = cur if k == 1 else mem
                    ins = nc.vector.scalar_tensor_tensor(mem[:], src[:], LIF_BETA, cur[:], ALU.mult, ALU.add)
                elif kind == 1:
                    ins = nc.vector.tensor_tensor(mem[:], mem[:], spk[(k + 1) % 2][:], ALU.subtract)
                else:
                    src = cur if n == 0 else mem
                    ins = nc.vector.tensor_scalar(spk[k % 2][:], src[:], LIF_THRESHOLD, None, ALU.is_gt)
                ins.then_inc(done, 1)
                if kind == 2 and k > 0:
                    dve.wait_ge(done, 13 * g + n + 1)
                    if k == 1:
                        reach(dve, sem("f_x1"), g)
                        ins = nc.vector.tensor_tensor(count[:], spk[0][:], spk[1][:], ALU.add)
                    else:
                        dve.wait_ge(sem("f_count"), 4 * g + k - 1)
                        ins = nc.vector.tensor_tensor(count[:], count[:], spk[k % 2][:], ALU.add)
                    ins.then_inc(sem("f_count"), 1)

            def ffn(g, first=False, last=False):
                if not last:
                    ffn_stats(g + 1)
                else:
                    null_key(LAYERS[1])
                for f in range(FC):
                    if not last and f == 6:
                        ffn_in_lo(g + 1)
                    if not first:
                        for n in (2 * f, 2 * f + 1):
                            if n < 13:
                                fire(g - 1, n)
                    if not last and f == 2:
                        ffn_normalise(g + 1)
                    if last and f == 4:
                        split_lo(LAYERS[1])
                if not first:
                    add_to_x(g - 1)

            dve.wait_ge(sem("t_oev"), TILES)
            ffn_stats(0)
            ffn_normalise(0)
            ffn_in_lo(0)
            ffn(0, first=True)
            ffn(1)
            with dve.Fori(2, GROUPS - 1) as g:
                ffn(g)
            ffn(GROUPS - 1, last=True)
            split_out_lo(LAYERS[1])
            masks(LAYERS[1])
            dve.wait_ge(sem("f_dn"), FC * GROUPS)
            dve.wait_ge(sem("f_lo"), FC * GROUPS)

            def last_group(i):
                for n in {-1: range(0, 4), 0: range(4, 9), 1: range(9, 13)}.get(i, ()):
                    fire(GROUPS - 1, n)
                if i == 1:
                    add_to_x(GROUPS - 1)
                if i == TILES - 2:
                    for k in range(KD):
                        dve.wait_ge(sem("d_whi"), k + 1)
                        nc.vector.scalar_tensor_tensor(bqkv[1][:, k, :], raw_bqkv[:, k, :], g1col[:, k:k + 1], bqkv[0][:, k, :].bitcast(F32),
                                                       ALU.mult, ALU.subtract).then_inc(sem("d_wlo"), 1)
                    for k in range(KD):
                        nc.vector.tensor_scalar(bwr[:, k, :], bwr[:, k, :], g2col[:, k:k + 1], None, ALU.mult).then_inc(sem("d_wlo"), 1)
                    dve.wait_ge(sem("d_whi"), KD + 1)
                    nc.vector.tensor_tensor(bwo[1][:], raw_bwo[:], bwo[0][:].bitcast(F32), ALU.subtract).then_inc(sem("d_wlo"), 1)

            attention(LAYERS[1], lambda t: None, last_group)
            dve.wait_ge(sem("t_oev"), 2 * TILES)

            def block_step(i, par):
                other = (par + 1) % 2
                t = i - 1
                if live(t):
                    dve.wait_ge(sem("t_xhi"), BLK + t + 1)
                    nc.vector.tensor_tensor(nxT[1][:], psQ[:, 0, 0:D].rearrange("p (k q) -> p k q", q=P),
                                            nxT[0][:].bitcast(F32), ALU.subtract).then_inc(sem("t_xlo"), 1)
                t = i
                if live(t):
                    dve.wait_ge(sem("d_r1"), t + 1)
                    reach(dve, sem("t_xTp"), BLK + t)
                    nc.vector.tensor_scalar(nx[:], O[:, t, :], r1[par][:, 0:1], None, ALU.mult).then_inc(sem("d_nx"), 1)
                t = i + 4
                if live(t):
                    reach(dve, sem("t_mv"), BLK + t)
                    nc.vector.bn_stats(dst6[:], O[:, t, :]).then_inc(sem("t_st"), 1)
                t = i - 6
                if live(t):
                    dve.wait_ge(sem("t_wo"), BLK + t + 1)
                    nc.vector.tensor_tensor(O[:, t, :], psW[:, 0:D], O[:, t, :], ALU.add).then_inc(sem("d_X1"), 1)
                t = i + 4
                if live(t):
                    apart(dve, (sem("t_st"), BLK + t + 1))
                    nc.vector.bn_aggr(dmv[par][:], dst6[:]).then_inc(sem("t_mv"), 1)
                t = i - 5
                if live(t):
                    dve.wait_ge(sem("t_ohi"), BLK + t + 1)
                    nc.vector.tensor_tensor(boT[1][:], psM[:, 0:D].rearrange("p (k q) -> p k q", q=P),
                                            boT[0][:].bitcast(F32), ALU.subtract).then_inc(sem("t_olo"), 1)
                t = i - 3
                if live(t):
                    dve.wait_ge(sem("t_sp"), BLK + t + 1)
                    scores = psS[:, :, 0:CB * S].rearrange("p a (c j) -> p c a j", j=S)
                    nc.vector.tensor_reduce(bm[:].rearrange("p (c a) -> p c a", a=2), scores, AX.X, ALU.max).then_inc(sem("t_m0"), 1)
                    dve.wait_ge(sem("t_m0"), BLK + t + 1)
                    reach(dve, sem("t_pn"), BLK + t)
                    nc.vector.tensor_tensor(be[:].rearrange("p (c a) j -> p c a j", a=2), scores,
                                            bm[:].rearrange("p (c a) -> p c a", a=2).unsqueeze(3).to_broadcast([P, CB, 2, S]),
                                            ALU.subtract).then_inc(sem("t_sub"), 1)
                t = i + 3
                if live(t):
                    dve.wait_ge(sem("t_rstd"), BLK + t + 1)
                    nc.vector.tensor_scalar(O[:, t, :], O[:, t, :], dmv[other][:, 0:1], drs[other][:, 0:1], ALU.subtract,
                                            ALU.mult).then_inc(sem("d_X0"), 1)
                t = i - 8
                if live(t):
                    dve.wait_ge(sem("d_r2"), t + 1)
                    reach(dve, sem("d_xfTp"), t)
                    reach(dve, sem("d_xfa"), t)
                    nc.vector.tensor_scalar(xf[:], O[:, t, :], r2[par][:, 0:1], None, ALU.mult).then_inc(sem("d_xf"), 1)
                t = i - 10
                if live(t):
                    dve.wait_ge(sem("d_lgp"), t + 1)
                    nc.vector.tensor_tensor(logits[:, t, :], psW[:, D:D + E], ebias[:], ALU.add).then_inc(sem("d_lg"), 1)
                t = i - 3
                if live(t):
                    dve.wait_ge(sem("t_ex"), BLK + t + 1)
                    nc.vector.tensor_reduce(bden[:], be[:], AX.X, ALU.add).then_inc(sem("t_den"), 1)
                    dve.wait_ge(sem("t_den"), BLK + t + 1)
                    nc.vector.reciprocal(brd[:], bden[:]).then_inc(sem("t_rden"), 1)

            dve.wait_ge(sem("emptied"), 16)
            pipeline(dve, block_step, 4, 10)
            def split_expert(n):
                slot = n % EP if isinstance(n, int) else n
                dve.wait_ge(sem("e_whi"), n)
                for k in range(KD):
                    w13 = slice(2 * k * D, 2 * k * D + 2 * D)
                    nc.vector.scalar_tensor_tensor(W[:, slot, 1, w13], raw_w[:, slot, 1, w13], g2col[:, k:k + 1],
                                                   W[:, slot, 0, w13].bitcast(F32), ALU.mult, ALU.subtract)
                w2 = slice(2 * KD * D, EW)
                nc.vector.tensor_tensor(W[:, slot, 1, w2], raw_w[:, slot, 1, w2], W[:, slot, 0, w2].bitcast(F32),
                                        ALU.subtract).then_inc(sem("e_wlo"), 1)

            def route():
                c = sem("r_chain")
                done = 0

                def then(ins):
                    nonlocal done
                    done += 1
                    ins.then_inc(c, 1)
                    dve.wait_ge(c, done)

                wide = lambda v: v.unsqueeze(2).to_broadcast([P, TILES, E])
                index = iota8[:].unsqueeze(1).to_broadcast([P, TILES, E])
                dve.wait_ge(sem("d_lg"), TILES)
                dve.wait_ge(sem("d_R"), TILES)
                dve.wait_ge(sem("d_iota"), 3)
                then(nc.vector.tensor_reduce(rc[0][:], logits[:], AX.X, ALU.max))
                nc.vector.tensor_tensor(rt[0][:], logits[:], wide(rc[0][:]), ALU.subtract).then_inc(sem("r_exp_in"), 1)
                dve.wait_ge(sem("r_exp"), 1)
                then(nc.vector.tensor_reduce(rc[0][:], rt[0][:], AX.X, ALU.add))
                then(nc.vector.reciprocal(rc[1][:], rc[0][:]))
                then(nc.vector.tensor_tensor(rt[0][:], rt[0][:], wide(rc[1][:]), ALU.mult))
                for n in range(2):
                    then(nc.vector.tensor_reduce(rc[2 + n][:], rt[0][:], AX.X, ALU.max))
                    then(nc.vector.tensor_tensor(rt[3][:], rt[0][:], wide(rc[2 + n][:]), ALU.is_lt))
                    then(nc.vector.scalar_tensor_tensor(rt[3][:], rt[3][:], float(E), index, ALU.mult, ALU.add))
                    then(nc.vector.tensor_reduce(rc[0][:], rt[3][:], AX.X, ALU.min))
                    then(nc.vector.tensor_tensor(rt[1 + n][:], index, wide(rc[0][:]), ALU.is_equal))
                    if n == 0:
                        then(nc.vector.scalar_tensor_tensor(rt[0][:], rt[1][:], -2.0, rt[0][:], ALU.mult, ALU.add))
                nc.vector.tensor_tensor(rc[4][:], rc[3][:], rc[2][:], ALU.subtract).then_inc(sem("r_exp_in"), 1)
                then(nc.vector.tensor_tensor(chosen[:], rt[1][:], rt[2][:], ALU.add))
                nc.vector.tensor_copy(before[:], before_f[:]).then_inc(sem("r_chosen"), 1)
                dve.wait_ge(sem("r_exp"), 2)
                then(nc.vector.tensor_scalar(rc[0][:], rc[4][:], 1.0, None, ALU.add))
                then(nc.vector.reciprocal(top_w[0][:], rc[0][:]))
                then(nc.vector.tensor_tensor(top_w[1][:], rc[4][:], top_w[0][:], ALU.mult))
                dve.wait_ge(sem("r_ranked"), 1)
                in_tile, of_tile = (psS[:, b, 0:TILES * E].rearrange("p (t e) -> p t e", e=E) for b in range(2))
                then(nc.vector.tensor_copy(upto[0][:], of_tile))
                src, step = 0, 1
                while step < TILES:
                    nc.vector.tensor_copy(upto[1 - src][:, 0:step, :], upto[src][:, 0:step, :])
                    then(nc.vector.tensor_tensor(upto[1 - src][:, step:TILES, :], upto[src][:, step:TILES, :],
                                                 upto[src][:, 0:TILES - step, :], ALU.add))
                    src, step = 1 - src, 2 * step
                total = upto[src][:, TILES - 1, :]
                then(nc.vector.tensor_tensor(rt[0][:].rearrange("p t e -> p (t e)").rearrange("p (e n) -> p e n", e=E),
                                             total.unsqueeze(2).to_broadcast([P, E, TILES]),
                                             iota_rows[:].unsqueeze(1).to_broadcast([P, E, TILES]), ALU.is_gt))
                then(nc.vector.tensor_reduce(n_tiles[:], rt[0][:].rearrange("p t e -> p (t e)").rearrange("p (e n) -> p e n", e=E),
                                             AX.X, ALU.add))
                then(nc.vector.tensor_copy(end_tile[0][:], n_tiles[:]))
                e_src, step = 0, 1
                while step < E:
                    nc.vector.tensor_copy(end_tile[1 - e_src][:, 0:step], end_tile[e_src][:, 0:step])
                    then(nc.vector.tensor_tensor(end_tile[1 - e_src][:, step:E], end_tile[e_src][:, step:E],
                                                 end_tile[e_src][:, 0:E - step], ALU.add))
                    e_src, step = 1 - e_src, 2 * step
                ends = end_tile[e_src]
                then(nc.vector.tensor_tensor(n_tiles[:], ends[:], n_tiles[:], ALU.subtract))
                place_of = upto[1 - src]
                then(nc.vector.tensor_tensor(place_of[:], upto[src][:], of_tile, ALU.subtract))
                then(nc.vector.tensor_tensor(place_of[:], place_of[:], in_tile, ALU.add))
                then(nc.vector.scalar_tensor_tensor(place_of[:], n_tiles[:].unsqueeze(1).to_broadcast([P, TILES, E]), float(P),
                                                    place_of[:], ALU.mult, ALU.add))
                for k in range(TOP_K):
                    then(nc.vector.tensor_tensor(rt[1 + k][:], rt[1 + k][:], place_of[:], ALU.mult))
                    then(nc.vector.tensor_reduce(rc[k][:], rt[1 + k][:], AX.X, ALU.add))
                    nc.vector.tensor_copy(pos[k][:], rc[k][:]).then_inc(sem("r_pos"), 1)
                then(nc.vector.tensor_tensor(by_end[:], iota_tile[:].unsqueeze(2).to_broadcast([1, ROUTED, E]),
                                             ends[0:1, :].unsqueeze(1).to_broadcast([1, ROUTED, E]), ALU.is_ge))
                then(nc.vector.tensor_reduce(slot_f[0][:], by_end[:], AX.X, ALU.add))
                then(nc.vector.tensor_scalar(slot_f[1][:], slot_f[0][:], float(E - 1), -float(EP), ALU.is_ge, ALU.mult))
                then(nc.vector.scalar_tensor_tensor(slot_f[1][:], slot_f[0][:], float(SHARED_SLOT + 1), slot_f[1][:], ALU.add, ALU.add))
                nc.vector.tensor_scalar(slots[:], slot_f[1][:], float(2 * EW), None, ALU.mult).then_inc(sem("r_slots"), 1)

            def expert_step(i, m, shared=None):
                par = m % 2
                t = i - 2
                if kind(t, shared):
                    dve.wait_ge(sem("e_sg"), t + 1)
                    reach(dve, sem("e_hTp"), t - 1)
                    nc.vector.tensor_tensor(eh[par][:], sg[:], psQ[:, par, D:2 * D], ALU.mult).then_inc(sem("e_h"), 1)
                t = i
                if kind(t, shared):
                    dve.wait_ge(sem("e_xhi"), t + 1)
                    nc.vector.tensor_tensor(exT[par][1][:], psM[:, 0:D].rearrange("p (k q) -> p k q", q=P),
                                            exT[par][0][:].bitcast(F32), ALU.subtract).then_inc(sem("e_xlo"), 1)
                if kind(t, shared) == "routed":
                    r = t - TILES
                    dve.wait_ge(sem(f"e_rows{m // 2}"), loaded(t, m))
                    nc.vector.tensor_copy(ids[:, bass.ds(r, 1)], rows[:, m, D:ROW].bitcast(I32)).then_inc(sem("e_id"), 1)
                t = i - 4
                if kind(t, shared) == "shared":
                    dve.wait_ge(sem("e_dn"), t + 1)
                    nc.vector.tensor_tensor(X[:, t, :], psW[:, 0:D], X[:, t, :], ALU.add).then_inc(sem("e_out"), 1)
                elif kind(t, shared) == "routed":
                    r = t - TILES
                    dve.wait_ge(sem("e_id"), r + 1)
                    reach(dve, sem(f"e_stored{par}"), stored(r, par))
                    nc.vector.tensor_copy(idx[par][:], ids[:, bass.ds(r, 1)]).then_inc(sem("e_idx"), 1)
                t = i - 3
                if kind(t, shared):
                    dve.wait_ge(sem("e_hhi"), t + 1)
                    nc.vector.tensor_tensor(ehT[1][:], psT[:, 0, 0:D].rearrange("p (k q) -> p k q", q=P),
                                            ehT[0][:].bitcast(F32), ALU.subtract).then_inc(sem("e_hlo"), 1)

            route()
            split_expert(1)
            split_expert(2)
            expert_steps(dve, expert_step, split_expert)
            for g in range(GROUPS):
                dve.wait_ge(sem("y_second"), g + 1)
                for j in range(G4):
                    t = G4 * g + j
                    ins = nc.vector.scalar_tensor_tensor(both[g][:, j, 1, :], both[g][:, j, 0, :], top_w[0][:, t:t + 1],
                                                         both[g][:, j, 1, :], ALU.mult, ALU.add)
                ins.then_inc(sem("y_both"), 1)

        @block.tensor
        def _(pe):
            def attention(L, between):
                n = L["n"]
                done = L["done"]

                def step(i, par):
                    t = i - 1
                    if live(t):
                        pe.wait_ge(sem("t_kn"), done + t + 1)
                        if live(t + 1):
                            pe.wait_ge(sem("t_xlo"), done + t + 2)
                        nc.tensor.transpose(psM[:, 0:P], kn[:].rearrange("p a d -> p (a d)"), ident[:]).then_inc(sem("t_kTp"), 1)
                    t = i - 3
                    if live(t):
                        pe.wait_ge(sem("t_pn"), done + t + 1)
                        if live(t + 1):
                            pe.wait_ge(sem("t_qT"), done + t + 2)
                        for c in range(CH):
                            mm = nc.tensor.transpose(psT[:, c // 4, c % 4 * P:c % 4 * P + P],
                                                     pn[:, 2 * c:2 * c + 2, :].rearrange("p a j -> p (a j)"), ident[:])
                        mm.then_inc(sem("t_pTp"), 1)
                    t = i
                    if live(t):
                        pe.wait_ge(sem("t_xlo"), done + t + 1)
                        reach(pe, sem("t_kT"), done + t)
                        if isinstance(t, int) and t == 0:
                            pe.wait_ge(sem("l_wlo"), nth(L, "wlo", 2 * KD))
                        for k in range(KD):
                            for j, (u, w) in enumerate(PASSES):
                                mm = nc.tensor.matmul(psM[:, 0:KVN], xT[u][:, k, :], wkvn[w][:, k, :],
                                                      start=(k == 0 and j == 0), stop=(k == KD - 1 and j == 2))
                        mm.then_inc(sem("t_kvp"), 1)
                        reach(pe, sem("t_qn"), done + t)
                        for half in range(2):
                            for k in range(KD):
                                for j, (u, w) in enumerate(PASSES):
                                    if live(i - 3) and half == 1 and k == KD - 1 and j == 2:
                                        pe.wait_ge(sem("t_pT"), done + i - 2)
                                        pe.wait_ge(sem("t_left"), done + i - 1)
                                        pe.wait_ge(sem(f"t_vv{(par + 1) % 2}"), 32 * done + spread(i - 3, (par + 1) % 2))
                                    mm = nc.tensor.matmul(psQ[:, half, :], xT[u][:, k, :], wq[w][:, k, half * 512:half * 512 + 512],
                                                          start=(k == 0 and j == 0), stop=(k == KD - 1 and j == 2))
                        mm.then_inc(sem("t_qp"), 1)
                    t = i - 3
                    if live(t):
                        vpar = (par + 1) % 2
                        if not live(i):
                            pe.wait_ge(sem("t_pT"), done + t + 1)
                            pe.wait_ge(sem(f"t_vv{vpar}"), 32 * done + spread(t, vpar))
                            if live(t + 1):
                                pe.wait_ge(sem("t_left"), done + t + 2)
                        for c4 in range(2):
                            out4 = psS[:, c4, :].rearrange("p (c b q) -> p c b q", b=2, q=S)
                            for b in range(2):
                                for half in range(2):
                                    f = slice(half * S, half * S + S)
                                    mm = nc.tensor.matmul(out4[f, :, b, :], vv[vpar][f, b, :],
                                                          pT[f, 4 * c4:4 * c4 + 4, b * S:b * S + S],
                                                          start=(b == 0), stop=(b == 1), skip_group_check=True)
                            mm.then_inc(sem("t_pv" if c4 else "t_pv0"), 1)
                    t = i - 1
                    if live(t):
                        pe.wait_ge(sem("t_qs" if L["cosine"] else "t_qn"), done + t + 1)
                        reach(pe, sem("t_pT"), done + t - 1)
                        for c in range(CH):
                            mm = nc.tensor.transpose(psT[:, c // 4, c % 4 * P:c % 4 * P + P], qn[:, c * P:c * P + P], ident[:])
                        mm.then_inc(sem("t_qTp"), 1)
                    t = i + 1
                    if live(t):
                        pe.wait_ge(sem("t_xn"), done + t + 1)
                        reach(pe, sem("t_kvs"), done + t)
                        for k in range(KD):
                            mm = nc.tensor.transpose(psM[:, k * P:k * P + P], xn[:, k * P:k * P + P], ident[:])
                        mm.then_inc(sem("t_xTp"), 1)
                    t = i - 3
                    if live(t):
                        if isinstance(t, int) and t == 0:
                            pe.wait_ge(sem("l_wlo"), nth(L, "wlo", 2 * KD + 1))
                        pe.wait_ge(sem("t_ohi0"), done + t + 1)
                        reach(pe, sem("t_oev"), done + t)
                        for u in range(2):
                            if u:
                                pe.wait_ge(sem("t_olo"), done + t + 1)
                            for c in range(CH):
                                if not u and c == CH // 2:
                                    pe.wait_ge(sem("t_ohi"), done + t + 1)
                                for w in range(2 - u):
                                    mm = nc.tensor.matmul(psW[:, 0:D], oT[u][:, c, :], wout[w][:, c, :],
                                                          start=(u == 0 and c == 0 and w == 0), stop=(u == 1 and c == CH - 1))
                        mm.then_inc(sem("t_wo"), 1)
                    t = i - 1
                    if live(t):
                        reach(pe, sem("t_olo"), done + t - 1)
                        reach(pe, sem("t_left"), done + t)
                        pe.wait_ge(sem("t_kT"), done + t + 1)
                        apart(pe, (sem("t_qT"), done + t + 1))
                        for c in range(CH):
                            for half in range(2):
                                for b in range(2):
                                    f = slice(half * DH, half * DH + DH)
                                    q = slice(b * S, b * S + S)
                                    mm = nc.tensor.matmul(psS[q, half, c * S:c * S + S], qT[f, c, q], kT[f, q],
                                                          start=True, stop=True, skip_group_check=True)
                        mm.then_inc(sem("t_sp"), 1)

                pipeline(pe, step, 2, 3, between)

            pe.wait_ge(sem("const_pool"), CONSTANTS)

            def rel_layer(k):
                pe.wait_ge(sem("rel_act"), k + 1)
                for c in range(KD):
                    mm = nc.tensor.transpose(psW[:, c * P:c * P + P], r_h[:, c * P:c * P + P], ident[:])
                mm.then_inc(sem("rel_Tp"), 1)
                pe.wait_ge(sem("rel_T"), k + 1)
                if k == 0:
                    for c in range(KD):
                        mm = nc.tensor.matmul(psS[:, 0, 0:D], r_hT[:, c, :], r_w1[:, c, :], start=(c == 0), stop=(c == KD - 1))
                    mm.then_inc(sem("rel_mm"), 1)
                else:
                    for c in range(KD):
                        mm = nc.tensor.matmul(psW[0:H, 0:P], r_w2[:, c, :], r_hT[:, c, :], start=(c == 0), stop=(c == KD - 1))
                    mm.then_inc(sem("rel_outp"), 1)

            rel_layer(0)
            attention(LAYERS[0], lambda i: rel_layer(1) if i == 0 else None)
            def ffn_in(g):
                pe.wait_ge(sem("f_c0"), g + 1)
                reach(pe, sem("f_clo"), g)
                for k in range(KD):
                    for j in range(G4):
                        mm = nc.tensor.transpose(psT[:, k, j * P:j * P + P], c0[:, j, k * P:k * P + P], ident[:])
                mm.then_inc(sem("f_cTp"), 1)

            def ffn_up(g, f):
                s = FC * g + f
                if f % FC == 0:
                    pe.wait_ge(sem("f_clo"), g + f // FC + 1)
                reach(pe, sem("f_relu"), s - 3)
                for k in range(KD):
                    for j, (u, w) in enumerate(PASSES):
                        mm = nc.tensor.matmul(up_bank[f % 4], wfc[u][:, k, f % FC * P:f % FC * P + P], cT[w][:, k, :],
                                              start=(k == 0 and j == 0), stop=(k == KD - 1 and j == 2))
                mm.then_inc(sem("f_up"), 1)

            def ffn_down(g, f):
                s = FC * g + f
                pe.wait_ge(sem("f_lo"), s + 1)
                if f == 0:
                    reach(pe, sem("f_y"), g)
                for t in range(G4):
                    for j, (u, w) in enumerate(PASSES):
                        mm = nc.tensor.matmul(psS[:, t // 2, t % 2 * D:t % 2 * D + D], hT[f % 2][u][:, t * P:t * P + P], wpr[w][:, f, :],
                                              start=(f == 0 and j == 0 and t % 2 == 0), stop=(f == FC - 1 and j == 2),
                                              skip_group_check=True)
                mm.then_inc(sem("f_dn"), 1)

            def ffn(g, last=False):
                for f in range(FC - 2):
                    ffn_up(g, f + 2)
                    ffn_down(g, f)
                    if f == FC - 4 and not last:
                        ffn_in(g + 1)
                ffn_down(g, FC - 2)
                if not last:
                    ffn_up(g, FC)
                ffn_down(g, FC - 1)
                if not last:
                    ffn_up(g, FC + 1)

            pe.wait_ge(sem("f_wlo"), KD + 1)
            ffn_in(0)
            ffn_up(0, 0)
            ffn_up(0, 1)
            ffn(0)
            with pe.Fori(1, GROUPS - 1) as g:
                ffn(g)
            ffn(GROUPS - 1, last=True)
            pe.wait_ge(sem("f_relu"), FC * GROUPS)
            pe.wait_ge(sem("f_clo"), GROUPS)
            pe.wait_ge(sem("f_y"), GROUPS)
            attention(LAYERS[1], None)
            def block_step(i, par):
                t = i - 6
                if live(t):
                    pe.wait_ge(sem("t_olo"), BLK + t + 1)
                    reach(pe, sem("d_X1"), t)
                    if live(i - 11):
                        pe.wait_ge(sem("d_lg"), i - 10)
                    for c in range(CB):
                        for j, (u, w) in enumerate(PASSES):
                            mm = nc.tensor.matmul(psW[:, 0:D], boT[u][:, c, :], bwo[w][:, c, :],
                                                  start=(c == 0 and j == 0), stop=(c == CB - 1 and j == 2))
                    mm.then_inc(sem("t_wo"), 1)
                t = i - 5
                if live(t):
                    vpar = (par + 1) % 2
                    apart(pe, (sem("t_pT"), BLK + t + 1),
                              (sem(f"t_vv{vpar}"), 32 * BLK + spread(t, vpar)),
                              (sem("t_olo"), BLK + t))
                    o = psM[:, 0:D].rearrange("p (c b q) -> p c b q", b=2, q=S)
                    for b in range(2):
                        for half in range(2):
                            f = slice(half * S, half * S + S)
                            mm = nc.tensor.matmul(o[f, :, b, :], bvv[vpar][f, b, :], bpT[f, :, b * S:b * S + S],
                                                  start=True, stop=True, skip_group_check=True)
                    mm.then_inc(sem("t_pv"), 1)
                t = i - 3
                if live(t):
                    apart(pe, (sem("t_kT"), BLK + t + 1),
                              (sem("t_sub"), BLK + t))
                    for c in range(CB):
                        for half in range(2):
                            for b in range(2):
                                f = slice(half * DH, half * DH + DH)
                                q = slice(b * S, b * S + S)
                                mm = nc.tensor.matmul(psS[q, half, c * S:c * S + S], bqT[f, c, q], bkT[f, q],
                                                      start=True, stop=True, skip_group_check=True)
                    mm.then_inc(sem("t_sp"), 1)
                t = i - 4
                if live(t):
                    pe.wait_ge(sem("t_pn"), BLK + t + 1)
                    reach(pe, sem("t_pT"), BLK + t)
                    for c in range(CB):
                        mm = nc.tensor.transpose(psT[:, 1, c * P:c * P + P],
                                                 bpn[:, 2 * c:2 * c + 2, :].rearrange("p a j -> p (a j)"), ident[:])
                    mm.then_inc(sem("t_pTp"), 1)
                t = i - 9
                if live(t):
                    pe.wait_ge(sem("d_xf"), t + 1)
                    if live(i - 1):
                        pe.wait_ge(sem("t_xlo"), BLK + i)
                    reach(pe, sem("d_xff"), t)
                    for k in range(KD):
                        mm = nc.tensor.transpose(psQ[:, 0, D + k * P:D + k * P + P], xf[:, k * P:k * P + P], ident[:])
                    mm.then_inc(sem("d_xfTp"), 1)
                t = i - 10
                if live(t):
                    pe.wait_ge(sem("d_xff"), t + 1)
                    if live(i - 6):
                        pe.wait_ge(sem("d_X1"), i - 5)
                    reach(pe, sem("d_lg"), t)
                    for k in range(KD):
                        mm = nc.tensor.matmul(psW[:, D:D + E], xff[:, k, :], bwr[:, k, :], start=(k == 0), stop=(k == KD - 1))
                    mm.then_inc(sem("d_lgp"), 1)
                t = i - 2
                if live(t):
                    pe.wait_ge(sem("t_kn"), BLK + t + 1)
                    reach(pe, sem("t_kT"), BLK + t)
                    for c in range(CB):
                        nc.tensor.transpose(psT[:, 0, c * P:c * P + P], bq[:, c * P:c * P + P], ident[:])
                    nc.tensor.transpose(psT[:, 0, D:D + P], bk[:].rearrange("p a d -> p (a d)"), ident[:]).then_inc(sem("t_qTp"), 1)
                t = i - 1
                if live(t):
                    pe.wait_ge(sem("t_xlo"), BLK + t + 1)
                    reach(pe, sem("t_vp"), BLK + t)
                    for k in range(KD):
                        for j, (u, w) in enumerate(PASSES):
                            mm = nc.tensor.matmul(psQ[:, 1, 0:QKV], nxT[u][:, k, :], bqkv[w][:, k, :],
                                                  start=(k == 0 and j == 0), stop=(k == KD - 1 and j == 2))
                    mm.then_inc(sem("t_qp"), 1)
                t = i
                if live(t):
                    pe.wait_ge(sem("d_nx"), t + 1)
                    reach(pe, sem("t_xlo"), BLK + t)
                    if live(i - 9):
                        pe.wait_ge(sem("d_xff"), i - 8)
                    for k in range(KD):
                        mm = nc.tensor.transpose(psQ[:, 0, k * P:k * P + P], nx[:, k * P:k * P + P], ident[:])
                    mm.then_inc(sem("t_xTp"), 1)

            pe.wait_ge(sem("d_wlo"), 2 * KD + 1)
            pipeline(pe, block_step, 4, 10)
            weights_at = None
            weights = W[:].rearrange("p s w n -> p (s w n)")

            def offsets(t, n):
                return nc.values_load_multi_w_load_instructions(
                    slots[0:1, bass.ds(t - TILES, n)], engines=(mybir.EngineType.PE,), min_val=0, max_val=(EP - 1) * 2 * EW,
                    skip_runtime_bounds_check_because="they are worked out as one of nine places")[1]

            def expert_step(i, m, shared=None):
                other = (m + 1) % 2
                if isinstance(i, int) and i - 1 == TILES:
                    pe.wait_ge(sem("r_slots"), 1)
                if not isinstance(i, int) and not shared:
                    if m == 0:
                        nonlocal weights_at
                        weights_at = offsets(i - 4, 7)
                    w2_at, w13_at = weights_at[m], weights_at[m + 3]
                else:
                    w2_at, w13_at = (offsets(t, 1)[0] if kind(t, shared) == "routed" else SHARED_SLOT * 2 * EW for t in (i - 4, i - 1))
                t = i
                if kind(t, shared):
                    pe.wait_ge(sem(f"e_rows{m // 2}"), loaded(t, m))
                    reach(pe, sem("e_xlo"), t)
                    for k in range(KD):
                        mm = nc.tensor.transpose(psM[:, k * P:k * P + P], rows[:, m, k * P:k * P + P], ident[:])
                    mm.then_inc(sem("e_xTp"), 1)
                t = i - 4
                if kind(t, shared):
                    pe.wait_ge(sem("e_hlo"), t + 1)
                    reach(pe, sem("e_out"), t)
                    for c in range(KD):
                        for j, (u, w) in enumerate(PASSES):
                            mm = nc.tensor.matmul(psW[:, 0:D], ehT[u][:, c, :], weights[:, bass.ds(w2_at + w * EW + (2 * KD + c) * D, D)],
                                                  start=(c == 0 and j == 0), stop=(c == KD - 1 and j == 2))
                    mm.then_inc(sem("e_dn"), 1)
                t = i - 3
                if kind(t, shared):
                    pe.wait_ge(sem("e_h"), t + 1)
                    reach(pe, sem("e_hlo"), t)
                    for c in range(KD):
                        mm = nc.tensor.transpose(psT[:, 0, c * P:c * P + P], eh[other][:, c * P:c * P + P], ident[:])
                    mm.then_inc(sem("e_hTp"), 1)
                t = i - 1
                if kind(t, shared):
                    if isinstance(t, int) and t in (0, TILES):
                        pe.wait_ge(sem("e_wlo"), EP if t else 1)
                    pe.wait_ge(sem("e_xlo"), t + 1)
                    reach(pe, sem("e_h"), t - 1)
                    for k in range(KD):
                        for j, (u, w) in enumerate(PASSES):
                            mm = nc.tensor.matmul(psQ[:, other, :], exT[other][u][:, k, :], weights[:, bass.ds(w13_at + w * EW + 2 * k * D, 2 * D)],
                                                  start=(k == 0 and j == 0), stop=(k == KD - 1 and j == 2))
                    mm.then_inc(sem("e_up"), 1)

            pe.wait_ge(sem("r_chosen"), 1)
            for b, what in enumerate((before, ones)):
                mm = nc.tensor.matmul(psS[:, b, 0:TILES * E], what[:], chosen[:].rearrange("p t e -> p (t e)"), start=True, stop=True)
            mm.then_inc(sem("r_ranked"), 1)
            expert_steps(pe, expert_step)


def layout(inputs):
    c = np.ascontiguousarray
    i = {k: np.asarray(v) for k, v in inputs.items()}
    first = lambda name, s: c(np.concatenate([i[s][None], i[name]], axis=0).transpose(0, 2, 1))
    return {
        "x": c(i["x"].reshape(SEQS * S, D)), "null": c(i["cond_64"]), "fside": c(i["fside_16xSxS_0"]),
        "mask0": c(i["mask_BxS_bf1"]).view(np.int32), "mask1": c(i["mask_BxS_bk0"]).view(np.int32),
        "g_norm": c(i["L0_cond_g_norm"]), "Wq0": c(i["L0_cond_Wq"]), "Wkv0": c(i["L0_cond_Wkv"]),
        "q_scale": c(i["L0_cond_q_scale"]), "k_scale": c(i["L0_cond_k_scale"]), "nb0": c(i["L0_cond_null_attn_bias"]),
        "rw0": c(i["L0_cond_w0"].reshape(D)), "rb0": c(i["L0_cond_b0"]), "rg0": c(i["L0_cond_g0"]),
        "rw1": c(i["L0_cond_w1"]), "rb1": c(i["L0_cond_b1"]), "rg1": c(i["L0_cond_g1"]),
        "rw2": c(i["L0_cond_w2"]), "rb2": c(i["L0_cond_b2"]), "Wout0": c(i["L0_cond_Wout"]),
        "g_out0": c(i["L0_cond_g_out"]), "Wfc": c(i["L0_ffn_W_fc"].T), "Wproj": c(i["L0_ffn_W_proj"].T),
        "g_in": c(i["L1_cond_g_in"]), "nb1": c(i["L1_cond_null_attn_bias"]), "Wq1": c(i["L1_cond_Wq"]),
        "Wkv1": c(i["L1_cond_Wkv"]), "Wo1": c(i["L1_cond_Wo"]), "g_out1": c(i["L1_cond_g_out"]),
        "g1": c(i["L1_ffn_g1"]), "g2": c(i["L1_ffn_g2"]),
        "Wqkv": c(np.concatenate([i["L1_ffn_Wq"], i["L1_ffn_Wkc"], i["L1_ffn_Wvc"]], axis=0).T),
        "Wo": c(i["L1_ffn_Wo"].T), "Wr": c(i["L1_ffn_Wr"].T), "ebias": c(i["L1_ffn_expert_bias"]),
        "W1": first("L1_ffn_eW1", "L1_ffn_sW1"), "W2": first("L1_ffn_eW2", "L1_ffn_sW2"),
        "W3": first("L1_ffn_eW3", "L1_ffn_sW3"),
    }


def kernel(**inputs):
    import concourse.bacc as bacc
    from concourse.bass_utils import run_bass_kernel_spmd

    nc = bacc.Bacc("TRN2", target_bir_lowering=False, num_devices=1)
    arrays = layout(inputs)
    args = {n: nc.dram_tensor(n, v.shape, mybir.dt.from_np(v.dtype), kind="ExternalInput").ap() for n, v in arrays.items()}
    out = nc.dram_tensor("out", (SEQS * S, D), F32, kind="ExternalOutput").ap()
    build(nc, args, out)
    r = run_bass_kernel_spmd(nc, [arrays], core_ids=[0])
    return np.asarray(r.results[0]["out"]).reshape(SEQS, S, D)
```

```python
from contextlib import ExitStack

import concourse.bass as bass
import numpy as np
from concourse import mybir

F32 = mybir.dt.float32
F32R = mybir.dt.float32r
BF16 = mybir.dt.bfloat16
U8 = mybir.dt.uint8
I32 = mybir.dt.int32
ALU = mybir.AluOpType
ACT = mybir.ActivationFunctionType
AX = mybir.AxisListType

P = 128
SEQS, S, D = 64, 64, 256
TILES = SEQS * S // P
KD = D // P
H, DH = 16, 64
INNER = H * DH
CH = INNER // P
KVN = 2 * DH + H
FF = 4 * D
FC = FF // P
G4 = 4
GROUPS = TILES // G4
GT = G4 * P
HB = 4
CB = HB * DH // P
QKV = D + 2 * DH
E = 8
EP = E + 1
TOP_K = 2
ROUTED = TOP_K * TILES + E
SHARED_SLOT = 1
FIRST = TILES // 2
NOWHERE = 1 << 20
EW = 3 * KD * D
WHOLE = 1.5 * 2.0 ** 23
ORDER = (SHARED_SLOT, 2, 3, 4, 0, 5, 6, 7, 8)
NEG = -1e30
LIF_STEPS, LIF_BETA, LIF_THRESHOLD = 5, 0.9, 1.0

BLK = 2 * TILES

CONSTANTS = 10

PASSES = ((0, 0), (0, 1), (1, 0))


def reach(eng, sem, n):
    if not isinstance(n, int) or n > 0:
        eng.wait_ge(sem, n)


def spread(t, par):
    return 32 * (t - par) + 64


def live(t):
    return not isinstance(t, int) or 0 <= t < TILES


def pipeline(eng, body, ahead, behind, between=None):
    first, last = behind + 1, TILES - ahead
    first += first % 2
    last -= last % 2
    for i in range(-ahead, first):
        body(i, i % 2)
        if between:
            between(i)
    with eng.Fori(first // 2, last // 2) as pair:
        body(2 * pair, 0)
        body(2 * pair + 1, 1)
    for i in range(last, TILES + behind):
        body(i, i % 2)
        if between:
            between(i)


SPLIT_STEP = [-1] * 3 + [5 + n // 2 for n in range(12)] + [12 + 5 * n // 12 for n in range(12)]
SUM_STEP = tuple(TILES + ROUTED + n for n in (-4, -3, -2, 1, 2, 3))


def expert_steps(eng, step, first_half=None, other_half=None):
    end = FIRST + ROUTED
    for i in range(0, FIRST + 8):
        step(i, i % 4)
        if first_half:
            first_half(i)
    with eng.Fori((FIRST + 8) // 4, end // 4) as quad:
        for m in range(4):
            step(4 * quad + m, m, "routed")
    for i in range(end, TILES + ROUTED + 4):
        step(i, i % 4)
        if other_half:
            other_half(i)


def kind(t, what):
    if not isinstance(t, int):
        return what
    return "routed" if FIRST <= t < FIRST + ROUTED else "shared" if 0 <= t < TILES + ROUTED else None


def tokens(t):
    return t if isinstance(t, int) and t < FIRST else t - ROUTED


def loaded(r, m):
    return 4 * (r - m) + 16


def stored(r, par):
    return 8 * (r - par)


def build(nc, a, out):
    ctx = ExitStack()
    with ctx:
        base = -(-nc.sbuf_base // 64) * 64
        place = {}

        def region(name, nbytes, at=None):
            nonlocal base
            if at is None:
                at, base = base, base + nbytes
            place[name] = [at, at + nbytes]
            return at

        def sb(where, name, shape, dt):
            n = int(np.prod(shape[1:])) * (1 if dt == U8 else 2 if dt == BF16 else 4)
            at, end = place[where]
            place[where][0] = at + -(-n // 32) * 32
            assert place[where][0] <= end, (where, name, place[where][0] - end)
            return nc.alloc_sbuf_tensor_at(name, shape, dt, offset=at)

        K = 1024
        region("x", 32 * K)
        region("stage", 18 * K)
        region("bias", 4 * K)
        region("const", 12 * K)
        work = region("work", 41 * K)
        attw = region("attw", 35 * K)
        ffw = region("ffw", 32 * K)
        region("o", 32 * K)
        assert base <= 229344, base
        region("ffn_work", 41 * K, at=work)
        region("blk_w", 32 * K, at=ffw)
        region("xf_all", 41 * K, at=work)
        assert attw == work + 41 * K

        X = sb("x", "X", [P, TILES, D], F32)
        O = sb("o", "O", [P, TILES, D], F32)

        sems = {}

        def sem(name):
            if name not in sems:
                sems[name] = ctx.enter_context(nc.semaphore(name))
            return sems[name]

        def apart(eng, *waits):
            for signal, n in waits:
                reach(eng, signal, n)
                eng.sem_inc(sem("apart"), 1)

        psQ = ctx.enter_context(nc.psum_tensor("psQ", [P, 2, 512], F32))
        psS = ctx.enter_context(nc.psum_tensor("psS", [P, 2, 512], F32))
        psT = ctx.enter_context(nc.psum_tensor("psT", [P, 2, 512], F32))
        psW = ctx.enter_context(nc.psum_tensor("psW", [P, 512], F32))
        psM = ctx.enter_context(nc.psum_tensor("psM", [P, 512], F32))

        ident = sb("const", "ident", [P, P], F32)
        rms_eps = sb("const", "rms_eps", [P, 1], F32)
        ln_eps = sb("const", "ln_eps", [P, 1], F32)
        mhalf = sb("const", "mhalf", [P, 32], F32)
        route_at = place["const"][0]
        mask_w = sb("const", "mask_w", [P, TILES, S // 4], I32)
        negmask = sb("const", "negmask", [P, TILES, S], BF16)
        assert place["const"][0] >= route_at + 6 * K
        bias_t = sb("bias", "bias_t", [P, H, S], F32)
        region("masked", 4 * K, at=ffw + 28 * K)
        masked = sb("masked", "masked_bias", [P, H, S], F32)
        gcol = sb("const", "gcol", [P, KD], F32)
        nkb = sb("const", "nkb", [P, DH], F32)
        nvb = sb("const", "nvb", [P, DH], F32)
        nvcol = sb("const", "nvcol", [P, 1], F32)
        nbias = sb("const", "nbias", [P, H], F32)
        ksc = sb("const", "ksc", [P, 1], F32)
        qsc = sb("const", "qsc", [P, 1], F32)
        ksrow = sb("const", "ksrow", [P, DH], F32)
        qsrow = sb("const", "qsrow", [P, DH], F32)
        tiny = sb("const", "tiny", [P, 8], F32)

        wq = [sb("attw", f"wq{i}", [P, KD, INNER], F32R) for i in range(2)]
        wkvn = [sb("attw", f"wkvn{i}", [P, KD, KVN], F32R) for i in range(2)]
        wout = [sb("attw", f"wout{i}", [P, CH, D], F32R) for i in range(2)]
        st6 = sb("work", "st6", [P, 6], F32)
        mv = [sb("work", f"mv{i}", [P, 2], F32) for i in range(2)]
        vareps = sb("work", "vareps", [P, 1], F32)
        rstd = [sb("work", f"rstd{i}", [P, 1], F32) for i in range(2)]
        xn = sb("work", "xn", [P, D], F32)
        xT = [sb("work", f"xT{i}", [P, KD, P], F32R) for i in range(2)]
        kvs = sb("work", "kvs", [P, KVN], F32)
        junk = sb("work", "junk", [P, DH], F32)
        sq = sb("work", "sq", [P, INNER], F32)
        qss = sb("work", "qss", [P, H + 1], F32)
        qmx = sb("work", "qmx", [P, H + 1], F32)
        rq = [sb("work", f"rq{i}", [P, H], F32) for i in range(2)]
        rk = sb("work", "rk", [P, 1], F32)
        qn = sb("work", "qn", [P, INNER], F32)
        kn = sb("work", "kn", [P, 2, DH], F32)
        sn = [sb("work", f"sn{i}", [P, H], F32) for i in range(2)]
        vp = [sb("work", f"vp{i}", [P, DH], F32) for i in range(2)]
        vv = [sb("work", f"vv{i}", [P, 2, DH], F32) for i in range(2)]
        qT = sb("work", "qT", [P, CH, P], F32)
        kT = sb("work", "kT", [P, P], F32)
        m16 = sb("work", "m16", [P, H], F32)
        mm16 = sb("work", "mm16", [P, H], F32)
        ex = sb("work", "ex", [P, H, S + 1], F32)
        den = sb("work", "den", [P, H], F32)
        rden = sb("work", "rden", [P, H], F32)
        pn = sb("work", "pn", [P, H, S], F32)
        pT = sb("work", "pT", [P, CH, P], F32)
        oT = [sb("work", f"oT{i}", [P, CH, P], F32R) for i in range(2)]

        wfc = [sb("ffw", f"wfc{i}", [P, KD, FF], F32R) for i in range(2)]
        wpr = [sb("ffw", f"wpr{i}", [P, FC, D], F32R) for i in range(2)]
        gout0 = sb("const", "gout0", [P, KD], F32)
        c0 = sb("ffn_work", "c0", [P, G4, D], F32)
        cT = [sb("ffn_work", f"cT{i}", [P, KD, GT], F32R) for i in range(2)]
        hf = [sb("ffn_work", f"hf{i}", [P, GT], F32) for i in range(2)]
        hT = [[sb("ffn_work", f"hT{i}{j}", [P, GT], F32R) for j in range(2)] for i in range(2)]
        cur = sb("ffn_work", "cur", [P, G4 * D], F32)
        mem = sb("ffn_work", "mem", [P, G4 * D], F32)
        spk = [sb("ffn_work", f"spk{i}", [P, G4 * D], BF16) for i in range(2)]
        count = sb("ffn_work", "count", [P, G4 * D], BF16)
        up_bank = (psQ[:, 0, :], psQ[:, 1, :], psW[:], psM[:])
        fst6 = sb("ffn_work", "fst6", [P, G4, 6], F32)
        fmv = sb("ffn_work", "fmv", [P, G4, 2], F32)
        fve = sb("ffn_work", "fve", [P, G4], F32)
        frs = sb("ffn_work", "frs", [P, G4], F32)

        bqkv = [sb("blk_w", f"bqkv{i}", [P, KD, QKV], F32R) for i in range(2)]
        bwo = [sb("blk_w", f"bwo{i}", [P, KD, D], F32R) for i in range(2)]
        bwr = sb("blk_w", "bwr", [P, KD, E], F32)
        gout1 = sb("blk_w", "gout1", [P, D], F32)
        g1col = sb("blk_w", "g1col", [P, KD], F32)
        g2col = sb("const", "g2col", [P, KD], F32)
        ebias = sb("const", "ebias", [P, E], F32)
        dst6 = sb("blk_w", "dst6", [P, 6], F32)
        dmv = [sb("blk_w", f"dmv{i}", [P, 2], F32) for i in range(2)]
        dvar = sb("blk_w", "dvar", [P, 1], F32)
        drs = [sb("blk_w", f"drs{i}", [P, 1], F32) for i in range(2)]
        ss1 = [sb("blk_w", f"ss1{i}", [P, 1], F32) for i in range(2)]
        ms1 = sb("blk_w", "ms1", [P, 1], F32)
        r1 = [sb("blk_w", f"r1{i}", [P, 1], F32) for i in range(2)]
        ss2 = [sb("blk_w", f"ss2{i}", [P, 1], F32) for i in range(2)]
        ms2 = sb("blk_w", "ms2", [P, 1], F32)
        r2 = [sb("blk_w", f"r2{i}", [P, 1], F32) for i in range(2)]
        sqj = [sb("blk_w", f"sqj{i}", [P, D], F32) for i in range(2)]
        nx = sb("blk_w", "nx", [P, D], F32)
        nxT = [sb("blk_w", f"nxT{i}", [P, KD, P], F32R) for i in range(2)]
        bq = sb("blk_w", "bq", [P, D], F32)
        bk = sb("blk_w", "bk", [P, 2, DH], F32)
        bqT = sb("blk_w", "bqT", [P, CB, P], F32)
        bkT = sb("blk_w", "bkT", [P, P], F32)
        bm = sb("blk_w", "bm", [P, HB], F32)
        be = sb("blk_w", "be", [P, HB, S], F32)
        bden = sb("blk_w", "bden", [P, HB], F32)
        brd = sb("blk_w", "brd", [P, HB], F32)
        bpn = sb("blk_w", "bpn", [P, HB, S], F32)
        bpT = sb("blk_w", "bpT", [P, CB, P], F32)
        bvv = [sb("blk_w", f"bvv{i}", [P, 2, DH], F32) for i in range(2)]
        boT = [sb("blk_w", f"boT{i}", [P, CB, P], F32R) for i in range(2)]
        xf = sb("blk_w", "xf", [P, D], F32)
        xff = sb("blk_w", "xff", [P, KD, P], F32)
        xf_at = place["xf_all"][0]
        xf_all = sb("xf_all", "xf_all", [P, TILES, D], F32)
        w_at = place["xf_all"][0]
        W = nc.alloc_sbuf_tensor_at("W", [P, EP, 2, EW], F32R, offset=w_at)
        raw_w = nc.alloc_sbuf_tensor_at("raw_w", [P, EP, 2, EW], F32, offset=w_at)
        assert w_at + 12 * K * SHARED_SLOT >= attw and w_at + 12 * K * EP <= 229344
        v_all = sb("xf_all", "v_all", [P, TILES, DH], F32)

        logits_at = place["const"][0]
        logits = sb("const", "logits", [P, TILES, E], F32)
        iota8 = sb("const", "iota8", [P, E], F32)
        before_f = sb("const", "before_f", [P, P], F32)
        before = sb("const", "before", [P, P], BF16)
        ones = sb("const", "ones", [P, P], BF16)
        top_w = [sb("const", f"top_w{i}", [P, TILES], F32) for i in range(TOP_K)]
        slots = sb("const", "slots", [1, ROUTED], I32)
        region("route", 6 * K, at=route_at)
        region("route2", 4 * K, at=place["bias"][0] - 4 * K)
        rt = [sb("route2", f"rt{i}", [P, TILES, E], F32) for i in range(4)]
        rc = [sb("route", f"rc{i}", [P, TILES], F32) for i in range(5)]
        chosen = sb("route", "chosen", [P, TILES, E], BF16)
        upto = [sb("route", f"upto{i}", [P, TILES, E], F32) for i in range(2)]
        iota_rows = sb("route", "iota_rows", [P, TILES], F32)
        iota_tile = sb("route", "iota_tile", [P, ROUTED], F32)
        iota_row = sb("route", "iota_row", [P, P], F32)
        iota_part = sb("route", "iota_part", [P, 1], F32)
        number = sb("route", "number", [P, TOP_K * TILES], F32)
        pos = sb("route", "pos", [P, TOP_K, TILES], F32)
        pos_tile = sb("route", "pos_tile", [P, TOP_K * TILES], F32)
        pos_row = sb("route", "pos_row", [P, TOP_K * TILES], F32)
        hot_at = w_at + 5 * 12 * K
        hot_row = nc.alloc_sbuf_tensor_at("hot_row", [P, TOP_K * TILES, P], BF16, offset=hot_at)
        hot_tile, hot_part, hot_number = (nc.alloc_sbuf_tensor_at(f"hot_{n}", [P, TOP_K * TILES, ROUTED], BF16, offset=hot_at + 16 * K + 9216 * i)
                                          for i, n in enumerate(("tile", "part", "number")))
        n_tiles = sb("route", "n_tiles", [P, E], F32)
        end_tile = [sb("route", f"end_tile{i}", [P, E], F32) for i in range(2)]

        region("tile", 18 * K, at=place["stage"][0])
        rows = sb("tile", "rows", [P, 4, D], F32)
        exT = [[sb("tile", f"exT{i}{j}", [P, KD, P], F32R) for j in range(2)] for i in range(2)]
        sg = sb("tile", "sg", [P, D], F32)
        eh = [sb("tile", f"eh{i}", [P, D], F32) for i in range(2)]
        ehT = [sb("tile", f"ehT{j}", [P, KD, P], F32R) for j in range(2)]
        result = [sb("tile", f"result{i}", [P, D], F32) for i in range(2)]
        source = sb("const", "source", [P, ROUTED + 8], I32)
        target = sb("const", "target", [P, ROUTED], I32)
        src = [sb("tile", f"src{i}", [P, 1], I32) for i in range(4)]
        idx = [sb("tile", f"idx{i}", [P, 1], I32) for i in range(2)]
        by_end = sb("tile", "by_end", [1, ROUTED, E], F32)
        slot_f = [sb("route", f"slot_f{i}", [1, ROUTED], F32) for i in range(2)]
        YS = (0, 0, 0, 1, 1, 1, 2, 2)
        both = [nc.alloc_sbuf_tensor_at(f"both{i}", [P, G4, TOP_K, D], F32, offset=w_at + 24 * K + 8 * K * i) for i in range(GROUPS)]
        blank = nc.alloc_sbuf_tensor_at("blank", [1, D], F32, offset=logits_at)
        xf_dram = nc.dram_tensor("xf", (1 + SEQS * S, D), F32, kind="Internal").ap()
        results = nc.dram_tensor("results", (SEQS * S * TOP_K, D), F32, kind="Internal").ap()

        raw_q = nc.alloc_sbuf_tensor_at("raw_q", [P, KD, INNER], F32, offset=place["stage"][0])
        raw_kvn = nc.alloc_sbuf_tensor_at("raw_kvn", [P, KD, KVN], F32, offset=place["stage"][0] + 8 * K)
        raw_o = nc.alloc_sbuf_tensor_at("raw_o", [P, CH, D], F32, offset=place["stage"][0] + 8 * K + 1152)
        raw_bqkv = nc.alloc_sbuf_tensor_at("raw_bqkv", [P, KD, QKV], F32, offset=place["stage"][0])
        raw_bwo = nc.alloc_sbuf_tensor_at("raw_bwo", [P, KD, D], F32, offset=place["stage"][0] + 3 * K)
        rp = place["o"][1] - 32 * K
        NPOS = 2 * S - 1
        region("relpos", 32 * K, at=rp)
        r_w1 = sb("relpos", "r_w1", [P, KD, D], F32)
        r_w2 = sb("relpos", "r_w2", [P, KD, H], F32)
        r_rows = {n: sb("relpos", f"r_{n}", [P, D], F32) for n in ("w0", "b0", "g0", "b1", "g1")}
        r_b2 = sb("relpos", "r_b2", [H, 1], F32)
        r_pos = sb("relpos", "r_pos", [P, 1], F32)
        r_h = sb("relpos", "r_h", [P, D], F32)
        r_hT = sb("relpos", "r_hT", [P, KD, P], F32)
        r_st = sb("relpos", "r_st", [P, 6], F32)
        r_mv = sb("relpos", "r_mv", [P, 2], F32)
        r_rs = sb("relpos", "r_rs", [P, 2], F32)
        r_out = sb("relpos", "r_out", [H, P], F32)
        wn_tmp = sb("relpos", "wn_tmp", [P, H, DH], F32)
        rel_dram = nc.dram_tensor("rel_bias", (H, S, P), F32, kind="Internal").ap()

        x_dram = a["x"].rearrange("(t p) d -> p t d", p=P)
        out_dram = out.rearrange("(t p) d -> p t d", p=P)

        LAYERS = (
            dict(n="a", done=0, cosine=True, mask="mask0", g="g_norm", wq="Wq0", wkv="Wkv0", wo="Wout0", nb="nb0"),
            dict(n="c", done=TILES, cosine=False, mask="mask1", g="g_in", wq="Wq1", wkv="Wkv1", wo="Wo1", nb="nb1"),
        )

        LOADED = {"a": 16 * 17, "c": 16 * 11}
        COUNTS = dict(loaded=LOADED["a"], braw=32, causal=2, nk=6, wnp=KD, wn=KD, whi=2 * KD + 1,
                     wlo=2 * KD + 1, mask=1)

        def nth(L, name, n):
            return n + COUNTS[name] if L["done"] else n

        block = ctx.enter_context(nc.Block())

        @block.sync
        def _(sp):
            def load_layer(L):
                ld = sem("l_loaded")
                sp.dma_start(gcol[:], a[L["g"]].rearrange("(k p) -> p k", p=P), allow_slow_non_contiguous=True).then_inc(ld, 16)
                sp.dma_start(nkb[:], a["null"][0:1, :].to_broadcast([P, DH])).then_inc(ld, 16)
                sp.dma_start(nvb[:], a["null"][1:2, :].to_broadcast([P, DH])).then_inc(ld, 16)
                for half in range(2):
                    sp.dma_start(nvcol[half * DH:(half + 1) * DH, :], a["null"][1:2, :].rearrange("o d -> d o"),
                                 allow_slow_non_contiguous=True).then_inc(ld, 16)
                sp.dma_start(nbias[:], a[L["nb"]].rearrange("(o h) -> o h", o=1).to_broadcast([P, H])).then_inc(ld, 16)
                for b in range(2):
                    sp.dma_start(mask_w[b * S:(b + 1) * S, :, :], a[L["mask"]].rearrange("(t b) j -> b t j", b=2)[b:b + 1]
                                 .to_broadcast([S, TILES, S // 4])).then_inc(ld, 16)
                sp.dma_start(raw_q[:], a[L["wq"]].rearrange("(k p) n -> p k n", p=P)).then_inc(ld, 16)
                sp.dma_start(raw_kvn[:, :, 0:2 * DH], a[L["wkv"]].rearrange("(k p) n -> p k n", p=P)).then_inc(ld, 16)
                sp.dma_start(raw_o[:], a[L["wo"]].rearrange("(k p) n -> p k n", p=P)).then_inc(ld, 16)

            def load_ffn():
                sp.wait_ge(sem("l_wlo"), 2 * KD + 1)
                sp.dma_start(gout0[:], a["g_out0"].rearrange("(k p) -> p k", p=P), allow_slow_non_contiguous=True).then_inc(sem("f_loaded"), 16)
                sp.dma_start(raw_q[:], a["Wfc"].rearrange("(k p) n -> p k n", p=P)).then_inc(sem("f_loaded"), 16)
                sp.dma_start(raw_o[:], a["Wproj"].rearrange("(k p) n -> p k n", p=P)).then_inc(sem("f_loaded"), 16)

            def load_block():
                sp.wait_ge(sem("l_wlo"), nth(LAYERS[1], "wlo", 2 * KD + 1))
                ld = sem("d_loaded")
                for col, name in ((g1col, "g1"), (g2col, "g2")):
                    sp.dma_start(col[:], a[name].rearrange("(k p) -> p k", p=P), allow_slow_non_contiguous=True).then_inc(ld, 16)
                sp.dma_start(gout1[:], a["g_out1"].rearrange("(o d) -> o d", o=1).to_broadcast([P, D])).then_inc(ld, 16)
                sp.dma_start(ebias[:], a["ebias"].rearrange("(o e) -> o e", o=1).to_broadcast([P, E])).then_inc(ld, 16)
                sp.dma_start(raw_bqkv[:], a["Wqkv"].rearrange("(k p) n -> p k n", p=P)).then_inc(ld, 16)
                sp.dma_start(raw_bwo[:], a["Wo"].rearrange("(k p) n -> p k n", p=P)).then_inc(ld, 16)
                sp.dma_start(bwr[:], a["Wr"].rearrange("(k p) n -> p k n", p=P)).then_inc(ld, 16)

            def spread_v(L, before_loop):
                n = L["n"]
                done = L["done"]

                def step(t, par):
                    apart(sp, (sem("t_vp"), done + t + 1))
                    reach(sp, sem("t_pv"), done + t - 1)
                    for half in range(2):
                        for b in range(2):
                            sp.dma_start(vv[par][half * DH:(half + 1) * DH, b, :],
                                         vp[par][b * S:(b + 1) * S, :]).then_inc(sem(f"t_vv{par}"), 16)

                for t in range(2):
                    step(t, t)
                before_loop()
                with sp.Fori(1, TILES // 2) as pair:
                    step(2 * pair, 0)
                    step(2 * pair + 1, 1)

            sp.dma_start(X[:, 0:4, :], x_dram[:, 0:4, :]).then_inc(sem("x_in0"), 16)
            load_layer(LAYERS[0])
            for half in range(2):
                for row, name in ((ksc, "k_scale"), (qsc, "q_scale")):
                    sp.dma_start(row[half * DH:(half + 1) * DH, :], a[name].rearrange("(d o) -> d o", o=1),
                                 allow_slow_non_contiguous=True).then_inc(sem("l_loaded"), 16)
            for row, name in ((ksrow, "k_scale"), (qsrow, "q_scale")):
                sp.dma_start(row[:], a[name].rearrange("(o d) -> o d", o=1).to_broadcast([P, DH])).then_inc(sem("l_loaded"), 16)
            for name, key in (("w0", "rw0"), ("b0", "rb0"), ("g0", "rg0"), ("b1", "rb1"), ("g1", "rg1")):
                sp.dma_start(r_rows[name][:], a[key].rearrange("(o d) -> o d", o=1).to_broadcast([P, D])).then_inc(sem("rel_loaded"), 16)
            sp.dma_start(r_w1[:], a["rw1"].rearrange("(k p) n -> p k n", p=P)).then_inc(sem("rel_loaded"), 16)
            sp.dma_start(r_w2[:], a["rw2"].rearrange("(k p) n -> p k n", p=P)).then_inc(sem("rel_loaded"), 16)
            sp.dma_start(r_b2[:], a["rb2"].rearrange("(h o) -> h o", o=1), allow_slow_non_contiguous=True).then_inc(sem("rel_loaded"), 16)
            sp.dma_start(X[:, 4:TILES, :], x_dram[:, 4:TILES, :]).then_inc(sem("x_in1"), 16)
            sp.wait_ge(sem("rel_out"), 1)
            sp.dma_start(rel_dram, r_out[:].unsqueeze(1).to_broadcast([H, S, P])).then_inc(sem("rel_stored"), 16)
            sp.wait_ge(sem("rel_stored"), 16)
            for half in range(2):
                sp.dma_start(bias_t[half * S:(half + 1) * S, :, :],
                             bass.AP(rel_dram.tensor, S - 1, [[P - 1, S], [S * P, H], [1, S]])).then_inc(sem("l_braw"), 16)
            spread_v(LAYERS[0], before_loop=load_ffn)
            sp.wait_ge(sem("const_pool"), CONSTANTS)
            sp.dma_start(xf_dram[0:1, :], blank[:]).then_inc(sem("xf_stored"), 16)
            sp.wait_ge(sem("f_wlo"), KD + 1)
            sp.wait_ge(sem("t_oev"), TILES)
            load_layer(LAYERS[1])
            sp.wait_ge(sem("t_bm"), TILES)
            for half in range(2):
                sp.dma_start(bias_t[half * S:(half + 1) * S, :, :], a["fside"].rearrange("h i j -> i h j")).then_inc(sem("l_braw"), 16)
            spread_v(LAYERS[1], before_loop=load_block)
            def load_expert(p, slot, done):
                w13 = raw_w[:, slot, 1, 0:2 * KD * D].rearrange("p (k w n) -> p k w n", k=KD, w=2)
                for j, w in enumerate(("W1", "W3")):
                    sp.dma_start(w13[:, :, j, :], a[w][p].rearrange("(k p) n -> p k n", p=P)).then_inc(done, 16)
                sp.dma_start(raw_w[:, slot, 1, 2 * KD * D:EW].rearrange("p (k n) -> p k n", k=KD),
                             a["W2"][p].rearrange("(k p) n -> p k n", p=P)).then_inc(done, 16)

            sp.wait_ge(sem("t_oev"), 2 * TILES)
            for p in range(2):
                load_expert(p, SHARED_SLOT + p, sem("e_first"))

            def spread_block_v(t, par):
                apart(sp, (sem("t_vp"), BLK + t + 1))
                reach(sp, sem("t_pv"), BLK + t - 1)
                for half in range(2):
                    for b in range(2):
                        sp.dma_start(bvv[par][half * DH:(half + 1) * DH, b, :],
                                     v_all[b * S:(b + 1) * S, t, :]).then_inc(sem(f"t_vv{par}"), 16)

            for t in range(2):
                spread_block_v(t, t)
            with sp.Fori(1, TILES // 2) as pair:
                spread_block_v(2 * pair, 0)
                spread_block_v(2 * pair + 1, 1)
            for j in range(4):
                sp.wait_ge(sem("d_xfa"), 8 * j + 8)
                sp.dma_start(xf_dram[1:1 + SEQS * S, :].rearrange("(t p) d -> p t d", p=P)[:, 8 * j:8 * j + 8, :],
                             xf_all[:, 8 * j:8 * j + 8, :]).then_inc(sem("xf_stored"), 16)

            sp.wait_ge(sem("d_R"), TILES)
            sp.wait_ge(sem("d_lg"), TILES)
            sp.wait_ge(sem("d_xfa"), TILES)
            for p in (2, 3, EP - 1):
                load_expert(p, (p + 1) % EP, sem("e_rest"))
            sp.wait_ge(sem("r_ranked"), 2)
            for p in range(4, EP - 1):
                load_expert(p, p + 1, sem("e_last"))

            for par in range(2):
                sp.wait_ge(sem(f"e_stored{par}"), 16 * ROUTED // 2)
            for g in range(GROUPS):
                for k in range(TOP_K):
                    sp.dma_start(both[g][:, :, k, :], results.rearrange("(k g j p) d -> k g p j d", j=G4, p=P, k=TOP_K)[k, g]
                                 ).then_inc(sem(f"y_in{YS[g]}"), 16)
            for g in range(GROUPS):
                if g < len(SUM_STEP):
                    sp.wait_ge(sem("y_acc"), g + 1)
                else:
                    sp.wait_ge(sem("y_last"), g + 1 - len(SUM_STEP))
                sp.dma_start(out_dram[:, G4 * g:G4 * g + G4, :], X[:, G4 * g:G4 * g + G4, :]).then_inc(sem("stored"), 16)
            sp.wait_ge(sem("stored"), 16 * GROUPS)

        @block.gpsimd
        def _(pool):
            c = sem("const_pool")
            nc.gpsimd.memset(ident[:], 0.0).then_inc(c, 1)
            nc.gpsimd.memset(mhalf[:], -0.5).then_inc(c, 1)
            nc.gpsimd.memset(ln_eps[:], 1e-5).then_inc(c, 1)
            nc.gpsimd.memset(rms_eps[:], 1e-6).then_inc(c, 1)
            nc.gpsimd.iota(r_pos[:], pattern=[[0, 1]], base=S - 1, channel_multiplier=-1,
                           allow_small_or_imprecise_dtypes=True).then_inc(c, 1)
            nc.gpsimd.memset(before_f[:], 1.0).then_inc(c, 1)
            nc.gpsimd.memset(ones[:], 1.0).then_inc(c, 1)
            nc.gpsimd.memset(blank[:], 0.0).then_inc(c, 1)
            pool.wait_ge(c, 8)
            nc.gpsimd.affine_select(out=before_f[:], in_=before_f[:], compare_op=ALU.is_gt, fill=0.0, base=0,
                                    pattern=[[1, P]], channel_multiplier=-1).then_inc(c, 1)
            nc.gpsimd.affine_select(out=ident[:], in_=ident[:], compare_op=ALU.not_equal, fill=1.0, base=0,
                                    pattern=[[-1, P]], channel_multiplier=1).then_inc(c, 1)

            pool.wait_ge(sem("nk_ss"), 1)
            nc.gpsimd.tensor_tensor(tiny[:, 2:3], tiny[:, 1:2], mhalf[:, 0:1], ALU.pow).then_inc(sem("nk_r"), 1)
            def rel_rstd(k):
                pool.wait_ge(sem("rel_mv"), k + 1)
                nc.gpsimd.tensor_scalar(r_rs[:, 0:1], r_mv[:, 1:2], 1.0, 1e-5, ALU.mult, ALU.add).then_inc(sem("rel_rstd"), 1)
                pool.wait_ge(sem("rel_rstd"), 2 * k + 1)
                nc.gpsimd.tensor_tensor(r_rs[:, 1:2], r_rs[:, 0:1], mhalf[:, 0:1], ALU.pow).then_inc(sem("rel_rstd"), 1)

            def causal(L):
                pool.wait_ge(sem("l_braw"), nth(L, "braw", 32))
                pool.wait_ge(sem("t_rstd"), L["done"] + 3)
                if L["cosine"]:
                    pool.wait_ge(sem("t_rk"), 2)
                    pool.wait_ge(sem("t_rq"), 1)
                else:
                    pool.wait_ge(sem("f_lo"), FC * GROUPS)
                for half in range(2):
                    v = bias_t[half * S:(half + 1) * S, :, :]
                    nc.gpsimd.affine_select(out=v, in_=v, compare_op=ALU.is_ge, fill=NEG, base=0,
                                            pattern=[[0, H], [-1, S]], channel_multiplier=1).then_inc(sem("l_causal"), 1)
                pool.wait_ge(sem("l_causal"), nth(L, "causal", 2))

            rel_rstd(0)

            def attention(L, between):
                n = L["n"]
                done = L["done"]

                def step(i, par):
                    t = i - 2
                    if live(t):
                        pool.wait_ge(sem("t_rden"), done + t + 1)
                        reach(pool, sem("t_pTp"), done + t)
                        nc.gpsimd.tensor_tensor(pn[:], ex[:, :, 0:S], rden[:].unsqueeze(2).to_broadcast([P, H, S]),
                                                ALU.mult).then_inc(sem("t_pn"), 1)
                    t = i
                    if live(t) and L["cosine"]:
                        pool.wait_ge(sem("t_kmx"), done + t + 1)
                        reach(pool, sem("t_kn"), done + t)
                        nc.gpsimd.tensor_tensor(rk[:], qmx[:, H:H + 1], mhalf[:, 0:1], ALU.pow).then_inc(sem("t_rk"), 1)
                    t = i - 1
                    if live(t):
                        if isinstance(t, int) and t == 0:
                            causal(L)
                            pool.wait_ge(sem("l_mask"), nth(L, "mask", 1))
                        reach(pool, sem("t_m0"), done + t)
                        nc.gpsimd.tensor_tensor(masked[:], bias_t[:], negmask[:, bass.ds(t, 1), :].to_broadcast([P, H, S]),
                                                ALU.add).then_inc(sem("t_bm"), 1)
                    t = i + 2
                    if live(t):
                        pool.wait_ge(sem("t_mv"), done + t + 1)
                        reach(pool, sem("t_rstd"), done + t)
                        nc.gpsimd.tensor_tensor(vareps[:], mv[par][:, 1:2], ln_eps[:], ALU.add).then_inc(sem("t_ve"), 1)
                        pool.wait_ge(sem("t_ve"), done + t + 1)
                        reach(pool, sem("t_xn"), done + t - 1)
                        nc.gpsimd.tensor_tensor(rstd[par][:], vareps[:], mhalf[:, 0:1], ALU.pow).then_inc(sem("t_rstd"), 1)
                    t = i
                    if live(t) and L["cosine"]:
                        pool.wait_ge(sem("t_qmx"), done + t + 1)
                        reach(pool, sem("t_snr"), 2 * t - 2)
                        nc.gpsimd.tensor_tensor(rq[par][:], qmx[:, 0:H], mhalf[:, 0:H], ALU.pow).then_inc(sem("t_rq"), 1)
                        pool.wait_ge(sem("t_rq"), done + t + 1)
                        by_head = qn[:].rearrange("p (h d) -> p h d", h=H)
                        nc.gpsimd.tensor_tensor(by_head, by_head, rq[par][:].unsqueeze(2).to_broadcast([P, H, DH]),
                                                ALU.mult).then_inc(sem("t_qs"), 1)

                pipeline(pool, step, 2, 3, between)

            def second_layer(i):
                if i == -1:
                    rel_rstd(1)

            attention(LAYERS[0], second_layer)
            def ffn_norm(g):
                pool.wait_ge(sem("f_mv"), G4 * g + G4)
                nc.gpsimd.tensor_tensor(fve[:], fmv[:, :, 1], ln_eps[:].to_broadcast([P, G4]), ALU.add).then_inc(sem("f_ve"), 1)
                pool.wait_ge(sem("f_ve"), g + 1)
                nc.gpsimd.tensor_tensor(frs[:], fve[:], mhalf[:, 0:G4], ALU.pow).then_inc(sem("f_rs"), 1)

            def ffn_lo(s, par):
                pool.wait_ge(sem("f_hi"), s + 1)
                nc.gpsimd.tensor_tensor(hT[par][1][:], hf[par][:], hT[par][0][:].bitcast(F32), ALU.subtract).then_inc(sem("f_lo"), 1)

            def ffn(g, first=False, last=False):
                for f in range(FC):
                    ffn_lo(FC * g + f, f % 2)
                    if not last and f == 0:
                        ffn_norm(g + 1)

            ffn_norm(0)
            ffn(0, first=True)
            ffn(1)
            with pool.Fori(2, GROUPS - 1) as g:
                ffn(g)
            ffn(GROUPS - 1, last=True)
            pool.wait_ge(sem("f_dn"), FC * GROUPS)

            attention(LAYERS[1], None)
            def mean_root(n, t, par, ss, ms, r, used):
                pool.wait_ge(sem(f"d_ss{n}"), t + 1)
                reach(pool, sem(f"d_r{n}"), t)
                nc.gpsimd.tensor_tensor(ms[:], ss[par][:], rms_eps[:], ALU.add).then_inc(sem(f"d_ms{n}"), 1)
                pool.wait_ge(sem(f"d_ms{n}"), t + 1)
                reach(pool, sem(used), t - 1)
                nc.gpsimd.tensor_tensor(r[par][:], ms[:], mhalf[:, 0:1], ALU.pow).then_inc(sem(f"d_r{n}"), 1)

            def block_step(i, par):
                other = (par + 1) % 2
                t = i - 4
                if live(t):
                    pool.wait_ge(sem("t_rden"), BLK + t + 1)
                    reach(pool, sem("t_pTp"), BLK + t)
                    nc.gpsimd.tensor_tensor(bpn[:], be[:], brd[:].unsqueeze(2).to_broadcast([P, HB, S]), ALU.mult).then_inc(sem("t_pn"), 1)
                t = i - 7
                if live(t):
                    pool.wait_ge(sem("d_X1"), t + 1)
                    nc.gpsimd.tensor_tensor(X[:, t, :], X[:, t, :], O[:, t, :], ALU.add).then_inc(sem("d_R"), 1)
                t = i - 7
                if live(t):
                    mean_root(2, t, other, ss2, ms2, r2, "d_xf")
                t = i + 4
                if live(t):
                    pool.wait_ge(sem("t_mv"), BLK + t + 1)
                    reach(pool, sem("t_rstd"), BLK + t)
                    nc.gpsimd.tensor_tensor(dvar[:], dmv[par][:, 1:2], ln_eps[:], ALU.add).then_inc(sem("t_ve"), 1)
                    pool.wait_ge(sem("t_ve"), BLK + t + 1)
                    reach(pool, sem("d_X0"), t - 1)
                    nc.gpsimd.tensor_tensor(drs[par][:], dvar[:], mhalf[:, 0:1], ALU.pow).then_inc(sem("t_rstd"), 1)
                t = i + 2
                if live(t):
                    mean_root(1, t, par, ss1, ms1, r1, "d_nx")
                t = i + 3
                if live(t):
                    pool.wait_ge(sem("d_X0"), t + 1)
                    nc.gpsimd.tensor_tensor(O[:, t, :], O[:, t, :], gout1[:], ALU.mult).then_inc(sem("d_X"), 1)

            pool.wait_ge(sem("xf_stored"), 16)
            nc.gpsimd.iota(iota8[:], pattern=[[1, E]], base=0, channel_multiplier=0,
                           allow_small_or_imprecise_dtypes=True).then_inc(sem("const_pool"), 1)
            pool.wait_ge(sem("t_oev"), 2 * TILES)
            nc.gpsimd.iota(iota_rows[:], pattern=[[P, TILES]], base=0, channel_multiplier=0,
                           allow_small_or_imprecise_dtypes=True).then_inc(sem("const_pool"), 1)
            for what, n, first, by_part in ((iota_tile, ROUTED, 0, 0), (iota_row, P, 0, 0), (iota_part, 1, 0, 1), (number, TOP_K * TILES, 1, 0)):
                nc.gpsimd.iota(what[:], pattern=[[1, n]], base=first, channel_multiplier=by_part,
                               allow_small_or_imprecise_dtypes=True).then_inc(sem("const_pool"), 1)
            pipeline(pool, block_step, 4, 10)
            def fetch(r, m):
                apart(pool, (sem("e_src"), r + 1))
                if not isinstance(r, int) or r > 3:
                    apart(pool, (sem("e_xTp"), FIRST + r - 3))
                nc.gpsimd.indirect_dma_start(out=rows[:, m, :], out_offset=None, in_=xf_dram,
                                             in_offset=bass.IndirectOffsetOnAxis(ap=src[m][:], axis=0)).then_inc(sem(f"e_rows{m}"), 16)

            def store_result(r, par):
                apart(pool, (sem("e_idx"), r + 1),
                            (sem("e_out"), FIRST + r + 1))
                nc.gpsimd.indirect_dma_start(out=results, out_offset=bass.IndirectOffsetOnAxis(ap=idx[par][:], axis=0),
                                             in_=result[par][:], in_offset=None, bounds_check=SEQS * S * TOP_K - 1,
                                             oob_is_err=False).then_inc(sem(f"e_stored{par}"), 16)

            pool.wait_ge(sem("r_hot"), 1)
            nc.gpsimd.tensor_tensor(hot_number[:], hot_tile[:], number[:].unsqueeze(2).to_broadcast([P, TOP_K * TILES, ROUTED]),
                                    ALU.mult).then_inc(sem("r_hots"), 1)
            pool.wait_ge(sem("xf_stored"), 16 * 5)
            for r in range(8):
                fetch(r, r % 4)
            with pool.Fori(0, ROUTED // 4 - 2) as quad:
                for m in range(4):
                    store_result(4 * quad + m, m % 2)
                    fetch(4 * quad + m + 8, m)
            for r in range(ROUTED - 8, ROUTED):
                store_result(r, r % 2)
            for g in range(len(SUM_STEP)):
                pool.wait_ge(sem("y_both"), g + 1)
                pool.wait_ge(sem("e_out"), ROUTED + G4 * g + G4)
                x = X[:, G4 * g:G4 * g + G4, :]
                nc.gpsimd.tensor_tensor(x, x, both[g][:, :, 1, :], ALU.add).then_inc(sem("y_acc"), 1)

        @block.scalar
        def _(act):
            def split_hi(L):
                n = L["n"]
                act.wait_ge(sem("l_loaded"), nth(L, "loaded", LOADED[n]))
                act.wait_ge(sem("l_wn"), nth(L, "wn", KD))
                for k in range(KD):
                    nc.scalar.activation(wkvn[0][:, k, :], raw_kvn[:, k, :], ACT.Copy, scale=gcol[:, k:k + 1]).then_inc(sem("l_whi"), 1)

            def split_q_hi(k):
                nc.scalar.activation(wq[0][:, k, :], raw_q[:, k, :], ACT.Copy, scale=gcol[:, k:k + 1]).then_inc(sem("l_whi"), 1)

            def split_out_hi():
                nc.scalar.activation(wout[0][:], raw_o[:], ACT.Copy).then_inc(sem("l_whi"), 1)

            def rel_silu(k):
                act.wait_ge(sem("rel_ln"), k + 1)
                nc.scalar.activation(r_h[:], r_h[:], ACT.Silu).then_inc(sem("rel_act"), 1)

            def rel_transposed(k):
                act.wait_ge(sem("rel_Tp"), k + 1)
                nc.scalar.activation(r_hT[:], psW[:, 0:D], ACT.Copy).then_inc(sem("rel_T"), 1)

            def attention(L, between):
                n = L["n"]
                done = L["done"]

                def step(i, par):
                    t = i - 1
                    if live(t):
                        act.wait_ge(sem("t_kTp"), done + t + 1)
                        reach(act, sem("t_sp"), done + t)
                        nc.scalar.activation(kT[:], psM[:, 0:P], ACT.Copy, scale=ksc[:, 0:1]).then_inc(sem("t_kT"), 1)
                    t = i - 3
                    if live(t):
                        act.wait_ge(sem("t_pTp"), done + t + 1)
                        reach(act, sem("t_pv"), done + t)
                        nc.scalar.activation(pT[:], psT[:].rearrange("p a (c q) -> p (a c) q", q=P), ACT.Copy).then_inc(sem("t_pT"), 1)
                    t = i
                    if live(t):
                        act.wait_ge(sem("t_kvp"), done + t + 1)
                        reach(act, sem("t_sn"), done + t)
                        nc.scalar.activation(kvs[:], psM[:, 0:KVN], ACT.Copy).then_inc(sem("t_kvs"), 1)
                        if L["cosine"]:
                            act.wait_ge(sem("t_kvs"), done + t + 1)
                            reach(act, sem("t_kmx"), done + t)
                            nc.scalar.activation(junk[:], kvs[:, 0:DH], ACT.Square, accum_out=qss[:, H:H + 1]).then_inc(sem("t_kss"), 1)
                    t = i - 2
                    if live(t):
                        act.wait_ge(sem("t_sub"), done + t + 1)
                        nc.scalar.activation(ex[:], ex[:], ACT.Exp).then_inc(sem("t_ex"), 1)
                    t = i - 3
                    if live(t):
                        reach(act, sem("t_wo"), done + t)
                        for half, pv, ohi in ((0, "t_pv0", "t_ohi0"), (1, "t_pv", "t_ohi")):
                            act.wait_ge(sem(pv), done + t + 1)
                            nc.scalar.activation(oT[0][:, CH // 2 * half:CH // 2 * (half + 1), :],
                                                 psS[:, half, :].rearrange("p (c q) -> p c q", q=P), ACT.Identity,
                                                 bias=nvcol[:, 0:1]).then_inc(sem(ohi), 1)
                    t = i - 1
                    if live(t):
                        act.wait_ge(sem("t_qTp"), done + t + 1)
                        nc.scalar.activation(qT[:], psT[:].rearrange("p a (c q) -> p (a c) q", q=P), ACT.Copy).then_inc(sem("t_qT"), 1)
                    t = i + 1
                    if live(t):
                        act.wait_ge(sem("t_xTp"), done + t + 1)
                        nc.scalar.activation(xT[0][:], psM[:, 0:D].rearrange("p (k q) -> p k q", q=P), ACT.Copy).then_inc(sem("t_xhi"), 1)
                    t = i
                    if live(t):
                        act.wait_ge(sem("t_qp"), done + t + 1)
                        nc.scalar.activation(qn[:], psQ[:].rearrange("p a n -> p (a n)"), ACT.Copy).then_inc(sem("t_qn"), 1)
                        if L["cosine"]:
                            act.wait_ge(sem("t_qn"), done + t + 1)
                            reach(act, sem("t_ssq"), done + t)
                            nc.scalar.activation(sq[:], qn[:], ACT.Square).then_inc(sem("t_sq"), 1)
                    t = i - 3
                    if live(t):
                        act.wait_ge(sem("t_wo"), done + t + 1)
                        nc.scalar.activation(O[:, t, :], psW[:, 0:D], ACT.Copy).then_inc(sem("t_oev"), 1)

                pipeline(act, step, 2, 3, between)

            split_hi(LAYERS[0])
            for k in range(KD):
                split_q_hi(k)
            rel_silu(0)
            rel_transposed(0)

            def second_layer(i):
                if i == -1:
                    rel_silu(1)
                elif i == 0:
                    rel_transposed(1)
                    act.wait_ge(sem("rel_outp"), 1)
                    nc.scalar.activation(r_out[:], psW[0:H, 0:P], ACT.Identity, bias=r_b2[:, 0:1]).then_inc(sem("rel_out"), 1)
                    split_out_hi()
                elif i == TILES - 2:
                    act.wait_ge(sem("f_loaded"), 48)
                    for k in range(KD):
                        nc.scalar.activation(wfc[0][:, k, :], raw_q[:, k, :], ACT.Copy, scale=gout0[:, k:k + 1]).then_inc(sem("f_whi"), 1)
                    nc.scalar.activation(wpr[0][:], raw_o[:], ACT.Copy).then_inc(sem("f_whi"), 1)

            attention(LAYERS[0], second_layer)
            def ffn_in_hi(g):
                act.wait_ge(sem("f_cTp"), g + 1)
                nc.scalar.activation(cT[0][:], psT[:], ACT.Copy).then_inc(sem("f_chi"), 1)

            def ffn_relu(s, f):
                act.wait_ge(sem("f_up"), s + 1)
                reach(act, sem("f_lo"), s - 1)
                nc.scalar.activation(hf[f % 2][:], up_bank[f % 4], ACT.Relu).then_inc(sem("f_relu"), 1)

            def ffn_hi(s, par):
                act.wait_ge(sem("f_relu"), s + 1)
                nc.scalar.activation(hf[par][:], hf[par][:], ACT.Square).then_inc(sem("f_h"), 1)
                act.wait_ge(sem("f_h"), s + 1)
                reach(act, sem("f_dn"), s - 1)
                nc.scalar.activation(hT[par][0][:], hf[par][:], ACT.Copy).then_inc(sem("f_hi"), 1)

            def ffn_out(g):
                act.wait_ge(sem("f_dn"), FC * g + FC)
                reach(act, sem("f_lif"), 13 * g)
                nc.scalar.activation(cur[:].rearrange("p (a n) -> p a n", a=2), psS[:], ACT.Copy).then_inc(sem("f_y"), 1)

            def ffn(g, first=False, last=False):
                for f in range(FC):
                    if f == FC - 1 and not last:
                        act.wait_ge(sem("f_up"), FC * g + FC)
                        ffn_in_hi(g + 1)
                    ffn_relu(FC * g + f, f)
                    ffn_hi(FC * g + f, f % 2)
                    if f == 0 and not first:
                        ffn_out(g - 1)
                    if last and f == 2:
                        split_hi(LAYERS[1])
                    elif last and f in (3, 4):
                        split_q_hi(f - 3)
                    elif last and f == 5:
                        split_out_hi()

            ffn_in_hi(0)
            ffn(0, first=True)
            ffn(1)
            with act.Fori(2, GROUPS - 1) as g:
                ffn(g)
            ffn(GROUPS - 1, last=True)
            ffn_out(GROUPS - 1)
            def block_weights(i):
                if i == TILES - 2:
                    act.wait_ge(sem("d_loaded"), 16 * 7)
                    for k in range(KD):
                        nc.scalar.activation(bqkv[0][:, k, :], raw_bqkv[:, k, :], ACT.Copy, scale=g1col[:, k:k + 1]).then_inc(sem("d_whi"), 1)
                    nc.scalar.activation(bwo[0][:], raw_bwo[:], ACT.Copy).then_inc(sem("d_whi"), 1)

            attention(LAYERS[1], block_weights)
            act.wait_ge(sem("t_oev"), 2 * TILES)

            def block_step(i, par):
                t = i + 2
                if live(t):
                    act.wait_ge(sem("d_X"), t + 1)
                    reach(act, sem("d_ms1"), t - 1)
                    reach(act, sem("d_ss1"), t)
                    nc.scalar.activation(sqj[0][:], O[:, t, :], ACT.Square, scale=float(D) ** -0.5, accum_out=ss1[par][:]).then_inc(sem("d_ss1"), 1)
                t = i - 5
                if live(t):
                    act.wait_ge(sem("t_pv"), BLK + t + 1)
                    reach(act, sem("t_wo"), BLK + t)
                    nc.scalar.activation(boT[0][:], psM[:, 0:D].rearrange("p (k q) -> p k q", q=P), ACT.Copy).then_inc(sem("t_ohi"), 1)
                t = i - 4
                if live(t):
                    act.wait_ge(sem("t_pTp"), BLK + t + 1)
                    reach(act, sem("t_pv"), BLK + t)
                    nc.scalar.activation(bpT[:], psT[:, 1, 0:D].rearrange("p (k q) -> p k q", q=P), ACT.Copy).then_inc(sem("t_pT"), 1)
                t = i - 9
                if live(t):
                    act.wait_ge(sem("d_xfTp"), t + 1)
                    reach(act, sem("d_lgp"), t)
                    nc.scalar.activation(xff[:], psQ[:, 0, D:2 * D].rearrange("p (k q) -> p k q", q=P), ACT.Copy).then_inc(sem("d_xff"), 1)
                t = i - 9
                if live(t):
                    nc.scalar.activation(xf_all[:, t, :], xf[:], ACT.Copy).then_inc(sem("d_xfa"), 1)
                t = i - 3
                if live(t):
                    act.wait_ge(sem("t_sub"), BLK + t + 1)
                    nc.scalar.activation(be[:], be[:], ACT.Exp).then_inc(sem("t_ex"), 1)
                t = i - 2
                if live(t):
                    act.wait_ge(sem("t_qTp"), BLK + t + 1)
                    reach(act, sem("t_sp"), BLK + t)
                    nc.scalar.activation(bqT[:], psT[:, 0, 0:D].rearrange("p (k q) -> p k q", q=P), ACT.Copy).then_inc(sem("t_qT"), 1)
                    nc.scalar.activation(bkT[:], psT[:, 0, D:D + P], ACT.Copy, scale=float(DH) ** -0.5).then_inc(sem("t_kT"), 1)
                t = i - 1
                if live(t):
                    act.wait_ge(sem("t_qp"), BLK + t + 1)
                    reach(act, sem("t_qTp"), BLK + t)
                    nc.scalar.activation(bq[:], psQ[:, 1, 0:D], ACT.Copy).then_inc(sem("t_qn"), 1)
                    nc.scalar.activation(bk[:], psQ[:, 1, D:D + DH].unsqueeze(1).to_broadcast([P, 2, DH]), ACT.Copy).then_inc(sem("t_kn"), 1)
                    nc.scalar.activation(v_all[:, t, :], psQ[:, 1, D + DH:QKV], ACT.Copy).then_inc(sem("t_vp"), 1)
                t = i
                if live(t):
                    act.wait_ge(sem("t_xTp"), BLK + t + 1)
                    reach(act, sem("t_qp"), BLK + t)
                    nc.scalar.activation(nxT[0][:], psQ[:, 0, 0:D].rearrange("p (k q) -> p k q", q=P), ACT.Copy).then_inc(sem("t_xhi"), 1)

                t = i - 6
                if live(t):
                    act.wait_ge(sem("d_X1"), t + 1)
                    reach(act, sem("d_ms2"), t - 1)
                    reach(act, sem("d_ss2"), t)
                    nc.scalar.activation(sqj[1][:], O[:, t, :], ACT.Square, scale=float(D) ** -0.5, accum_out=ss2[par][:]).then_inc(sem("d_ss2"), 1)

            pipeline(act, block_step, 4, 10)
            def split_expert(n, part):
                if (n, part) == (0, 0):
                    act.wait_ge(sem("e_first"), 2 * 48)
                elif (n, part) == (2, 0):
                    act.wait_ge(sem("e_rest"), 3 * 48)
                elif (n, part) == (5, 0):
                    act.wait_ge(sem("e_last"), 4 * 48)
                slot = ORDER[n]
                third = slice(part * 2 * D, part * 2 * D + 2 * D)
                nc.scalar.activation(W[:, slot, 0, third], raw_w[:, slot, 1, third], ACT.Copy,
                                     scale=g2col[:, part:part + 1] if part < KD else 1.0).then_inc(sem("e_whi"), 1)

            def expert_step(i, m, shared=None):
                par = m % 2
                t = i - 2
                if kind(t, shared):
                    act.wait_ge(sem("e_up"), t + 1)
                    reach(act, sem("e_h"), t)
                    nc.scalar.activation(sg[:], psQ[:, par, 0:D], ACT.Silu).then_inc(sem("e_sg"), 1)
                t = i
                if kind(t, shared):
                    act.wait_ge(sem("e_xTp"), t + 1)
                    reach(act, sem("e_up"), t - 1)
                    nc.scalar.activation(exT[par][0][:], psM[:, 0:D].rearrange("p (k q) -> p k q", q=P), ACT.Copy).then_inc(sem("e_xhi"), 1)
                t = i - 4
                if kind(t, shared) == "routed":
                    act.wait_ge(sem("e_dn"), t + 1)
                    reach(act, sem(f"e_stored{par}"), stored(t - FIRST, par))
                    nc.scalar.activation(result[par][:], psW[:, 0:D], ACT.Copy).then_inc(sem("e_out"), 1)
                t = i - 3
                if kind(t, shared):
                    act.wait_ge(sem("e_hTp"), t + 1)
                    reach(act, sem("e_dn"), t)
                    nc.scalar.activation(ehT[0][:], psT[:, 0, 0:D].rearrange("p (k q) -> p k q", q=P), ACT.Copy).then_inc(sem("e_hhi"), 1)

            act.wait_ge(sem("d_xfa"), TILES)
            act.wait_ge(sem("d_R"), TILES)
            for part in range(3):
                split_expert(0, part)
            act.wait_ge(sem("r_exp_in"), 1)
            nc.scalar.activation(rt[0][:], rt[0][:], ACT.Exp).then_inc(sem("r_exp"), 1)
            act.wait_ge(sem("r_exp_in"), 2)
            nc.scalar.activation(rc[4][:], rc[4][:], ACT.Exp).then_inc(sem("r_exp"), 1)

            def first_half(i):
                if i in (1, 2):
                    act.wait_ge(sem("r_hot"), 1)
                    k = slice((i - 1) * TILES, i * TILES)
                    nc.scalar.activation(hot_part[:, k, :], hot_tile[:, k, :], ACT.Copy, scale=iota_part[:, 0:1]).then_inc(sem("r_hots"), 1)
                for piece in range(3 * EP):
                    if SPLIT_STEP[piece] == i:
                        split_expert(piece // 3, piece % 3)

            def second_results(g):
                act.wait_ge(sem(f"y_in{YS[g]}"), 16 * TOP_K * YS.count(YS[g]))
                for j in range(G4):
                    t = G4 * g + j
                    ins = nc.scalar.activation(both[g][:, j, 1, :], both[g][:, j, 1, :], ACT.Copy, scale=top_w[1][:, t:t + 1])
                ins.then_inc(sem("y_second"), 1)

            def other_half(i):
                if i in SUM_STEP:
                    second_results(SUM_STEP.index(i))

            expert_steps(act, expert_step, first_half, other_half)
            for g in range(len(SUM_STEP), GROUPS):
                second_results(g)

        @block.vector
        def _(dve):
            def null_key(L):
                n = L["n"]
                dve.wait_ge(sem("l_loaded"), nth(L, "loaded", LOADED[n]))
                nk = sem("l_nk")
                if L["cosine"]:
                    nc.vector.tensor_tensor(junk[:], nkb[:], nkb[:], ALU.mult).then_inc(nk, 1)
                    nc.vector.tensor_tensor(qsrow[:], qsrow[:], ksrow[:], ALU.mult).then_inc(nk, 1)
                    nc.vector.tensor_tensor(ksc[:], ksc[:], qsc[:], ALU.mult).then_inc(nk, 1)
                    dve.wait_ge(nk, nth(L, "nk", 3))
                    nc.vector.tensor_reduce(tiny[:, 0:1], junk[:], AX.X, ALU.add).then_inc(nk, 1)
                    nc.vector.tensor_scalar(ksc[:], ksc[:], float(DH) ** 0.5, None, ALU.mult)
                    dve.wait_ge(nk, nth(L, "nk", 4))
                    nc.vector.tensor_scalar(tiny[:, 1:2], tiny[:, 0:1], 1e-24, None, ALU.max).then_inc(sem("nk_ss"), 1)
                    dve.wait_ge(sem("nk_r"), 1)
                    nc.vector.tensor_scalar(nkb[:], nkb[:], tiny[:, 2:3], float(DH) ** 0.5, ALU.mult, ALU.mult).then_inc(nk, 1)
                    dve.wait_ge(nk, nth(L, "nk", 5))
                    nc.vector.tensor_tensor(nkb[:], nkb[:], qsrow[:], ALU.mult).then_inc(nk, 1)
                    dve.wait_ge(nk, nth(L, "nk", 6))
                else:
                    nc.vector.tensor_scalar(nkb[:], nkb[:], float(DH) ** -0.5, None, ALU.mult).then_inc(nk, 1)
                    nc.vector.memset(ksc[:], float(DH) ** -0.5)
                    dve.wait_ge(nk, nth(L, "nk", 1))
                for k in range(KD):
                    prod = wn_tmp[:]
                    if k:
                        dve.wait_ge(sem("l_wn"), nth(L, "wn", k))
                    nc.vector.tensor_tensor(prod, raw_q[:, k, :].rearrange("p (h d) -> p h d", h=H),
                                            nkb[:].unsqueeze(1).to_broadcast([P, H, DH]), ALU.mult).then_inc(sem("l_wnp"), 1)
                    dve.wait_ge(sem("l_wnp"), nth(L, "wnp", k + 1))
                    nc.vector.tensor_reduce(raw_kvn[:, k, 2 * DH:KVN], prod, AX.X, ALU.add).then_inc(sem("l_wn"), 1)

            def split_lo(L):
                n = L["n"]
                lo = sem("l_wlo")
                for k in range(KD):
                    dve.wait_ge(sem("l_whi"), nth(L, "whi", k + 1))
                    nc.vector.scalar_tensor_tensor(wkvn[1][:, k, :], raw_kvn[:, k, :], gcol[:, k:k + 1],
                                                   wkvn[0][:, k, :].bitcast(F32), ALU.mult, ALU.subtract).then_inc(lo, 1)
                for k in range(KD):
                    dve.wait_ge(sem("l_whi"), nth(L, "whi", KD + k + 1))
                    nc.vector.scalar_tensor_tensor(wq[1][:, k, :], raw_q[:, k, :], gcol[:, k:k + 1],
                                                   wq[0][:, k, :].bitcast(F32), ALU.mult, ALU.subtract).then_inc(lo, 1)

            def split_out_lo(L):
                dve.wait_ge(sem("l_whi"), nth(L, "whi", 2 * KD + 1))
                nc.vector.tensor_tensor(wout[1][:], raw_o[:], wout[0][:].bitcast(F32), ALU.subtract).then_inc(sem("l_wlo"), 1)

            def masks(L):
                nc.vector.tensor_scalar(negmask[:], mask_w[:].bitcast(U8), -1.0, -NEG, ALU.add, ALU.mult).then_inc(sem("l_mask"), 1)

            def rel_norm(k, src):
                c = sem("rel_chain")
                nc.vector.bn_stats(r_st[:], src).then_inc(c, 1)
                dve.wait_ge(c, 4 * k + 2)
                nc.vector.bn_aggr(r_mv[:], r_st[:]).then_inc(sem("rel_mv"), 1)
                dve.wait_ge(sem("rel_rstd"), 2 * k + 2)
                nc.vector.tensor_scalar(r_h[:], src, r_mv[:, 0:1], r_rs[:, 1:2], ALU.subtract, ALU.mult).then_inc(c, 1)
                dve.wait_ge(c, 4 * k + 3)
                nc.vector.tensor_tensor(r_h[:], r_h[:], r_rows[f"g{k}"][:], ALU.mult).then_inc(sem("rel_ln"), 1)

            def attention(L, start, between):
                n = L["n"]
                done = L["done"]

                def step(i, par):
                    t = i - 2
                    if live(t):
                        dve.wait_ge(sem("t_sp"), done + t + 1)
                        dve.wait_ge(sem("t_bm"), done + t + 1)
                        reach(dve, sem("t_pn"), done + t)
                        keys = ex[:, :, 0:S]
                        keys4 = keys.rearrange("p (c a) j -> p c a j", a=2)
                        scores = psS[:].rearrange("p a (c j) -> p c a j", j=S)
                        nc.vector.tensor_tensor(keys4, scores, masked[:].rearrange("p (c a) j -> p c a j", a=2),
                                                ALU.add).then_inc(sem("t_left"), 1)
                        if L["cosine"]:
                            dve.wait_ge(sem("t_rq"), done + t + 1)
                            nc.vector.tensor_tensor(sn[par][:], sn[par][:], rq[par][:], ALU.mult).then_inc(sem("t_snr"), 1)
                            dve.wait_ge(sem("t_snr"), 2 * t + 1)
                            nc.vector.tensor_tensor(sn[par][:], sn[par][:], nbias[:], ALU.add).then_inc(sem("t_snr"), 1)
                            dve.wait_ge(sem("t_snr"), 2 * t + 2)
                        dve.wait_ge(sem("t_left"), done + t + 1)
                        nc.vector.tensor_reduce(m16[:], keys, AX.X, ALU.max).then_inc(sem("t_m0"), 1)
                        dve.wait_ge(sem("t_m0"), done + t + 1)
                        nc.vector.tensor_tensor(mm16[:], m16[:], sn[par][:], ALU.max).then_inc(sem("t_m1"), 1)
                        dve.wait_ge(sem("t_m1"), done + t + 1)
                        nc.vector.tensor_tensor(keys, keys, mm16[:].unsqueeze(2).to_broadcast([P, H, S]), ALU.subtract)
                        nc.vector.tensor_tensor(ex[:, :, S], sn[par][:], mm16[:], ALU.subtract).then_inc(sem("t_sub"), 1)
                    t = i
                    if live(t) and L["cosine"]:
                        dve.wait_ge(sem("t_kss"), done + t + 1)
                        reach(dve, sem("t_rk"), done + t)
                        nc.vector.tensor_scalar(qmx[:, H:H + 1], qss[:, H:H + 1], 1e-24, None, ALU.max).then_inc(sem("t_kmx"), 1)
                    t = i
                    if live(t):
                        dve.wait_ge(sem("t_kvs"), done + t + 1)
                        reach(dve, sem(f"t_vv{par}"), 32 * done + spread(t - 2, par))
                        nc.vector.tensor_tensor(vp[par][:], kvs[:, DH:2 * DH], nvb[:], ALU.subtract).then_inc(sem("t_vp"), 1)
                    t = i + 1
                    if live(t):
                        dve.wait_ge(sem("t_rstd"), done + t + 1)
                        reach(dve, sem("t_xTp"), done + t)
                        q = (par + 1) % 2
                        nc.vector.tensor_scalar(xn[:], X[:, t, :], mv[q][:, 0:1], rstd[q][:, 0:1], ALU.subtract,
                                                ALU.mult).then_inc(sem("t_xn"), 1)
                    t = i + 2
                    if live(t):
                        start(t)
                        reach(dve, sem("t_mv"), done + t)
                        nc.vector.bn_stats(st6[:], X[:, t, :]).then_inc(sem("t_st"), 1)
                    t = i - 2
                    if live(t):
                        dve.wait_ge(sem("t_ex"), done + t + 1)
                        nc.vector.tensor_reduce(den[:], ex[:], AX.X, ALU.add).then_inc(sem("t_den"), 1)
                        dve.wait_ge(sem("t_den"), done + t + 1)
                        nc.vector.reciprocal(rden[:], den[:]).then_inc(sem("t_rden"), 1)
                    t = i + 2
                    if live(t):
                        apart(dve, (sem("t_st"), done + t + 1))
                        nc.vector.bn_aggr(mv[par][:], st6[:]).then_inc(sem("t_mv"), 1)
                    t = i - 3
                    if live(t):
                        dve.wait_ge(sem("t_ohi"), done + t + 1)
                        nc.vector.scalar_tensor_tensor(oT[1][:], psS[:].rearrange("p a (c q) -> p (a c) q", q=P), nvcol[:, 0:1],
                                                       oT[0][:].bitcast(F32), ALU.add, ALU.subtract).then_inc(sem("t_olo"), 1)
                    t = i + 1
                    if live(t):
                        dve.wait_ge(sem("t_xhi"), done + t + 1)
                        nc.vector.tensor_tensor(xT[1][:], psM[:, 0:D].rearrange("p (k q) -> p k q", q=P),
                                                xT[0][:].bitcast(F32), ALU.subtract).then_inc(sem("t_xlo"), 1)
                    t = i
                    if live(t):
                        reach(dve, sem("t_kTp"), done + t)
                        if L["cosine"]:
                            dve.wait_ge(sem("t_rk"), done + t + 1)
                            nc.vector.tensor_scalar(kn[:], kvs[:, 0:DH].unsqueeze(1).to_broadcast([P, 2, DH]), rk[:, 0:1],
                                                    None, ALU.mult).then_inc(sem("t_kn"), 1)
                            reach(dve, sem("t_sub"), done + t - 1)
                            nc.vector.tensor_copy(sn[par][:], kvs[:, 2 * DH:KVN]).then_inc(sem("t_sn"), 1)
                            dve.wait_ge(sem("t_sq"), done + t + 1)
                            nc.vector.tensor_reduce(qss[:, 0:H], sq[:].rearrange("p (h d) -> p h d", h=H), AX.X,
                                                    ALU.add).then_inc(sem("t_ssq"), 1)
                            dve.wait_ge(sem("t_ssq"), done + t + 1)
                            reach(dve, sem("t_rq"), done + t)
                            nc.vector.tensor_scalar(qmx[:, 0:H], qss[:, 0:H], 1e-24, None, ALU.max).then_inc(sem("t_qmx"), 1)
                        else:
                            nc.vector.tensor_copy(kn[:], kvs[:, 0:DH].unsqueeze(1).to_broadcast([P, 2, DH])).then_inc(sem("t_kn"), 1)
                            reach(dve, sem("t_sub"), done + t - 1)
                            nc.vector.tensor_tensor(sn[par][:], kvs[:, 2 * DH:KVN], nbias[:], ALU.add).then_inc(sem("t_sn"), 1)

                pipeline(dve, step, 2, 3, between)

            dve.wait_ge(sem("const_pool"), CONSTANTS)
            null_key(LAYERS[0])
            dve.wait_ge(sem("rel_loaded"), 16 * 8)
            nc.vector.scalar_tensor_tensor(r_h[:], r_rows["w0"][:], r_pos[:, 0:1], r_rows["b0"][:], ALU.mult,
                                           ALU.add).then_inc(sem("rel_chain"), 1)
            dve.wait_ge(sem("rel_chain"), 1)
            rel_norm(0, r_h[:])
            split_lo(LAYERS[0])

            def second_layer(i):
                if i == -1:
                    dve.wait_ge(sem("rel_mm"), 1)
                    nc.vector.tensor_tensor(r_h[:], psS[:, 0, 0:D], r_rows["b1"][:], ALU.add).then_inc(sem("rel_chain"), 2)
                    dve.wait_ge(sem("rel_chain"), 5)
                    rel_norm(1, r_h[:])
                    masks(LAYERS[0])
                elif i == 1:
                    split_out_lo(LAYERS[0])
                elif i == TILES - 2:
                    for k in range(KD):
                        dve.wait_ge(sem("f_whi"), k + 1)
                        nc.vector.scalar_tensor_tensor(wfc[1][:, k, :], raw_q[:, k, :], gout0[:, k:k + 1], wfc[0][:, k, :].bitcast(F32),
                                                       ALU.mult, ALU.subtract).then_inc(sem("f_wlo"), 1)
                elif i == TILES + 1:
                    dve.wait_ge(sem("f_whi"), KD + 1)
                    nc.vector.tensor_tensor(wpr[1][:], raw_o[:], wpr[0][:].bitcast(F32), ALU.subtract).then_inc(sem("f_wlo"), 1)

            def x_there(t):
                if isinstance(t, int) and t < 4:
                    dve.wait_ge(sem("x_in0"), 16)
                else:
                    dve.wait_ge(sem("x_in1"), 16)

            attention(LAYERS[0], x_there, second_layer)
            def ffn_stats(g):
                for j in range(G4):
                    reach(dve, sem("f_mv"), G4 * g)
                    nc.vector.bn_stats(fst6[:, j, :], O[:, G4 * g + j, :]).then_inc(sem("f_st"), 1)
                for j in range(G4):
                    apart(dve, (sem("f_st"), G4 * g + j + 1),
                               (sem("f_c0"), g))
                    nc.vector.bn_aggr(fmv[:, j, :], fst6[:, j, :]).then_inc(sem("f_mv"), 1)

            def ffn_normalise(g):
                dve.wait_ge(sem("f_rs"), g + 1)
                reach(dve, sem("f_cTp"), g)
                for j in range(G4):
                    ins = nc.vector.tensor_scalar(c0[:, j, :], O[:, G4 * g + j, :], fmv[:, j, 0:1], frs[:, j:j + 1],
                                                  ALU.subtract, ALU.mult)
                ins.then_inc(sem("f_c0"), 1)

            def ffn_in_lo(g):
                dve.wait_ge(sem("f_chi"), g + 1)
                nc.vector.tensor_tensor(cT[1][:], psT[:], cT[0][:].bitcast(F32), ALU.subtract).then_inc(sem("f_clo"), 1)

            def add_to_x(g):
                dve.wait_ge(sem("f_count"), 4 * g + 4)
                rows = X[:, bass.ts(g, G4), :]
                nc.vector.scalar_tensor_tensor(rows, count[:].rearrange("p (t d) -> p t d", d=D), 1.0 / LIF_STEPS, rows,
                                               ALU.mult, ALU.add).then_inc(sem("f_x1"), 1)

            def fire(g, n):
                done = sem("f_lif")
                reach(dve, done, 13 * g + n)
                if n == 0:
                    dve.wait_ge(sem("f_y"), g + 1)
                    reach(dve, sem("f_count"), 4 * g)
                kind, k = (2, 0) if n == 0 else ((n - 1) % 3, (n - 1) // 3 + 1)
                if kind == 2 and k >= 2:
                    dve.wait_ge(sem("f_count"), 4 * g + k - 1)
                if kind == 0:
                    src = cur if k == 1 else mem
                    ins = nc.vector.scalar_tensor_tensor(mem[:], src[:], LIF_BETA, cur[:], ALU.mult, ALU.add)
                elif kind == 1:
                    ins = nc.vector.tensor_tensor(mem[:], mem[:], spk[(k + 1) % 2][:], ALU.subtract)
                else:
                    src = cur if n == 0 else mem
                    ins = nc.vector.tensor_scalar(spk[k % 2][:], src[:], LIF_THRESHOLD, None, ALU.is_gt)
                ins.then_inc(done, 1)
                if kind == 2 and k > 0:
                    dve.wait_ge(done, 13 * g + n + 1)
                    if k == 1:
                        reach(dve, sem("f_x1"), g)
                        ins = nc.vector.tensor_tensor(count[:], spk[0][:], spk[1][:], ALU.add)
                    else:
                        dve.wait_ge(sem("f_count"), 4 * g + k - 1)
                        ins = nc.vector.tensor_tensor(count[:], count[:], spk[k % 2][:], ALU.add)
                    ins.then_inc(sem("f_count"), 1)

            def ffn(g, first=False, last=False):
                if not last:
                    ffn_stats(g + 1)
                else:
                    null_key(LAYERS[1])
                for f in range(FC):
                    if not last and f == 6:
                        ffn_in_lo(g + 1)
                    if not first:
                        for n in (2 * f, 2 * f + 1):
                            if n < 13:
                                fire(g - 1, n)
                    if not last and f == 2:
                        ffn_normalise(g + 1)
                    if last and f == 4:
                        split_lo(LAYERS[1])
                if not first:
                    add_to_x(g - 1)

            dve.wait_ge(sem("t_oev"), TILES)
            ffn_stats(0)
            ffn_normalise(0)
            ffn_in_lo(0)
            ffn(0, first=True)
            ffn(1)
            with dve.Fori(2, GROUPS - 1) as g:
                ffn(g)
            ffn(GROUPS - 1, last=True)
            split_out_lo(LAYERS[1])
            masks(LAYERS[1])
            dve.wait_ge(sem("f_dn"), FC * GROUPS)
            dve.wait_ge(sem("f_lo"), FC * GROUPS)

            def last_group(i):
                for n in {-1: range(0, 4), 0: range(4, 9), 1: range(9, 13)}.get(i, ()):
                    fire(GROUPS - 1, n)
                if i == 1:
                    add_to_x(GROUPS - 1)
                if i == TILES - 2:
                    for k in range(KD):
                        dve.wait_ge(sem("d_whi"), k + 1)
                        nc.vector.scalar_tensor_tensor(bqkv[1][:, k, :], raw_bqkv[:, k, :], g1col[:, k:k + 1], bqkv[0][:, k, :].bitcast(F32),
                                                       ALU.mult, ALU.subtract).then_inc(sem("d_wlo"), 1)
                    for k in range(KD):
                        nc.vector.tensor_scalar(bwr[:, k, :], bwr[:, k, :], g2col[:, k:k + 1], None, ALU.mult).then_inc(sem("d_wlo"), 1)
                    dve.wait_ge(sem("d_whi"), KD + 1)
                    nc.vector.tensor_tensor(bwo[1][:], raw_bwo[:], bwo[0][:].bitcast(F32), ALU.subtract).then_inc(sem("d_wlo"), 1)

            attention(LAYERS[1], lambda t: None, last_group)
            dve.wait_ge(sem("t_oev"), 2 * TILES)

            def block_step(i, par):
                other = (par + 1) % 2
                t = i - 1
                if live(t):
                    dve.wait_ge(sem("t_xhi"), BLK + t + 1)
                    nc.vector.tensor_tensor(nxT[1][:], psQ[:, 0, 0:D].rearrange("p (k q) -> p k q", q=P),
                                            nxT[0][:].bitcast(F32), ALU.subtract).then_inc(sem("t_xlo"), 1)
                t = i
                if live(t):
                    dve.wait_ge(sem("d_r1"), t + 1)
                    reach(dve, sem("t_xTp"), BLK + t)
                    nc.vector.tensor_scalar(nx[:], O[:, t, :], r1[par][:, 0:1], None, ALU.mult).then_inc(sem("d_nx"), 1)
                t = i + 4
                if live(t):
                    reach(dve, sem("t_mv"), BLK + t)
                    nc.vector.bn_stats(dst6[:], O[:, t, :]).then_inc(sem("t_st"), 1)
                t = i - 6
                if live(t):
                    dve.wait_ge(sem("t_wo"), BLK + t + 1)
                    nc.vector.tensor_tensor(O[:, t, :], psW[:, 0:D], O[:, t, :], ALU.add).then_inc(sem("d_X1"), 1)
                t = i + 4
                if live(t):
                    apart(dve, (sem("t_st"), BLK + t + 1))
                    nc.vector.bn_aggr(dmv[par][:], dst6[:]).then_inc(sem("t_mv"), 1)
                t = i - 5
                if live(t):
                    dve.wait_ge(sem("t_ohi"), BLK + t + 1)
                    nc.vector.tensor_tensor(boT[1][:], psM[:, 0:D].rearrange("p (k q) -> p k q", q=P),
                                            boT[0][:].bitcast(F32), ALU.subtract).then_inc(sem("t_olo"), 1)
                t = i - 3
                if live(t):
                    dve.wait_ge(sem("t_sp"), BLK + t + 1)
                    scores = psS[:, :, 0:CB * S].rearrange("p a (c j) -> p c a j", j=S)
                    nc.vector.tensor_reduce(bm[:].rearrange("p (c a) -> p c a", a=2), scores, AX.X, ALU.max).then_inc(sem("t_m0"), 1)
                    dve.wait_ge(sem("t_m0"), BLK + t + 1)
                    reach(dve, sem("t_pn"), BLK + t)
                    nc.vector.tensor_tensor(be[:].rearrange("p (c a) j -> p c a j", a=2), scores,
                                            bm[:].rearrange("p (c a) -> p c a", a=2).unsqueeze(3).to_broadcast([P, CB, 2, S]),
                                            ALU.subtract).then_inc(sem("t_sub"), 1)
                t = i + 3
                if live(t):
                    dve.wait_ge(sem("t_rstd"), BLK + t + 1)
                    nc.vector.tensor_scalar(O[:, t, :], O[:, t, :], dmv[other][:, 0:1], drs[other][:, 0:1], ALU.subtract,
                                            ALU.mult).then_inc(sem("d_X0"), 1)
                t = i - 8
                if live(t):
                    dve.wait_ge(sem("d_r2"), t + 1)
                    reach(dve, sem("d_xfTp"), t)
                    reach(dve, sem("d_xfa"), t)
                    nc.vector.tensor_scalar(xf[:], O[:, t, :], r2[par][:, 0:1], None, ALU.mult).then_inc(sem("d_xf"), 1)
                t = i - 10
                if live(t):
                    dve.wait_ge(sem("d_lgp"), t + 1)
                    nc.vector.tensor_tensor(logits[:, t, :], psW[:, D:D + E], ebias[:], ALU.add).then_inc(sem("d_lg"), 1)
                t = i - 3
                if live(t):
                    dve.wait_ge(sem("t_ex"), BLK + t + 1)
                    nc.vector.tensor_reduce(bden[:], be[:], AX.X, ALU.add).then_inc(sem("t_den"), 1)
                    dve.wait_ge(sem("t_den"), BLK + t + 1)
                    nc.vector.reciprocal(brd[:], bden[:]).then_inc(sem("t_rden"), 1)

            dve.wait_ge(sem("xf_stored"), 16)
            pipeline(dve, block_step, 4, 10)
            def split_expert(n, part):
                slot = ORDER[n]
                dve.wait_ge(sem("e_whi"), 3 * n + part + 1)
                third = slice(part * 2 * D, part * 2 * D + 2 * D)
                hi = W[:, slot, 0, third].bitcast(F32)
                lo, raw = W[:, slot, 1, third], raw_w[:, slot, 1, third]
                if part < KD:
                    ins = nc.vector.scalar_tensor_tensor(lo, raw, g2col[:, part:part + 1], hi, ALU.mult, ALU.subtract)
                else:
                    ins = nc.vector.tensor_tensor(lo, raw, hi, ALU.subtract)
                ins.then_inc(sem("e_wlo"), 1)

            chained = 0

            def then(ins):
                nonlocal chained
                chained += 1
                ins.then_inc(sem("r_chain"), 1)
                dve.wait_ge(sem("r_chain"), chained)

            def route():
                wide = lambda v: v.unsqueeze(2).to_broadcast([P, TILES, E])
                index = iota8[:].unsqueeze(1).to_broadcast([P, TILES, E])
                dve.wait_ge(sem("d_lg"), TILES)
                dve.wait_ge(sem("d_R"), TILES)
                dve.wait_ge(sem("const_pool"), CONSTANTS + 6)
                dve.wait_ge(sem("d_xfa"), TILES)
                then(nc.vector.tensor_reduce(rc[0][:], logits[:], AX.X, ALU.max))
                nc.vector.tensor_tensor(rt[0][:], logits[:], wide(rc[0][:]), ALU.subtract).then_inc(sem("r_exp_in"), 1)
                dve.wait_ge(sem("r_exp"), 1)
                then(nc.vector.tensor_reduce(rc[0][:], rt[0][:], AX.X, ALU.add))
                then(nc.vector.reciprocal(rc[1][:], rc[0][:]))
                then(nc.vector.tensor_tensor(rt[0][:], rt[0][:], wide(rc[1][:]), ALU.mult))
                for n in range(2):
                    then(nc.vector.tensor_reduce(rc[2 + n][:], rt[0][:], AX.X, ALU.max))
                    then(nc.vector.tensor_tensor(rt[3][:], rt[0][:], wide(rc[2 + n][:]), ALU.is_lt))
                    then(nc.vector.scalar_tensor_tensor(rt[3][:], rt[3][:], float(E), index, ALU.mult, ALU.add))
                    then(nc.vector.tensor_reduce(rc[0][:], rt[3][:], AX.X, ALU.min))
                    then(nc.vector.tensor_tensor(rt[1 + n][:], index, wide(rc[0][:]), ALU.is_equal))
                    if n == 0:
                        then(nc.vector.scalar_tensor_tensor(rt[0][:], rt[1][:], -2.0, rt[0][:], ALU.mult, ALU.add))
                nc.vector.tensor_tensor(rc[4][:], rc[3][:], rc[2][:], ALU.subtract).then_inc(sem("r_exp_in"), 1)
                then(nc.vector.tensor_tensor(chosen[:], rt[1][:], rt[2][:], ALU.add))
                nc.vector.tensor_copy(before[:], before_f[:]).then_inc(sem("r_given"), 1)
                dve.wait_ge(sem("r_exp"), 2)
                then(nc.vector.tensor_scalar(rc[0][:], rc[4][:], 1.0, None, ALU.add))
                then(nc.vector.reciprocal(top_w[0][:], rc[0][:]))
                then(nc.vector.tensor_tensor(top_w[1][:], rc[4][:], top_w[0][:], ALU.mult))
                dve.wait_ge(sem("r_ranked"), 1)
                in_tile, of_tile = (psS[:, b, 0:TILES * E].rearrange("p (t e) -> p t e", e=E) for b in range(2))
                then(nc.vector.tensor_copy(upto[0][:], of_tile))
                src, step = 0, 1
                while step < TILES:
                    nc.vector.tensor_copy(upto[1 - src][:, 0:step, :], upto[src][:, 0:step, :])
                    then(nc.vector.tensor_tensor(upto[1 - src][:, step:TILES, :], upto[src][:, step:TILES, :],
                                                 upto[src][:, 0:TILES - step, :], ALU.add))
                    src, step = 1 - src, 2 * step
                total = upto[src][:, TILES - 1, :]
                then(nc.vector.tensor_tensor(rt[0][:].rearrange("p t e -> p (t e)").rearrange("p (e n) -> p e n", e=E),
                                             total.unsqueeze(2).to_broadcast([P, E, TILES]),
                                             iota_rows[:].unsqueeze(1).to_broadcast([P, E, TILES]), ALU.is_gt))
                then(nc.vector.tensor_reduce(n_tiles[:], rt[0][:].rearrange("p t e -> p (t e)").rearrange("p (e n) -> p e n", e=E),
                                             AX.X, ALU.add))
                then(nc.vector.tensor_copy(end_tile[0][:], n_tiles[:]))
                e_src, step = 0, 1
                while step < E:
                    nc.vector.tensor_copy(end_tile[1 - e_src][:, 0:step], end_tile[e_src][:, 0:step])
                    then(nc.vector.tensor_tensor(end_tile[1 - e_src][:, step:E], end_tile[e_src][:, step:E],
                                                 end_tile[e_src][:, 0:E - step], ALU.add))
                    e_src, step = 1 - e_src, 2 * step
                ends = end_tile[e_src]
                then(nc.vector.tensor_tensor(n_tiles[:], ends[:], n_tiles[:], ALU.subtract))
                place_of = upto[1 - src]
                then(nc.vector.tensor_tensor(place_of[:], upto[src][:], of_tile, ALU.subtract))
                then(nc.vector.tensor_tensor(place_of[:], place_of[:], in_tile, ALU.add))
                then(nc.vector.scalar_tensor_tensor(place_of[:], n_tiles[:].unsqueeze(1).to_broadcast([P, TILES, E]), float(P),
                                                    place_of[:], ALU.mult, ALU.add))
                for k in range(TOP_K):
                    then(nc.vector.tensor_tensor(rt[1 + k][:], rt[1 + k][:], place_of[:], ALU.mult))
                    then(nc.vector.tensor_reduce(pos[:, k, :], rt[1 + k][:], AX.X, ALU.add))
                places = pos[:].rearrange("p k t -> p (k t)")
                then(nc.vector.tensor_scalar(pos_tile[:], places, 1.0 / P, -(P - 1) / (2.0 * P), ALU.mult, ALU.add))
                then(nc.vector.tensor_scalar(pos_tile[:], pos_tile[:], WHOLE, None, ALU.add))
                then(nc.vector.tensor_scalar(pos_tile[:], pos_tile[:], -WHOLE, None, ALU.add))
                nc.vector.tensor_tensor(hot_tile[:], iota_tile[:].unsqueeze(1).to_broadcast([P, TOP_K * TILES, ROUTED]),
                                        pos_tile[:].unsqueeze(2).to_broadcast([P, TOP_K * TILES, ROUTED]), ALU.is_equal).then_inc(sem("r_hot"), 1)
                then(nc.vector.scalar_tensor_tensor(pos_row[:], pos_tile[:], -float(P), places, ALU.mult, ALU.add))
                return ends

            def one_hot_rows(c):
                n = TOP_K * TILES // 4
                q = slice(c * n, c * n + n)
                nc.vector.tensor_tensor(hot_row[:, q, :], iota_row[:].unsqueeze(1).to_broadcast([P, n, P]),
                                        pos_row[:, q].unsqueeze(2).to_broadcast([P, n, P]), ALU.is_equal).then_inc(sem("r_hots"), 1)

            def tile_slots(ends):
                then(nc.vector.tensor_tensor(by_end[:], iota_tile[0:1, :].unsqueeze(2).to_broadcast([1, ROUTED, E]),
                                             ends[0:1, :].unsqueeze(1).to_broadcast([1, ROUTED, E]), ALU.is_ge))
                then(nc.vector.tensor_reduce(slot_f[0][:], by_end[:], AX.X, ALU.add))
                then(nc.vector.tensor_scalar(slot_f[1][:], slot_f[0][:], float(E - 1), -float(EP), ALU.is_ge, ALU.mult))
                then(nc.vector.scalar_tensor_tensor(slot_f[1][:], slot_f[0][:], float(SHARED_SLOT + 1), slot_f[1][:], ALU.add, ALU.add))
                nc.vector.tensor_scalar(slots[:], slot_f[1][:], float(2 * EW), None, ALU.mult).then_inc(sem("r_given"), 1)

            def row_tables():
                dve.wait_ge(sem("r_ranked"), 2)
                part, num = psS[:, 0, 0:ROUTED], psS[:, 1, 0:ROUTED]
                flat = [rt[n][:].rearrange("p t e -> p (t e)")[:, 0:ROUTED] for n in range(3)]
                nc.vector.memset(source[:, ROUTED:], 0)
                then(nc.vector.tensor_copy(flat[0], part))
                then(nc.vector.scalar_tensor_tensor(flat[0], num, float(P), flat[0], ALU.mult, ALU.add))
                then(nc.vector.tensor_scalar(flat[1], num, TILES + 0.5, -float(SEQS * S), ALU.is_gt, ALU.mult))
                then(nc.vector.tensor_tensor(flat[1], flat[0], flat[1], ALU.add))
                then(nc.vector.tensor_scalar(source[:, 0:ROUTED], flat[1], -float(P - 1), 0.0, ALU.add, ALU.max))
                then(nc.vector.tensor_scalar(flat[2], num, 0.5, float(NOWHERE), ALU.is_lt, ALU.mult))
                then(nc.vector.scalar_tensor_tensor(target[:], flat[0], -float(P), flat[2], ALU.add, ALU.add))

            def expert_step(i, m, shared=None):
                par = m % 2
                t = i - 2
                if kind(t, shared):
                    dve.wait_ge(sem("e_sg"), t + 1)
                    reach(dve, sem("e_hTp"), t - 1)
                    nc.vector.tensor_tensor(eh[par][:], sg[:], psQ[:, par, D:2 * D], ALU.mult).then_inc(sem("e_h"), 1)
                t = i
                if kind(t, shared):
                    dve.wait_ge(sem("e_xhi"), t + 1)
                    nc.vector.tensor_tensor(exT[par][1][:], psM[:, 0:D].rearrange("p (k q) -> p k q", q=P),
                                            exT[par][0][:].bitcast(F32), ALU.subtract).then_inc(sem("e_xlo"), 1)
                r = i + 4 - FIRST
                if not isinstance(i, int) and shared == "routed" or isinstance(i, int) and 0 <= r < ROUTED:
                    n = (m + 4 - FIRST) % 4
                    if not isinstance(r, int) or r > 3:
                        dve.wait_ge(sem(f"e_rows{n}"), loaded(r - 4, n))
                    nc.vector.tensor_copy(src[n][:], source[:, bass.ds(r, 1)]).then_inc(sem("e_src"), 1)
                t = i - 4
                if kind(t, shared) == "shared":
                    dve.wait_ge(sem("e_dn"), t + 1)
                    x = X[:, bass.ds(tokens(t), 1), :].rearrange("p o d -> p (o d)")
                    nc.vector.tensor_tensor(x, psW[:, 0:D], x, ALU.add).then_inc(sem("e_out"), 1)
                elif kind(t, shared) == "routed":
                    r = t - FIRST
                    reach(dve, sem(f"e_stored{par}"), stored(r, par))
                    nc.vector.tensor_copy(idx[par][:], target[:, bass.ds(r, 1)]).then_inc(sem("e_idx"), 1)
                t = i - 3
                if kind(t, shared):
                    dve.wait_ge(sem("e_hhi"), t + 1)
                    nc.vector.tensor_tensor(ehT[1][:], psT[:, 0, 0:D].rearrange("p (k q) -> p k q", q=P),
                                            ehT[0][:].bitcast(F32), ALU.subtract).then_inc(sem("e_hlo"), 1)

            ends = route()
            for part in range(3):
                split_expert(0, part)

            def first_half(i):
                if i < 4:
                    one_hot_rows(i)
                elif i == 4:
                    tile_slots(ends)
                elif i == 6:
                    row_tables()
                for piece in range(3 * EP):
                    if SPLIT_STEP[piece] == i:
                        split_expert(piece // 3, piece % 3)

            def both_results(g):
                dve.wait_ge(sem("y_second"), g + 1)
                for j in range(G4):
                    t = G4 * g + j
                    ins = nc.vector.scalar_tensor_tensor(both[g][:, j, 1, :], both[g][:, j, 0, :], top_w[0][:, t:t + 1],
                                                         both[g][:, j, 1, :], ALU.mult, ALU.add)
                ins.then_inc(sem("y_both"), 1)

            def other_half(i):
                if i in SUM_STEP:
                    both_results(SUM_STEP.index(i))

            expert_steps(dve, expert_step, first_half, other_half)
            for g in range(len(SUM_STEP), GROUPS):
                both_results(g)
                dve.wait_ge(sem("y_both"), g + 1)
                dve.wait_ge(sem("e_out"), ROUTED + TILES)
                x = X[:, G4 * g:G4 * g + G4, :]
                nc.vector.tensor_tensor(x, x, both[g][:, :, 1, :], ALU.add).then_inc(sem("y_last"), 1)

        @block.tensor
        def _(pe):
            def attention(L, between):
                n = L["n"]
                done = L["done"]

                def step(i, par):
                    t = i - 1
                    if live(t):
                        pe.wait_ge(sem("t_kn"), done + t + 1)
                        if live(t + 1):
                            pe.wait_ge(sem("t_xlo"), done + t + 2)
                        nc.tensor.transpose(psM[:, 0:P], kn[:].rearrange("p a d -> p (a d)"), ident[:]).then_inc(sem("t_kTp"), 1)
                    t = i - 3
                    if live(t):
                        pe.wait_ge(sem("t_pn"), done + t + 1)
                        if live(t + 1):
                            pe.wait_ge(sem("t_qT"), done + t + 2)
                        for c in range(CH):
                            mm = nc.tensor.transpose(psT[:, c // 4, c % 4 * P:c % 4 * P + P],
                                                     pn[:, 2 * c:2 * c + 2, :].rearrange("p a j -> p (a j)"), ident[:])
                        mm.then_inc(sem("t_pTp"), 1)
                    t = i
                    if live(t):
                        pe.wait_ge(sem("t_xlo"), done + t + 1)
                        reach(pe, sem("t_kT"), done + t)
                        if isinstance(t, int) and t == 0:
                            pe.wait_ge(sem("l_wlo"), nth(L, "wlo", 2 * KD))
                        for k in range(KD):
                            for j, (u, w) in enumerate(PASSES):
                                mm = nc.tensor.matmul(psM[:, 0:KVN], xT[u][:, k, :], wkvn[w][:, k, :],
                                                      start=(k == 0 and j == 0), stop=(k == KD - 1 and j == 2))
                        mm.then_inc(sem("t_kvp"), 1)
                        reach(pe, sem("t_qn"), done + t)
                        for half in range(2):
                            for k in range(KD):
                                for j, (u, w) in enumerate(PASSES):
                                    if live(i - 3) and half == 1 and k == KD - 1 and j == 2:
                                        pe.wait_ge(sem("t_pT"), done + i - 2)
                                        pe.wait_ge(sem("t_left"), done + i - 1)
                                        pe.wait_ge(sem(f"t_vv{(par + 1) % 2}"), 32 * done + spread(i - 3, (par + 1) % 2))
                                    mm = nc.tensor.matmul(psQ[:, half, :], xT[u][:, k, :], wq[w][:, k, half * 512:half * 512 + 512],
                                                          start=(k == 0 and j == 0), stop=(k == KD - 1 and j == 2))
                        mm.then_inc(sem("t_qp"), 1)
                    t = i - 3
                    if live(t):
                        vpar = (par + 1) % 2
                        if not live(i):
                            pe.wait_ge(sem("t_pT"), done + t + 1)
                            pe.wait_ge(sem(f"t_vv{vpar}"), 32 * done + spread(t, vpar))
                            if live(t + 1):
                                pe.wait_ge(sem("t_left"), done + t + 2)
                        for c4 in range(2):
                            out4 = psS[:, c4, :].rearrange("p (c b q) -> p c b q", b=2, q=S)
                            for b in range(2):
                                for half in range(2):
                                    f = slice(half * S, half * S + S)
                                    mm = nc.tensor.matmul(out4[f, :, b, :], vv[vpar][f, b, :],
                                                          pT[f, 4 * c4:4 * c4 + 4, b * S:b * S + S],
                                                          start=(b == 0), stop=(b == 1), skip_group_check=True)
                            mm.then_inc(sem("t_pv" if c4 else "t_pv0"), 1)
                    t = i - 1
                    if live(t):
                        pe.wait_ge(sem("t_qs" if L["cosine"] else "t_qn"), done + t + 1)
                        reach(pe, sem("t_pT"), done + t - 1)
                        for c in range(CH):
                            mm = nc.tensor.transpose(psT[:, c // 4, c % 4 * P:c % 4 * P + P], qn[:, c * P:c * P + P], ident[:])
                        mm.then_inc(sem("t_qTp"), 1)
                    t = i + 1
                    if live(t):
                        pe.wait_ge(sem("t_xn"), done + t + 1)
                        reach(pe, sem("t_kvs"), done + t)
                        for k in range(KD):
                            mm = nc.tensor.transpose(psM[:, k * P:k * P + P], xn[:, k * P:k * P + P], ident[:])
                        mm.then_inc(sem("t_xTp"), 1)
                    t = i - 3
                    if live(t):
                        if isinstance(t, int) and t == 0:
                            pe.wait_ge(sem("l_wlo"), nth(L, "wlo", 2 * KD + 1))
                        pe.wait_ge(sem("t_ohi0"), done + t + 1)
                        reach(pe, sem("t_oev"), done + t)
                        for u in range(2):
                            if u:
                                pe.wait_ge(sem("t_olo"), done + t + 1)
                            for c in range(CH):
                                if not u and c == CH // 2:
                                    pe.wait_ge(sem("t_ohi"), done + t + 1)
                                for w in range(2 - u):
                                    mm = nc.tensor.matmul(psW[:, 0:D], oT[u][:, c, :], wout[w][:, c, :],
                                                          start=(u == 0 and c == 0 and w == 0), stop=(u == 1 and c == CH - 1))
                        mm.then_inc(sem("t_wo"), 1)
                    t = i - 1
                    if live(t):
                        reach(pe, sem("t_olo"), done + t - 1)
                        reach(pe, sem("t_left"), done + t)
                        pe.wait_ge(sem("t_kT"), done + t + 1)
                        apart(pe, (sem("t_qT"), done + t + 1))
                        for c in range(CH):
                            for half in range(2):
                                for b in range(2):
                                    f = slice(half * DH, half * DH + DH)
                                    q = slice(b * S, b * S + S)
                                    mm = nc.tensor.matmul(psS[q, half, c * S:c * S + S], qT[f, c, q], kT[f, q],
                                                          start=True, stop=True, skip_group_check=True)
                        mm.then_inc(sem("t_sp"), 1)

                pipeline(pe, step, 2, 3, between)

            pe.wait_ge(sem("const_pool"), CONSTANTS)

            def rel_layer(k):
                pe.wait_ge(sem("rel_act"), k + 1)
                for c in range(KD):
                    mm = nc.tensor.transpose(psW[:, c * P:c * P + P], r_h[:, c * P:c * P + P], ident[:])
                mm.then_inc(sem("rel_Tp"), 1)
                pe.wait_ge(sem("rel_T"), k + 1)
                if k == 0:
                    for c in range(KD):
                        mm = nc.tensor.matmul(psS[:, 0, 0:D], r_hT[:, c, :], r_w1[:, c, :], start=(c == 0), stop=(c == KD - 1))
                    mm.then_inc(sem("rel_mm"), 1)
                else:
                    for c in range(KD):
                        mm = nc.tensor.matmul(psW[0:H, 0:P], r_w2[:, c, :], r_hT[:, c, :], start=(c == 0), stop=(c == KD - 1))
                    mm.then_inc(sem("rel_outp"), 1)

            rel_layer(0)
            attention(LAYERS[0], lambda i: rel_layer(1) if i == 0 else None)
            def ffn_in(g):
                pe.wait_ge(sem("f_c0"), g + 1)
                reach(pe, sem("f_clo"), g)
                for k in range(KD):
                    for j in range(G4):
                        mm = nc.tensor.transpose(psT[:, k, j * P:j * P + P], c0[:, j, k * P:k * P + P], ident[:])
                mm.then_inc(sem("f_cTp"), 1)

            def ffn_up(g, f):
                s = FC * g + f
                if f % FC == 0:
                    pe.wait_ge(sem("f_clo"), g + f // FC + 1)
                reach(pe, sem("f_relu"), s - 3)
                for k in range(KD):
                    for j, (u, w) in enumerate(PASSES):
                        mm = nc.tensor.matmul(up_bank[f % 4], wfc[u][:, k, f % FC * P:f % FC * P + P], cT[w][:, k, :],
                                              start=(k == 0 and j == 0), stop=(k == KD - 1 and j == 2))
                mm.then_inc(sem("f_up"), 1)

            def ffn_down(g, f):
                s = FC * g + f
                pe.wait_ge(sem("f_lo"), s + 1)
                if f == 0:
                    reach(pe, sem("f_y"), g)
                for t in range(G4):
                    for j, (u, w) in enumerate(PASSES):
                        mm = nc.tensor.matmul(psS[:, t // 2, t % 2 * D:t % 2 * D + D], hT[f % 2][u][:, t * P:t * P + P], wpr[w][:, f, :],
                                              start=(f == 0 and j == 0 and t % 2 == 0), stop=(f == FC - 1 and j == 2),
                                              skip_group_check=True)
                mm.then_inc(sem("f_dn"), 1)

            def ffn(g, last=False):
                for f in range(FC - 2):
                    ffn_up(g, f + 2)
                    ffn_down(g, f)
                    if f == FC - 4 and not last:
                        ffn_in(g + 1)
                ffn_down(g, FC - 2)
                if not last:
                    ffn_up(g, FC)
                ffn_down(g, FC - 1)
                if not last:
                    ffn_up(g, FC + 1)

            pe.wait_ge(sem("f_wlo"), KD + 1)
            ffn_in(0)
            ffn_up(0, 0)
            ffn_up(0, 1)
            ffn(0)
            with pe.Fori(1, GROUPS - 1) as g:
                ffn(g)
            ffn(GROUPS - 1, last=True)
            pe.wait_ge(sem("f_relu"), FC * GROUPS)
            pe.wait_ge(sem("f_clo"), GROUPS)
            pe.wait_ge(sem("f_y"), GROUPS)
            attention(LAYERS[1], None)
            def block_step(i, par):
                t = i - 6
                if live(t):
                    pe.wait_ge(sem("t_olo"), BLK + t + 1)
                    reach(pe, sem("d_X1"), t)
                    if live(i - 11):
                        pe.wait_ge(sem("d_lg"), i - 10)
                    for c in range(CB):
                        for j, (u, w) in enumerate(PASSES):
                            mm = nc.tensor.matmul(psW[:, 0:D], boT[u][:, c, :], bwo[w][:, c, :],
                                                  start=(c == 0 and j == 0), stop=(c == CB - 1 and j == 2))
                    mm.then_inc(sem("t_wo"), 1)
                t = i - 5
                if live(t):
                    vpar = (par + 1) % 2
                    apart(pe, (sem("t_pT"), BLK + t + 1),
                              (sem(f"t_vv{vpar}"), 32 * BLK + spread(t, vpar)),
                              (sem("t_olo"), BLK + t))
                    o = psM[:, 0:D].rearrange("p (c b q) -> p c b q", b=2, q=S)
                    for b in range(2):
                        for half in range(2):
                            f = slice(half * S, half * S + S)
                            mm = nc.tensor.matmul(o[f, :, b, :], bvv[vpar][f, b, :], bpT[f, :, b * S:b * S + S],
                                                  start=True, stop=True, skip_group_check=True)
                    mm.then_inc(sem("t_pv"), 1)
                t = i - 3
                if live(t):
                    apart(pe, (sem("t_kT"), BLK + t + 1),
                              (sem("t_sub"), BLK + t))
                    for c in range(CB):
                        for half in range(2):
                            for b in range(2):
                                f = slice(half * DH, half * DH + DH)
                                q = slice(b * S, b * S + S)
                                mm = nc.tensor.matmul(psS[q, half, c * S:c * S + S], bqT[f, c, q], bkT[f, q],
                                                      start=True, stop=True, skip_group_check=True)
                    mm.then_inc(sem("t_sp"), 1)
                t = i - 4
                if live(t):
                    pe.wait_ge(sem("t_pn"), BLK + t + 1)
                    reach(pe, sem("t_pT"), BLK + t)
                    for c in range(CB):
                        mm = nc.tensor.transpose(psT[:, 1, c * P:c * P + P],
                                                 bpn[:, 2 * c:2 * c + 2, :].rearrange("p a j -> p (a j)"), ident[:])
                    mm.then_inc(sem("t_pTp"), 1)
                t = i - 9
                if live(t):
                    pe.wait_ge(sem("d_xf"), t + 1)
                    if live(i - 1):
                        pe.wait_ge(sem("t_xlo"), BLK + i)
                    reach(pe, sem("d_xff"), t)
                    for k in range(KD):
                        mm = nc.tensor.transpose(psQ[:, 0, D + k * P:D + k * P + P], xf[:, k * P:k * P + P], ident[:])
                    mm.then_inc(sem("d_xfTp"), 1)
                t = i - 10
                if live(t):
                    pe.wait_ge(sem("d_xff"), t + 1)
                    if live(i - 6):
                        pe.wait_ge(sem("d_X1"), i - 5)
                    reach(pe, sem("d_lg"), t)
                    for k in range(KD):
                        mm = nc.tensor.matmul(psW[:, D:D + E], xff[:, k, :], bwr[:, k, :], start=(k == 0), stop=(k == KD - 1))
                    mm.then_inc(sem("d_lgp"), 1)
                t = i - 2
                if live(t):
                    pe.wait_ge(sem("t_kn"), BLK + t + 1)
                    reach(pe, sem("t_kT"), BLK + t)
                    for c in range(CB):
                        nc.tensor.transpose(psT[:, 0, c * P:c * P + P], bq[:, c * P:c * P + P], ident[:])
                    nc.tensor.transpose(psT[:, 0, D:D + P], bk[:].rearrange("p a d -> p (a d)"), ident[:]).then_inc(sem("t_qTp"), 1)
                t = i - 1
                if live(t):
                    pe.wait_ge(sem("t_xlo"), BLK + t + 1)
                    reach(pe, sem("t_vp"), BLK + t)
                    for k in range(KD):
                        for j, (u, w) in enumerate(PASSES):
                            mm = nc.tensor.matmul(psQ[:, 1, 0:QKV], nxT[u][:, k, :], bqkv[w][:, k, :],
                                                  start=(k == 0 and j == 0), stop=(k == KD - 1 and j == 2))
                    mm.then_inc(sem("t_qp"), 1)
                t = i
                if live(t):
                    pe.wait_ge(sem("d_nx"), t + 1)
                    reach(pe, sem("t_xlo"), BLK + t)
                    if live(i - 9):
                        pe.wait_ge(sem("d_xff"), i - 8)
                    for k in range(KD):
                        mm = nc.tensor.transpose(psQ[:, 0, k * P:k * P + P], nx[:, k * P:k * P + P], ident[:])
                    mm.then_inc(sem("t_xTp"), 1)

            pe.wait_ge(sem("d_wlo"), 2 * KD + 1)
            pipeline(pe, block_step, 4, 10)
            weights_at = None
            weights = W[:].rearrange("p s w n -> p (s w n)")

            def offsets(t, n):
                return nc.values_load_multi_w_load_instructions(
                    slots[0:1, bass.ds(t - FIRST, n)], engines=(mybir.EngineType.PE,), min_val=0, max_val=(EP - 1) * 2 * EW,
                    skip_runtime_bounds_check_because="they are worked out as one of nine places")[1]

            def expert_step(i, m, shared=None):
                other = (m + 1) % 2
                if isinstance(i, int) and i - 1 == FIRST:
                    pe.wait_ge(sem("r_given"), 2)
                if not isinstance(i, int) and shared == "routed":
                    if m == 0:
                        nonlocal weights_at
                        weights_at = offsets(i - 4, 7)
                    w2_at, w13_at = weights_at[m], weights_at[m + 3]
                else:
                    w2_at, w13_at = (offsets(t, 1)[0] if kind(t, shared) == "routed" else SHARED_SLOT * 2 * EW for t in (i - 4, i - 1))
                t = i
                if kind(t, shared):
                    if kind(t, shared) == "routed":
                        pe.wait_ge(sem(f"e_rows{m}"), loaded(t - FIRST, m))
                        tile = rows[:, m, :]
                    else:
                        tile = xf_all[:, tokens(t), :]
                    reach(pe, sem("e_xlo"), t)
                    for k in range(KD):
                        mm = nc.tensor.transpose(psM[:, k * P:k * P + P], tile[:, k * P:k * P + P], ident[:])
                    mm.then_inc(sem("e_xTp"), 1)
                t = i - 4
                if kind(t, shared):
                    pe.wait_ge(sem("e_hlo"), t + 1)
                    reach(pe, sem("e_out"), t)
                    for c in range(KD):
                        for j, (u, w) in enumerate(PASSES):
                            mm = nc.tensor.matmul(psW[:, 0:D], ehT[u][:, c, :], weights[:, bass.ds(w2_at + w * EW + (2 * KD + c) * D, D)],
                                                  start=(c == 0 and j == 0), stop=(c == KD - 1 and j == 2))
                    mm.then_inc(sem("e_dn"), 1)
                t = i - 3
                if kind(t, shared):
                    pe.wait_ge(sem("e_h"), t + 1)
                    reach(pe, sem("e_hlo"), t)
                    for c in range(KD):
                        mm = nc.tensor.transpose(psT[:, 0, c * P:c * P + P], eh[other][:, c * P:c * P + P], ident[:])
                    mm.then_inc(sem("e_hTp"), 1)
                t = i - 1
                if kind(t, shared):
                    if isinstance(t, int) and t in (0, FIRST):
                        pe.wait_ge(sem("e_wlo"), 3 * EP if t else 3)
                    pe.wait_ge(sem("e_xlo"), t + 1)
                    reach(pe, sem("e_h"), t - 1)
                    for k in range(KD):
                        for j, (u, w) in enumerate(PASSES):
                            mm = nc.tensor.matmul(psQ[:, other, :], exT[other][u][:, k, :], weights[:, bass.ds(w13_at + w * EW + 2 * k * D, 2 * D)],
                                                  start=(k == 0 and j == 0), stop=(k == KD - 1 and j == 2))
                    mm.then_inc(sem("e_up"), 1)

            pe.wait_ge(sem("r_given"), 1)
            for b, what in enumerate((before, ones)):
                mm = nc.tensor.matmul(psS[:, b, 0:TILES * E], what[:], chosen[:].rearrange("p t e -> p (t e)"), start=True, stop=True)
            mm.then_inc(sem("r_ranked"), 1)
            pe.wait_ge(sem("d_xfa"), TILES)

            def first_half(i):
                if i == 4:
                    pe.wait_ge(sem("r_hots"), 4 + 2 + 1)
                    for b, what in enumerate((hot_part, hot_number)):
                        for q in range(TOP_K * TILES):
                            mm = nc.tensor.matmul(psS[:, b, 0:ROUTED], hot_row[:, q, :], what[:, q, :], start=(q == 0), stop=(q == TOP_K * TILES - 1))
                    mm.then_inc(sem("r_ranked"), 1)

            expert_steps(pe, expert_step, first_half)


def layout(inputs):
    c = np.ascontiguousarray
    i = {k: np.asarray(v) for k, v in inputs.items()}
    first = lambda name, s: c(np.concatenate([i[s][None], i[name]], axis=0).transpose(0, 2, 1))
    return {
        "x": c(i["x"].reshape(SEQS * S, D)), "null": c(i["cond_64"]), "fside": c(i["fside_16xSxS_0"]),
        "mask0": c(i["mask_BxS_bf1"]).view(np.int32), "mask1": c(i["mask_BxS_bk0"]).view(np.int32),
        "g_norm": c(i["L0_cond_g_norm"]), "Wq0": c(i["L0_cond_Wq"]), "Wkv0": c(i["L0_cond_Wkv"]),
        "q_scale": c(i["L0_cond_q_scale"]), "k_scale": c(i["L0_cond_k_scale"]), "nb0": c(i["L0_cond_null_attn_bias"]),
        "rw0": c(i["L0_cond_w0"].reshape(D)), "rb0": c(i["L0_cond_b0"]), "rg0": c(i["L0_cond_g0"]),
        "rw1": c(i["L0_cond_w1"]), "rb1": c(i["L0_cond_b1"]), "rg1": c(i["L0_cond_g1"]),
        "rw2": c(i["L0_cond_w2"]), "rb2": c(i["L0_cond_b2"]), "Wout0": c(i["L0_cond_Wout"]),
        "g_out0": c(i["L0_cond_g_out"]), "Wfc": c(i["L0_ffn_W_fc"].T), "Wproj": c(i["L0_ffn_W_proj"].T),
        "g_in": c(i["L1_cond_g_in"]), "nb1": c(i["L1_cond_null_attn_bias"]), "Wq1": c(i["L1_cond_Wq"]),
        "Wkv1": c(i["L1_cond_Wkv"]), "Wo1": c(i["L1_cond_Wo"]), "g_out1": c(i["L1_cond_g_out"]),
        "g1": c(i["L1_ffn_g1"]), "g2": c(i["L1_ffn_g2"]),
        "Wqkv": c(np.concatenate([i["L1_ffn_Wq"], i["L1_ffn_Wkc"], i["L1_ffn_Wvc"]], axis=0).T),
        "Wo": c(i["L1_ffn_Wo"].T), "Wr": c(i["L1_ffn_Wr"].T), "ebias": c(i["L1_ffn_expert_bias"]),
        "W1": first("L1_ffn_eW1", "L1_ffn_sW1"), "W2": first("L1_ffn_eW2", "L1_ffn_sW2"),
        "W3": first("L1_ffn_eW3", "L1_ffn_sW3"),
    }


def kernel(**inputs):
    import concourse.bacc as bacc
    from concourse.bass_utils import run_bass_kernel_spmd

    nc = bacc.Bacc("TRN2", target_bir_lowering=False, num_devices=1)
    arrays = layout(inputs)
    args = {n: nc.dram_tensor(n, v.shape, mybir.dt.from_np(v.dtype), kind="ExternalInput").ap() for n, v in arrays.items()}
    out = nc.dram_tensor("out", (SEQS * S, D), F32, kind="ExternalOutput").ap()
    build(nc, args, out)
    r = run_bass_kernel_spmd(nc, [arrays], core_ids=[0])
    return np.asarray(r.results[0]["out"]).reshape(SEQS, S, D)
```
